# Optimizing a Trainium2 kernel written in Bass

```python
import numpy as np
import jax
import jax.numpy as jnp

def _softmax(x, axis=-1):
    return jax.nn.softmax(x, axis=axis)

def _gelu(x):
    return jax.nn.gelu(x, approximate=True)

def _silu(x):
    return jax.nn.silu(x)

def _sigmoid(x):
    return jax.nn.sigmoid(x)

def _layernorm(x, axis=-1, eps=1e-05):
    m = jnp.mean(x, axis=axis, keepdims=True)
    v = jnp.var(x, axis=axis, keepdims=True)
    return (x - m) / jnp.sqrt(v + eps)

def _scatter_add(tgt, idx, src, axis=0):
    return tgt.at[idx].add(src)

def _segment_sum(src, seg, n):
    return jax.ops.segment_sum(src, seg, n)
kernel_name = 'mk_adj_resnorm_d4_adj_r2_deb8c4'

def setup_inputs(seed: int=0):
    np.random.seed(seed)
    _w = jnp.asarray

    def _rec_inputs():
        import jax
        import jax.numpy as jnp
        _gk = jax.random.key(seed)
        x = 7.22e-05 + 1 * jax.random.normal(jax.random.fold_in(_gk, 1), (16, 512, 128), jnp.float32)
        _w = (1.0 + jnp.arange(512, dtype=jnp.float32)) ** (-0.5)
        _w = _w / _w.mean()
        _pij = jnp.clip(0.00390625 * _w[:, None] * _w[None, :], 0.0, 1.0)
        _a = jax.random.uniform(jax.random.fold_in(_gk, 2), (512, 512)) < _pij
        _a = jnp.logical_or(_a, jnp.swapaxes(_a, -1, -2))
        _a = jnp.logical_or(_a, jnp.eye(512, dtype=bool))
        _af = _a.astype(jnp.float32)
        _af = _af * jax.random.uniform(jax.random.fold_in(_gk, 3), (512, 512), jnp.float32, 0.05, 0.000976562)
        adj = _af
        return (x, adj)
    x, adj = _rec_inputs()

    def _L0_gnn_setup():
        import jax, jax.numpy as jnp
        import numpy as np
        N_STEPS = 8
        SPATIAL_SCALE = 1.0
        key = jax.random.key(seed)
        ks = jax.random.split(key, 6)
        B, N, D = (32, 512, 128)
        x = jax.random.normal(ks[0], (B, N, D), dtype=jnp.float32)
        adj_mx = jax.random.uniform(ks[1], (N, N), dtype=jnp.float32) / N
        alpha_train = jnp.ones((N,), dtype=jnp.float32)
        w = jnp.eye(D, dtype=jnp.float32) + 0.01 * jax.random.normal(ks[2], (D, D), dtype=jnp.float32)
        d = jax.random.uniform(ks[3], (D,), dtype=jnp.float32)
        fc_in_w = jax.random.normal(ks[4], (D, D), dtype=jnp.float32) * (1.0 / np.sqrt(D))
        fc_in_b = jnp.zeros((D,), dtype=jnp.float32)
        return {'x': x, 'adj_mx': adj_mx, 'alpha_train': alpha_train, 'w': w, 'd': d, 'fc_in_w': fc_in_w, 'fc_in_b': fc_in_b, 'vt': 0}
    _L0_gnn_all = _L0_gnn_setup()
    _L0_gnn_in = {k: v for k, v in _L0_gnn_all.items() if k in ('alpha_train', 'w', 'd', 'fc_in_w', 'fc_in_b')}
    del _L0_gnn_all

    def _L1_gnn_setup():
        import jax, jax.numpy as jnp
        import numpy as np
        B, T, D, H = (64, 1024, 128, 128)
        MAX_SKIP = 4

        def _lstm_last(Wih, Whh, bih, bhh, xs):
            N, _, Hd = xs.shape
            bias = bih + bhh

            def step(carry, x_t):
                h, c = carry
                g = x_t @ Wih.T + h @ Whh.T + bias
                i, f, gg, o = jnp.split(g, 4, axis=-1)
                c = jax.nn.sigmoid(f) * c + jax.nn.sigmoid(i) * jnp.tanh(gg)
                h = jax.nn.sigmoid(o) * jnp.tanh(c)
                return ((h, c), None)
            init = (jnp.zeros((N, Hd), xs.dtype), jnp.zeros((N, Hd), xs.dtype))
            (h_last, _), _ = jax.lax.scan(step, init, jnp.swapaxes(xs, 0, 1))
            return h_last
        key = jax.random.key(seed)
        ks = jax.random.split(key, 8)
        s = 0.05
        x = jax.random.normal(ks[0], (B, T, D), jnp.float32)
        adj = jax.random.uniform(ks[1], (T, T), jnp.float32) / T
        Wg0 = jax.random.normal(ks[2], (D, H), jnp.float32) * s
        bg0 = jnp.zeros((H,), jnp.float32)
        Wg1 = jax.random.normal(ks[3], (H, H), jnp.float32) * s
        bg1 = jnp.zeros((H,), jnp.float32)
        Wih = jax.random.normal(ks[4], (MAX_SKIP, 4 * H, H), jnp.float32) * s
        Whh = jax.random.normal(ks[5], (MAX_SKIP, 4 * H, H), jnp.float32) * s
        bih = jax.random.normal(ks[6], (MAX_SKIP, 4 * H), jnp.float32) * s
        bhh = jax.random.normal(ks[7], (MAX_SKIP, 4 * H), jnp.float32) * s
        return dict(x=x, adj=adj, Wg0=Wg0, bg0=bg0, Wg1=Wg1, bg1=bg1, Wih=Wih, Whh=Whh, bih=bih, bhh=bhh)
    _L1_gnn_all = _L1_gnn_setup()
    _L1_gnn_in = {k: v for k, v in _L1_gnn_all.items() if k in ('Wg0', 'bg0', 'Wg1', 'bg1', 'Wih', 'Whh', 'bih', 'bhh')}
    del _L1_gnn_all

    def _L2_gnn_setup():
        import jax, jax.numpy as jnp
        import numpy as np
        BT, N, D, HEADS, E = (512, 64, 128, 4, 256)
        LRELU_SLOPE = 0.2
        EPS = 1e-08
        key = jax.random.key(seed)
        ks = jax.random.split(key, 8)
        d = D
        return {'H': jax.random.normal(ks[0], (BT, N, d), jnp.float32), 'W_lin': jax.random.normal(ks[1], (d, d), jnp.float32) / np.sqrt(d).astype(np.float32), 'W_val': jax.random.normal(ks[2], (d, d), jnp.float32) / np.sqrt(d).astype(np.float32), 'a': jax.random.normal(ks[3], (HEADS, d // HEADS), jnp.float32), 'W_out': jax.random.normal(ks[4], (d, d), jnp.float32) / np.sqrt(d).astype(np.float32), 'A0': jax.random.uniform(ks[5], (N, N), jnp.float32), 'src': jax.random.randint(ks[6], (E,), 0, N, jnp.int32), 'dst': jax.random.randint(ks[7], (E,), 0, N, jnp.int32)}
    _L2_gnn_all = _L2_gnn_setup()
    _L2_gnn_in = {k: v for k, v in _L2_gnn_all.items() if k in ('W_lin', 'W_val', 'a', 'W_out', 'src', 'dst')}
    del _L2_gnn_all

    def _L3_gnn_setup():
        import jax, jax.numpy as jnp
        import numpy as np
        B, N, IN_DIM, OUT_DIM, H = (2, 2048, 128, 128, 4)
        HEAD_DIM = OUT_DIM // H
        EDGE_P = 0.01
        key = jax.random.key(seed)
        k1, k2, k3 = jax.random.split(key, 3)
        h = jax.random.normal(k1, (B, N, IN_DIM), dtype=jnp.float32)
        W = jax.random.normal(k2, (IN_DIM, 3 * OUT_DIM), dtype=jnp.float32) / np.sqrt(IN_DIM)
        adj = (jax.random.uniform(k3, (N, N)) < EDGE_P).astype(jnp.float32)
        adj = jnp.maximum(adj, jnp.eye(N, dtype=jnp.float32))
        return {'h': h, 'W': W, 'adj': adj}
    _L3_gnn_all = _L3_gnn_setup()
    _L3_gnn_in = {k: v for k, v in _L3_gnn_all.items() if k in ('W',)}
    del _L3_gnn_all
    return {'x': x, 'adj': adj, 'L0_gnn_alpha_train': _L0_gnn_in['alpha_train'], 'L0_gnn_w': _L0_gnn_in['w'], 'L0_gnn_d': _L0_gnn_in['d'], 'L0_gnn_fc_in_w': _L0_gnn_in['fc_in_w'], 'L0_gnn_fc_in_b': _L0_gnn_in['fc_in_b'], 'L1_gnn_Wg0': _L1_gnn_in['Wg0'], 'L1_gnn_bg0': _L1_gnn_in['bg0'], 'L1_gnn_Wg1': _L1_gnn_in['Wg1'], 'L1_gnn_bg1': _L1_gnn_in['bg1'], 'L1_gnn_Wih': _L1_gnn_in['Wih'], 'L1_gnn_Whh': _L1_gnn_in['Whh'], 'L1_gnn_bih': _L1_gnn_in['bih'], 'L1_gnn_bhh': _L1_gnn_in['bhh'], 'L2_gnn_W_lin': _L2_gnn_in['W_lin'], 'L2_gnn_W_val': _L2_gnn_in['W_val'], 'L2_gnn_a': _L2_gnn_in['a'], 'L2_gnn_W_out': _L2_gnn_in['W_out'], 'L2_gnn_src': _L2_gnn_in['src'], 'L2_gnn_dst': _L2_gnn_in['dst'], 'L3_gnn_W': _L3_gnn_in['W']}

def reference(x, adj, L0_gnn_alpha_train, L0_gnn_w, L0_gnn_d, L0_gnn_fc_in_w, L0_gnn_fc_in_b, L1_gnn_Wg0, L1_gnn_bg0, L1_gnn_Wg1, L1_gnn_bg1, L1_gnn_Wih, L1_gnn_Whh, L1_gnn_bih, L1_gnn_bhh, L2_gnn_W_lin, L2_gnn_W_val, L2_gnn_a, L2_gnn_W_out, L2_gnn_src, L2_gnn_dst, L3_gnn_W):
    import jax
    import jax.numpy as jnp

    def _L0_gnn_ref(x, adj_mx, alpha_train, w, d, fc_in_w, fc_in_b, vt):
        import jax, jax.numpy as jnp
        import numpy as np
        N_STEPS = 8
        SPATIAL_SCALE = 1.0
        x0 = jax.lax.stop_gradient(x)
        h = jnp.einsum('bnd,ed->bne', x, fc_in_w) + fc_in_b
        alph = jax.nn.sigmoid(alpha_train)[:, None]
        d_clamped = jnp.clip(d, 0.0, 1.0)
        w_eff = w * d_clamped @ w.T
        dt = jnp.float32(SPATIAL_SCALE / N_STEPS)

        def euler_step(h, _):
            ax = jnp.einsum('nm,bmd->bnd', adj_mx, h)
            f = alph * 0.5 * (ax - h) + h @ w_eff - h + x0
            return (h + dt * f, None)
        h, _ = jax.lax.scan(euler_step, h, None, length=N_STEPS)
        return h

    def _L1_gnn_ref(x, adj, Wg0, bg0, Wg1, bg1, Wih, Whh, bih, bhh):
        import jax, jax.numpy as jnp
        import numpy as np
        B, T, D, H = (64, 1024, 128, 128)
        MAX_SKIP = 4

        def _lstm_last(Wih, Whh, bih, bhh, xs):
            N, _, Hd = xs.shape
            bias = bih + bhh

            def step(carry, x_t):
                h, c = carry
                g = x_t @ Wih.T + h @ Whh.T + bias
                i, f, gg, o = jnp.split(g, 4, axis=-1)
                c = jax.nn.sigmoid(f) * c + jax.nn.sigmoid(i) * jnp.tanh(gg)
                h = jax.nn.sigmoid(o) * jnp.tanh(c)
                return ((h, c), None)
            init = (jnp.zeros((N, Hd), xs.dtype), jnp.zeros((N, Hd), xs.dtype))
            (h_last, _), _ = jax.lax.scan(step, init, jnp.swapaxes(xs, 0, 1))
            return h_last
        h = jax.nn.relu(jnp.einsum('ts,bsh->bth', adj, x @ Wg0 + bg0))
        h = jax.nn.relu(jnp.einsum('ts,bsh->bth', adj, h @ Wg1 + bg1))
        Bv, Tv, Hd = h.shape
        for p in range(1, MAX_SKIP + 1):
            nw = Tv // p
            wins = h[:, :nw * p, :].reshape(Bv * nw, p, Hd)
            last = _lstm_last(Wih[p - 1], Whh[p - 1], bih[p - 1], bhh[p - 1], wins)
            idx = jnp.arange(nw) * p + (p - 1)
            h = h.at[:, idx, :].set(last.reshape(Bv, nw, Hd))
        return h

    def _L2_gnn_ref(H, W_lin, W_val, a, W_out, A0, src, dst):
        import jax, jax.numpy as jnp
        import numpy as np
        BT, N, D, HEADS, E = (512, 64, 128, 4, 256)
        LRELU_SLOPE = 0.2
        EPS = 1e-08
        bt, n, d = H.shape
        h, dh = a.shape
        Xq = (H @ W_lin.T).reshape(bt, n, h, dh)
        Xv = (H @ W_val.T).reshape(bt, n, h, dh)
        Qs = Xq[:, src]
        Kt = Xq[:, dst]
        e = jnp.einsum('behd,hd->beh', jax.nn.leaky_relu(Qs + Kt, LRELU_SLOPE), a)
        e = e + jnp.log(A0[src, dst] + EPS)[None, :, None]
        e_t = e.transpose(1, 0, 2)
        m = jax.ops.segment_max(e_t, src, num_segments=n)
        ex = jnp.exp(e_t - m[src])
        denom = jax.ops.segment_sum(ex, src, num_segments=n)
        attn = ex / denom[src]
        Vt = Xv[:, dst].transpose(1, 0, 2, 3)
        Y = jax.ops.segment_sum(attn[..., None] * Vt, src, num_segments=n)
        Y = Y.transpose(1, 0, 2, 3).reshape(bt, n, d)
        return Y @ W_out.T

    def _L3_gnn_ref(h, W, adj):
        import jax, jax.numpy as jnp
        import numpy as np
        B, N, IN_DIM, OUT_DIM, H = (2, 2048, 128, 128, 4)
        HEAD_DIM = OUT_DIM // H
        EDGE_P = 0.01
        Bn, Nn, _ = h.shape
        qkv = h @ W
        qkv = qkv.reshape(Bn, Nn, 3, H, HEAD_DIM).transpose(2, 0, 3, 1, 4)
        q, k, v = (qkv[0], qkv[1], qkv[2])
        mask = jnp.where(adj == 0, -jnp.inf, 0.0)
        scores = jnp.einsum('bhid,bhjd->bhij', q, k) / np.sqrt(HEAD_DIM) + mask
        attn = jax.nn.softmax(scores, axis=-1)
        out = jnp.einsum('bhij,bhjd->bhid', attn, v)
        return out.transpose(0, 2, 1, 3).reshape(Bn, Nn, OUT_DIM)
    x = _layernorm(x + _L0_gnn_ref(x, adj, L0_gnn_alpha_train, L0_gnn_w, L0_gnn_d, L0_gnn_fc_in_w, L0_gnn_fc_in_b, 0), axis=-1)
    x = _layernorm(x + _L1_gnn_ref(x, adj, L1_gnn_Wg0, L1_gnn_bg0, L1_gnn_Wg1, L1_gnn_bg1, L1_gnn_Wih, L1_gnn_Whh, L1_gnn_bih, L1_gnn_bhh), axis=-1)
    x = _layernorm(x + _L2_gnn_ref(x, L2_gnn_W_lin, L2_gnn_W_val, L2_gnn_a, L2_gnn_W_out, adj, L2_gnn_src, L2_gnn_dst), axis=-1)
    x = _layernorm(x + _L3_gnn_ref(x, L3_gnn_W, adj), axis=-1)
    return x

_drawn_inputs = setup_inputs


def setup_inputs(seed=0):
    import zlib

    import numpy as np

    out = dict(_drawn_inputs(seed))
    spreads = {'L0_gnn_alpha_train': (1.0, 0.6),
     'L0_gnn_fc_in_b': (0.0, 0.1),
     'L1_gnn_bg0': (0.0, 0.8),
     'L1_gnn_bg1': (0.0, 0.8)}
    factors = {'L1_gnn_Wg0': 8.0, 'L1_gnn_Wg1': 8.0, 'L1_gnn_Wih': 8.0, 'L1_gnn_Whh': 8.0}
    for name, (base, spread) in spreads.items():
        noise = np.random.default_rng([zlib.crc32(name.encode()), seed]).standard_normal(out[name].shape)
        drawn = base * np.exp(spread * noise) if base else spread * noise
        out[name] = jnp.asarray(drawn.astype(out[name].dtype))
    for name, factor in factors.items():
        out[name] = (out[name] * factor).astype(out[name].dtype)
    return out
```

```python
from contextlib import ExitStack
from math import comb

import concourse.bass as bass
from concourse import mybir

F32 = mybir.dt.float32
F32R = mybir.dt.float32r
I32 = mybir.dt.int32
ALU = mybir.AluOpType
ACT = mybir.ActivationFunctionType
AX = mybir.AxisListType

P = 128
BATCH = 16
N = 512
D = 128
C = N // P
GB = 4
NG = BATCH // GB
STEPS = 8
DT = 1.0 / STEPS
EPS = 1e-5
SKIPS = 4
EDGES = 256
EC = EDGES // P
HEADS = 4
DH = D // HEADS
BIG = -3.0e38


class Count:

    def __init__(self, sem, per, aside=None):
        self.sem, self.per, self.aside = sem, per, aside

    def at(self, g, n):
        return g * self.per + (self.per + n + 1)


def credit(eng, *counts):
    for c in counts:
        eng.sem_inc(c.sem, c.per)


def wait(eng, c, g, n):
    eng.wait_ge(c.sem, c.at(g, n))


def wait_apart(eng, c, g, n):
    eng.wait_ge(c.sem, c.at(g, n))
    eng.sem_inc(c.aside, 1)


def f(ap):
    return ap.bitcast(F32)


def products(pe, out, lhs, rhs, start=True, stop=True):
    pe.matmul(out, lhs[0], rhs[0], start=start, stop=False)
    pe.matmul(out, lhs[0], rhs[1], start=False, stop=False)
    return pe.matmul(out, lhs[1], rhs[0], start=False, stop=stop)


class Norm:

    def __init__(self, nc, ctx, name, per, aside, eps=None, slots=2):
        sb = lambda n, s: ctx.enter_context(nc.sbuf_tensor(f"{name}_{n}", s, F32))
        self.slots, self.eps = slots, eps
        self.sum = sb("sum", [P, slots, C, D])
        self.stats = sb("stats", [P, slots, C, 6])
        self.mean_var = sb("mean_var", [P, slots, C, 2])
        self.var_eps = sb("var_eps", [P, slots, C])
        self.rstd = sb("rstd", [P, slots, C])
        self.power = sb("power", [P, C])
        c = lambda n: Count(ctx.enter_context(nc.semaphore(f"{name}_{n}")), per, aside)
        self.summed, self.counted, self.averaged = c("summed"), c("counted"), c("averaged")
        self.eps_added, self.rooted, self.normed = c("eps_added"), c("rooted"), c("normed")

    def dve_stats(self, dve, g, n):
        k = n % self.slots
        wait(dve, self.summed, g, n)
        for c in range(C):
            last = dve.bn_stats(self.stats[:, k, c, :], self.sum[:, k, c, :])
        last.then_inc(self.counted.sem, 1)
        wait_apart(dve, self.counted, g, n)
        for c in range(C):
            last = dve.bn_aggr(self.mean_var[:, k, c, :], self.stats[:, k, c, :])
        last.then_inc(self.averaged.sem, 1)

    def pool_root(self, pool, g, n):
        k = n % self.slots
        wait_apart(pool, self.averaged, g, n)
        if self.eps is None:
            ins = pool.tensor_scalar(self.var_eps[:, k, :], self.mean_var[:, k, :, 1], EPS, None, ALU.add)
        else:
            ins = pool.tensor_tensor(self.var_eps[:, k, :], self.mean_var[:, k, :, 1], self.eps[:], ALU.add)
        ins.then_inc(self.eps_added.sem, 1)
        wait_apart(pool, self.eps_added, g, n)
        pool.tensor_tensor(self.rstd[:, k, :], self.var_eps[:, k, :], self.power[:],
                           ALU.pow).then_inc(self.rooted.sem, 1)

    def dve_apply(self, dve, g, n, out):
        k = n % self.slots
        wait(dve, self.rooted, g, n)
        for c in range(C):
            last = dve.tensor_scalar(out(c), self.sum[:, k, c, :], self.mean_var[:, k, c, 0:1],
                                     self.rstd[:, k, c:c + 1], ALU.subtract, ALU.mult)
        last.then_inc(self.normed.sem, 1)

    def start_dve(self, dve):
        credit(dve, self.summed, self.counted, self.averaged, self.normed)

    def start_pool(self, pool):
        credit(pool, self.eps_added, self.rooted)
        pool.memset(self.power[:], -0.5)


def diffusion_setup(nc, d, keep):
    at_s, a2t_s, ct_s, c2t_s, g_s, v_sum, x = keep
    with ExitStack() as ctx:
        sb = lambda n, s, t=F32: ctx.enter_context(nc.sbuf_tensor(n, s, t))
        sem = lambda n: ctx.enter_context(nc.semaphore(n))
        adj = sb("s_adj", [P, C, N])
        adjt = sb("s_adjt", [P, C, N])
        a_s = sb("s_a_split", [P, 2, C, N], F32R)
        pair = sb("s_pair", [P, C, N])
        al_row = sb("s_al_row", [P, N])
        al_col = sb("s_al_col", [P, C])
        be_col = sb("s_be_col", [P, C])
        wt = sb("s_wt", [P, D]); dw = sb("s_dw", [P, D]); dcol = sb("s_dcol", [P, 1])
        fcw = sb("s_fcw", [P, D]); bcol = sb("s_bcol", [P, 1]); bwide = sb("s_bwide", [P, D])
        ident = sb("s_ident", [P, P])
        wp = sb("s_wp", [P, STEPS + 1, D])
        tk = sb("s_tk", [P, STEPS + 1, D])
        ck = sb("s_ck", [P, STEPS + 1, D])
        colsum = sb("s_colsum", [P, 2, N])
        s_all = sb("s_sj", [P, C, 3, D])
        ps_a = ctx.enter_context(nc.psum_tensor("s_ps_a", [P, 4, 512], F32))
        ps_w = ctx.enter_context(nc.psum_tensor("s_ps_w", [P, 4, 512], F32))

        adj_in, small_in, x_in = sem("s_adj_in"), sem("s_small_in"), sem("s_x_in")
        act_alpha, act_hi, dve_lo = sem("s_act_alpha"), sem("s_act_hi"), sem("s_dve_lo")
        dve_step, pe_a, pe_w, dve_w, dve_s = (sem("s_dve_step"), sem("s_pe_a"), sem("s_pe_w"),
                                              sem("s_dve_w"), sem("s_dve_s"))
        pe_t, act_a = sem("s_pe_t"), sem("s_act_a")
        block = ctx.enter_context(nc.Block())
        rows = lambda a: a.rearrange("(c p) m -> p c m", p=P)

        @block.sync
        def _(sp):
            sp.dma_start(al_row[:], d["alpha"].rearrange("(a n) -> a n", a=1).to_broadcast([P, N])).then_inc(small_in, 16)
            sp.dma_start(al_col[:], d["alpha_cols"]).then_inc(small_in, 16)
            sp.dma_start(wt[:], d["wT"]).then_inc(small_in, 16)
            sp.dma_start(dcol[:], d["d"].rearrange("(p a) -> p a", a=1)).then_inc(small_in, 16)
            sp.dma_start(fcw[:], d["fc_w"]).then_inc(small_in, 16)
            sp.dma_start(bcol[:], d["fc_b"].rearrange("(p a) -> p a", a=1)).then_inc(small_in, 16)
            sp.dma_start(ident[:], d["ident"]).then_inc(small_in, 16)
            sp.dma_start(adjt[:], rows(d["adjT"])).then_inc(adj_in, 16)
            sp.dma_start(adj[:], rows(d["adj"])).then_inc(adj_in, 16)
            for b in range(BATCH):
                sp.dma_start(x[:, b], rows(d["x"][b])).then_inc(x_in, 16)
            sp.wait_ge(x_in, 16 * BATCH)

        @block.scalar
        def _(act):
            act.wait_ge(small_in, 7 * 16)
            act.activation(al_row[:], al_row[:], ACT.Tanh, scale=0.5)
            act.activation(al_col[:], al_col[:], ACT.Tanh, scale=0.5).then_inc(act_alpha, 1)
            act.wait_ge(dve_step, 3)
            act.copy(at_s[:, 0], adjt[:]).then_inc(act_hi, 1)
            act.wait_ge(dve_step, 5)
            act.copy(a_s[:, 0], adj[:]).then_inc(act_hi, 1)
            for c in range(C):
                act.wait_ge(pe_a, c + 1)
                act.copy(a2t_s[:, 0, c], ps_a[:, c]).then_inc(act_hi, 1)
            for c in range(C):
                act.wait_ge(pe_a, C + c + 1)
                act.copy(pair[:, c], ps_a[:, c]).then_inc(act_a, 1)
                act.copy(ct_s[:, 0, c], ps_a[:, c]).then_inc(act_hi, 1)
            for c in range(C):
                act.wait_ge(pe_t, c + 1)
                act.copy(a_s[:, 0, c], ps_a[:, c]).then_inc(act_hi, 1)
            for c in range(C):
                act.wait_ge(pe_a, 2 * C + c + 1)
                act.copy(c2t_s[:, 0, c], ps_a[:, c]).then_inc(act_hi, 1)

        @block.vector
        def _(dve):
            dve.wait_ge(act_alpha, 1)
            dve.tensor_scalar(al_row[:], al_row[:], DT / 4, DT / 4, ALU.mult, ALU.add)
            dve.tensor_scalar(al_col[:], al_col[:], DT / 4, DT / 4, ALU.mult, ALU.add).then_inc(dve_step, 1)
            dve.wait_ge(dve_step, 1)
            dve.tensor_scalar(be_col[:], al_col[:], -1.0, 1.0 - DT, ALU.mult, ALU.add)
            dve.wait_ge(adj_in, 32)
            for c in range(C):
                last = dve.tensor_tensor(adjt[:, c], adjt[:, c], al_row[:], ALU.mult)
            last.then_inc(dve_step, 1)
            dve.wait_ge(dve_step, 2)
            for c in range(C):
                blk = adjt[:, c, c * P:(c + 1) * P]
                last = dve.scalar_tensor_tensor(blk, ident[:], be_col[:, c:c + 1], blk, ALU.mult, ALU.add)
            last.then_inc(dve_step, 1)
            for c in range(C):
                last = dve.tensor_scalar(adj[:, c], adj[:, c], al_col[:, c:c + 1], None, ALU.mult)
            last.then_inc(dve_step, 1)
            dve.wait_ge(dve_step, 4)
            for c in range(C):
                blk = adj[:, c, c * P:(c + 1) * P]
                last = dve.scalar_tensor_tensor(blk, ident[:], be_col[:, c:c + 1], blk, ALU.mult, ALU.add)
            last.then_inc(dve_step, 1)
            dve.tensor_scalar(dcol[:], dcol[:], 0.0, 1.0, ALU.max, ALU.min).then_inc(dve_w, 1)
            dve.wait_ge(dve_w, 1)
            dve.tensor_scalar(dw[:], wt[:], dcol[:], None, ALU.mult)
            dve.tensor_copy(wp[:, 0], ident[:])
            dve.tensor_scalar(bwide[:], ident[:], 0.0, bcol[:], ALU.mult, ALU.add).then_inc(dve_w, 1)
            dve.wait_ge(act_hi, 1)
            dve.tensor_tensor(at_s[:, 1], adjt[:], f(at_s[:, 0]), ALU.subtract).then_inc(dve_lo, 1)
            dve.wait_ge(act_hi, 2)
            dve.tensor_tensor(a_s[:, 1], adj[:], f(a_s[:, 0]), ALU.subtract).then_inc(dve_lo, 1)
            for n, (lo, k) in enumerate(((1, 1), (2, 1), (3, 2), (5, 4))):
                dve.wait_ge(pe_w, n + 1)
                dve.tensor_scalar(wp[:, lo:lo + k], ps_w[:, 0, 0:k * D].rearrange("p (k d) -> p k d", k=k),
                                  DT if n == 0 else 1.0, None, ALU.mult).then_inc(dve_w, 1)
            for c in range(C):
                dve.wait_ge(act_hi, 2 + c + 1)
                dve.tensor_tensor(a2t_s[:, 1, c], ps_a[:, c], f(a2t_s[:, 0, c]), ALU.subtract).then_inc(dve_lo, 1)
            dve.wait_ge(dve_w, 6)
            for s in range(STEPS):
                for k in range(STEPS - s):
                    if s == 0:
                        last = dve.tensor_scalar(tk[:, k], wp[:, 0], DT, None, ALU.mult)
                    else:
                        last = dve.scalar_tensor_tensor(tk[:, k], wp[:, s], DT * comb(k + s, k), tk[:, k],
                                                        ALU.mult, ALU.add)
                last.then_inc(dve_s, 1)
                dve.wait_ge(dve_s, s + 1)
            dve.wait_ge(pe_w, 6)
            for q in range(STEPS + 1):
                k = STEPS - q
                src = ps_w[:, 1 + q // 4, (q % 4) * D:(q % 4 + 1) * D]
                if k == STEPS:
                    last = dve.tensor_copy(tk[:, k], src)
                else:
                    last = dve.scalar_tensor_tensor(tk[:, k], src, float(comb(STEPS, k)), tk[:, k], ALU.mult, ALU.add)
            last.then_inc(dve_w, 1)
            dve.wait_ge(dve_w, 7)
            for j in range(3):
                last = dve.tensor_copy(g_s[:, 0, :, j], tk[:, 3 * j:3 * j + 3])
            last.then_inc(dve_w, 1)
            dve.wait_ge(dve_w, 8)
            for j in range(3):
                last = dve.tensor_tensor(g_s[:, 1, :, j], tk[:, 3 * j:3 * j + 3], f(g_s[:, 0, :, j]), ALU.subtract)
            last.then_inc(dve_w, 1)
            dve.wait_ge(pe_w, 7)
            for q in range(STEPS + 1):
                k = STEPS - q
                src = ps_w[:, 1 + q // 4, (q % 4) * D:(q % 4 + 1) * D]
                last = dve.tensor_scalar(ck[:, k], src, float(comb(STEPS, k)), None, ALU.mult)
            last.then_inc(dve_w, 1)
            for c in range(C):
                dve.wait_ge(act_hi, 6 + c + 1)
                dve.tensor_tensor(ct_s[:, 1, c], ps_a[:, c], f(ct_s[:, 0, c]), ALU.subtract).then_inc(dve_lo, 1)
            for i, part in enumerate((at_s, a2t_s)):
                last = dve.tensor_reduce(colsum[:, i], f(part[:, 0]).rearrange("p c n -> p n c"), AX.X, ALU.add)
            last.then_inc(dve_w, 1)
            for c in range(C):
                dve.wait_ge(act_hi, 10 + c + 1)
                dve.tensor_tensor(a_s[:, 1, c], ps_a[:, c], f(a_s[:, 0, c]), ALU.subtract).then_inc(dve_lo, 1)
            for c in range(C):
                dve.wait_ge(act_hi, 14 + c + 1)
                dve.tensor_tensor(c2t_s[:, 1, c], ps_a[:, c], f(c2t_s[:, 0, c]), ALU.subtract).then_inc(dve_lo, 1)
            for i, part in enumerate((at_s, a2t_s)):
                for c in range(C):
                    dve.wait_ge(dve_w, 11 + i * C + c)
                    dve.tensor_tensor(colsum[:, i], colsum[:, i], f(part[:, 1, c]), ALU.add).then_inc(dve_w, 1)
            for c in range(C):
                dve.wait_ge(pe_w, 8 + c)
                dve.tensor_tensor(s_all[:, c], ps_w[:, c % 2, 0:3 * D].rearrange("p (j d) -> p j d", j=3),
                                  ck[:, 0:STEPS + 1:3], ALU.add).then_inc(dve_s, 1)
            for c in range(C):
                dve.wait_ge(pe_w, 12 + c)
                dve.tensor_tensor(v_sum[:, c], ps_w[:, 2 + c % 2, 0:D], s_all[:, c, 0], ALU.add).then_inc(dve_s, 1)

        @block.tensor
        def _(pe):
            pe.wait_ge(dve_w, 2)
            pe.matmul(ps_w[:, 0, 0:D], dw[:], wt[:], start=True, stop=True).then_inc(pe_w, 1)
            pe.wait_ge(dve_w, 3)
            pe.matmul(ps_w[:, 0, 0:D], wp[:, 1], wp[:, 1], start=True, stop=True).then_inc(pe_w, 1)
            pe.wait_ge(dve_w, 4)
            pe.matmul(ps_w[:, 0, 0:2 * D], wp[:, 2], wp[:, 1:3], start=True, stop=True).then_inc(pe_w, 1)
            pe.wait_ge(dve_w, 5)
            pe.matmul(ps_w[:, 0, 0:4 * D], wp[:, 4], wp[:, 1:5], start=True, stop=True).then_inc(pe_w, 1)
            pe.wait_ge(dve_lo, 2)
            for m in range(C):
                for k in range(C):
                    last = products(pe, ps_a[:, m], [a_s[:, h, k, m * P:(m + 1) * P] for h in range(2)],
                                    [at_s[:, h, k] for h in range(2)], k == 0, k == C - 1)
                last.then_inc(pe_a, 1)
            pe.wait_ge(dve_w, 6)
            for bank, lo, k in ((1, 0, 4), (2, 4, 4), (3, 8, 1)):
                last = pe.matmul(ps_w[:, bank, 0:k * D], fcw[:], wp[:, lo:lo + k], start=True, stop=True)
            last.then_inc(pe_w, 2)
            pe.wait_ge(dve_w, 7)
            for bank, lo, k in ((1, 0, 4), (2, 4, 4), (3, 8, 1)):
                last = pe.matmul(ps_w[:, bank, 0:k * D], bwide[:], wp[:, lo:lo + k], start=True, stop=True)
            last.then_inc(pe_w, 1)
            pe.wait_ge(dve_lo, 2 + C)
            for m in range(C):
                for k in range(C):
                    last = products(pe, ps_a[:, m], [a_s[:, h, k, m * P:(m + 1) * P] for h in range(2)],
                                    [a2t_s[:, h, k] for h in range(2)], k == 0, k == C - 1)
                last.then_inc(pe_a, 1)
            pe.wait_ge(act_a, C)
            pe.wait_ge(dve_lo, 2 + 2 * C)
            for m in range(C):
                for k in range(C):
                    last = pe.transpose(ps_a[:, m, k * P:(k + 1) * P], pair[:, k, m * P:(m + 1) * P], ident[:])
                last.then_inc(pe_t, 1)
            pe.wait_ge(dve_lo, 2 + 3 * C)
            for m in range(C):
                for k in range(C):
                    last = products(pe, ps_a[:, m], [a_s[:, h, k, m * P:(m + 1) * P] for h in range(2)],
                                    [ct_s[:, h, k] for h in range(2)], k == 0, k == C - 1)
                last.then_inc(pe_a, 1)
            pe.wait_ge(dve_lo, 2 + 4 * C)
            pe.wait_ge(dve_w, 11 + 2 * C)
            for c in range(C):
                if c >= 2:
                    pe.wait_ge(dve_s, STEPS + c - 1)
                for i in range(2):
                    last = pe.matmul(ps_w[:, c % 2, 0:3 * D], colsum[:, i, c * P:(c + 1) * P],
                                     ck[:, i + 1:STEPS + 1:3], start=i == 0, stop=i == 1)
                last.then_inc(pe_w, 1)
            pe.wait_ge(dve_s, STEPS + C)
            for c in range(C):
                if c >= 2:
                    pe.wait_ge(dve_s, STEPS + C + c - 1)
                for j, part in ((1, ct_s), (2, c2t_s)):
                    for k in range(C):
                        for h in range(2):
                            last = pe.matmul(ps_w[:, 2 + c % 2, 0:D], f(part[:, h, k, c * P:(c + 1) * P]), s_all[:, k, j],
                                             start=(j, k, h) == (1, 0, 0), stop=(j, k, h) == (2, C - 1, 1))
                last.then_inc(pe_w, 1)


def diffusion(nc, d, keep):
    at_s, a2t_s, ct_s, c2t_s, g_s, v_sum, x = keep
    with ExitStack() as ctx:
        sb = lambda n, s, t=F32: ctx.enter_context(nc.sbuf_tensor(n, s, t))
        count = lambda n, per: Count(ctx.enter_context(nc.semaphore(n)), per, aside)
        x_s = sb("x_split", [P, 2, GB, C, D], F32R)
        xt = sb("xt", [P, 2, N])
        base_s = sb("base_split", [P, 2, 3, 2, N], F32R)
        x_v = sb("x_plus_v", [P, GB, C, D])
        rest = sb("rest", [P, C, GB, D])
        z_s = sb("z_split", [P, 2, 2, C, GB, D], F32R)
        aside = ctx.enter_context(nc.semaphore("aside"))
        norm = Norm(nc, ctx, "ln0", C, aside)
        ps_base = ctx.enter_context(nc.psum_tensor("ps_base", [P, 2, 2, N], F32))
        ps_z = ctx.enter_context(nc.psum_tensor("ps_z", [P, 2, N], F32))
        ps_out = ctx.enter_context(nc.psum_tensor("ps_out", [P, 2, N], F32))

        xt_in = [count(f"xt_in{q}", 16 * GB // 2) for q in range(2)]
        x_hi, x_lo, xt_hi, xt_lo, xv_done = (count(n, GB) for n in ("x_hi", "x_lo", "xt_hi", "xt_lo", "xv_done"))
        base_ready, base_hi, base_lo = (count(n, 2 * GB) for n in ("base_ready", "base_hi", "base_lo"))
        z_ready, z_hi, z_lo, rest_done = (count(n, C * GB) for n in ("z_ready", "z_hi", "z_lo", "rest_done"))
        out_ready = count("out_ready", C)
        block = ctx.enter_context(nc.Block())

        @block.sync
        def _(sp):
            for q in range(2):
                credit(sp, xt_in[q])
            with sp.Fori(0, NG) as g:
                for b in range(GB):
                    wait(sp, xt_lo, g, b - 2)
                    sp.dma_start(xt[:, b % 2], d["xT"][bass.ds(g * GB + b, 1)].rearrange("a d n -> (a d) n")
                                 ).then_inc(xt_in[b % 2].sem, 16)

        @block.gpsimd
        def _(pool):
            credit(pool, x_hi, x_lo, xt_hi, xt_lo, xv_done)
            norm.start_pool(pool)
            rows = lambda g, b: x[:, bass.ds(g * GB + b, 1)].rearrange("p a c d -> p (a c) d")

            def split(g, n):
                b = n % GB
                wait_apart(pool, base_lo, g, 2 * (n - GB) + 1)
                pool.tensor_copy(x_s[:, 0, b], rows(g, n)).then_inc(x_hi.sem, 1)
                wait_apart(pool, x_hi, g, n)
                pool.tensor_tensor(x_s[:, 1, b], rows(g, n), f(x_s[:, 0, b]), ALU.subtract).then_inc(x_lo.sem, 1)

            def split_t(g, n):
                b = n % GB
                wait_apart(pool, xt_in[b % 2], g, 16 * (n // 2) + 15)
                wait_apart(pool, z_lo, g, C * (n - 2) + C - 1)
                pool.tensor_copy(base_s[:, b % 2, 0, 0], xt[:, b % 2]).then_inc(xt_hi.sem, 1)
                wait_apart(pool, xt_hi, g, n)
                pool.tensor_tensor(base_s[:, b % 2, 0, 1], xt[:, b % 2], f(base_s[:, b % 2, 0, 0]),
                                   ALU.subtract).then_inc(xt_lo.sem, 1)
                wait_apart(pool, rest_done, g, C * (n - GB) + C - 1)
                pool.tensor_tensor(x_v[:, b], rows(g, n), v_sum[:], ALU.add).then_inc(xv_done.sem, 1)

            def roots(g):
                for c in range(C):
                    norm.pool_root(pool, g, c)

            split(0, 0)
            split(0, 1)
            split_t(0, 0)
            split(0, 2)
            split_t(0, 1)
            split(0, 3)
            with pool.Fori(0, NG - 1) as g:
                for b in range(GB):
                    split(g, GB + b)
                    split_t(g, 2 + b)
                roots(g)
            split_t(NG - 1, 2)
            split_t(NG - 1, 3)
            roots(NG - 1)

        @block.scalar
        def _(act):
            credit(act, base_hi, z_hi)
            with act.Fori(0, NG) as g:
                def base(b):
                    for i in range(2):
                        wait(act, base_ready, g, 2 * b + i)
                        wait(act, z_lo, g, C * (b - 2) + C - 1)
                        act.copy(base_s[:, b % 2, i + 1, 0], ps_base[:, b % 2, i]).then_inc(base_hi.sem, 1)
                base(0)
                for b in range(GB):
                    if b + 1 < GB:
                        base(b + 1)
                    if b == 0:
                        wait(act, out_ready, g, -1)
                    for c in range(C):
                        wait(act, z_ready, g, C * b + c)
                        act.copy(z_s[:, :, 0, c, b], ps_z[:, c % 2, D:3 * D].rearrange("p (j d) -> p j d", j=2)
                                 ).then_inc(z_hi.sem, 1)

        @block.vector
        def _(dve):
            credit(dve, base_lo, z_lo, rest_done)
            norm.start_dve(dve)
            with dve.Fori(0, NG) as g:
                def base(b):
                    for i in range(2):
                        wait(dve, base_hi, g, 2 * b + i)
                        dve.tensor_tensor(base_s[:, b % 2, i + 1, 1], ps_base[:, b % 2, i],
                                          f(base_s[:, b % 2, i + 1, 0]), ALU.subtract).then_inc(base_lo.sem, 1)
                base(0)
                for b in range(GB):
                    if b + 1 < GB:
                        base(b + 1)
                    wait(dve, xv_done, g, b)
                    for c in range(C):
                        wait(dve, z_hi, g, C * b + c)
                        dve.tensor_tensor(rest[:, c, b], ps_z[:, c % 2, 0:D], x_v[:, b, c],
                                          ALU.add).then_inc(rest_done.sem, 1)
                        dve.tensor_tensor(z_s[:, :, 1, c, b], ps_z[:, c % 2, D:3 * D].rearrange("p (j d) -> p j d", j=2),
                                          f(z_s[:, :, 0, c, b]), ALU.subtract).then_inc(z_lo.sem, 1)
                for c in range(C):
                    wait(dve, out_ready, g, c)
                    wait(dve, norm.normed, g, c - 2)
                    wait(dve, rest_done, g, C * GB - 1)
                    dve.tensor_tensor(norm.sum[:, c % 2], ps_out[:, c % 2].rearrange("p (b d) -> p b d", b=GB),
                                      rest[:, c], ALU.add).then_inc(norm.summed.sem, 1)
                    norm.dve_stats(dve, g, c)
                    norm.dve_apply(dve, g, c, lambda b: x[:, bass.ds(g * GB + b, 1), c].rearrange("p a d -> p (a d)"))

        @block.tensor
        def _(pe):
            credit(pe, base_ready, z_ready, out_ready)
            with pe.Fori(0, NG) as g:
                def base(b):
                    wait(pe, x_lo, g, b)
                    for i, m in enumerate((at_s, a2t_s)):
                        wait(pe, base_lo, g, 2 * (b - 2) + i)
                        for c in range(C):
                            last = products(pe, ps_base[:, b % 2, i], [x_s[:, h, b, c] for h in range(2)],
                                            [m[:, h, c] for h in range(2)], c == 0, c == C - 1)
                        last.then_inc(base_ready.sem, 1)
                base(0)
                for b in range(GB):
                    if b + 1 < GB:
                        base(b + 1)
                    wait(pe, xt_lo, g, b)
                    wait(pe, base_lo, g, 2 * b + 1)
                    for c in range(C):
                        wait(pe, z_lo, g, C * b + c - 2)
                        for i in range(3):
                            last = products(pe, ps_z[:, c % 2, 0:3 * D],
                                            [base_s[:, b % 2, i, h, c * P:(c + 1) * P] for h in range(2)],
                                            [g_s[:, h, i] for h in range(2)], i == 0, i == 2)
                        last.then_inc(z_ready.sem, 1)
                wait(pe, z_lo, g, C * GB - 1)
                for c in range(C):
                    wait(pe, norm.summed, g, c - 2)
                    for j, m in enumerate((ct_s, c2t_s)):
                        for k in range(C):
                            last = products(pe, ps_out[:, c % 2], [m[:, h, k, c * P:(c + 1) * P] for h in range(2)],
                                            [z_s[:, j, h, k] for h in range(2)], j + k == 0, (j, k) == (1, C - 1))
                    last.then_inc(out_ready.sem, 1)


def lstm_steps():
    steps = [(1, 0, b, N, "igo") for b in range(GB)]
    for p in range(2, SKIPS + 1):
        steps += [(p, s, q, N // p, "igfo" if s else "igo") for s in range(p) for q in range(2)]
    return steps


LSTM = lstm_steps()
GATE = {"i": 0, "f": 1, "g": 2, "o": 3}
FIRST_GATE = [sum(len(t[4]) for t in LSTM[:k]) for k in range(len(LSTM) + 1)]


def gate_number(k, gate):
    return FIRST_GATE[k] + LSTM[k][4].index(gate)


def windows(tile, k):
    p, s, q, w, _ = LSTM[k]
    if p == 1:
        return tile[:, q]
    return tile[:, 2 * q:2 * q + 2, s:s + p * (w - 1) + 1:p]


def flat(tile, k):
    p, s, q, w, _ = LSTM[k]
    if p == 1:
        return tile
    return tile[:, 0:2 * w].rearrange("p (b w) -> p b w", b=2)


def columns(k):
    return LSTM[k][3] * (1 if LSTM[k][0] == 1 else 2)


def dilated(nc, d, x):
    with ExitStack() as ctx:
        sb = lambda n, s, t=F32: ctx.enter_context(nc.sbuf_tensor(n, s, t))
        sem = lambda n: ctx.enter_context(nc.semaphore(n))
        at_s = sb("d_at_split", [P, 2, C, N], F32R)
        wg_s = sb("d_wg_split", [P, 2, 2, D], F32R)
        wih_s = sb("d_wih_split", [P, 2, SKIPS, 4 * D], F32R)
        whh_s = sb("d_whh_split", [P, 2, SKIPS, 4 * D], F32R)
        gate_b = sb("d_gate_bias", [P, SKIPS, 4])
        ident = sb("d_ident", [P, P])
        ident_r = sb("d_ident_r", [P, P], F32R)
        b_stack = sb("d_b_stack", [96, 2, D], F32R)
        r_stack = sb("d_r_stack", [96, N], F32R)
        x_s = sb("d_x_split", [P, 2, GB, C, D], F32R)
        ax_s = sb("d_ax_split", [P, GB, 2, N], F32R)
        h1_s = sb("d_h1_split", [P, GB, 2, C, D], F32R)
        ps = ctx.enter_context(nc.psum_tensor("d_banks", [P, 8, N], F32))
        K, GATES = len(LSTM), FIRST_GATE[-1]
        aside = sem("d_aside")
        count = lambda n, per: Count(sem(n), per, aside)
        count = lambda n, per: Count(sem(n), per, aside)
        x_hi, x_lo = count("d_x_hi", GB), count("d_x_lo", GB)
        conv_ready, conv_hi, conv_lo = (count(n, 4 * GB) for n in ("d_conv_ready", "d_conv_hi", "d_conv_lo"))
        RING = 6
        assert GATES % RING == 0 and K == 22
        UNITS_AT = {6: 0, 8: 1, 10: 2, 12: 3, 14: 4, 16: 5, 18: 6, 20: 7}
        TAIL = ((8,), (9,), (10,), (11,))
        OUT_STAGE = 3 * GB

        def split(pool, g, ahead):
            for b in range(GB):
                src = x[:, bass.ds(g * GB + (ahead * GB + b), 1)].rearrange("p a c d -> p (a c) d")
                wait_apart(pool, conv_hi, g, b - 4 * GB * (1 - ahead))
                pool.tensor_copy(x_s[:, 0, b], src).then_inc(x_hi.sem, 1)
                wait_apart(pool, x_hi, g, b + GB * ahead)
                pool.tensor_tensor(x_s[:, 1, b], src, f(x_s[:, 0, b]), ALU.subtract).then_inc(x_lo.sem, 1)

        def unit(pe, g, n):
            stage, b = n // GB % 4, n % GB
            bank = ps[:, RING + n % 2]
            if stage == 0:
                wait(pe, x_lo, g, n // (4 * GB) * GB + b)
            wait(pe, conv_lo, g, n - 2)
            if stage == 0:
                for c in range(C):
                    last = products(pe, bank, [x_s[:, h, b, c] for h in range(2)],
                                    [at_s[:, h, c] for h in range(2)], c == 0, c == C - 1)
            elif stage == 1:
                for c in range(C):
                    cols = slice(c * P, (c + 1) * P)
                    products(pe, bank[:, cols], [ax_s[:, b, h, cols] for h in range(2)],
                             [wg_s[:, h, 0] for h in range(2)], True, False)
                    last = pe.matmul(bank[:, cols], r_stack[:, cols], b_stack[:, 0], start=False, stop=True)
            elif stage == 2:
                for c in range(C):
                    last = products(pe, bank, [h1_s[:, b, h, c] for h in range(2)],
                                    [at_s[:, h, c] for h in range(2)], c == 0, c == C - 1)
            else:
                products(pe, bank, [wg_s[:, h, 1] for h in range(2)],
                         [ax_s[:, b, h] for h in range(2)], True, False)
                last = pe.matmul(bank, b_stack[:, 1], r_stack[:], start=False, stop=True)
            last.then_inc(conv_ready.sem, 1)

        def unit_hi(act, g, n):
            stage, b = n // GB % 4, n % GB
            bank = ps[:, RING + n % 2]
            wait(act, conv_ready, g, n)
            if stage == 1:
                act.activation(h1_s[:, b, 0], bank.rearrange("p (c d) -> p c d", c=C), ACT.Relu
                               ).then_inc(conv_hi.sem, 1)
            elif stage == 3:
                act.activation(h_s[:, 0, b], bank, ACT.Relu).then_inc(conv_hi.sem, 1)
            else:
                act.copy(ax_s[:, b, 0], bank).then_inc(conv_hi.sem, 1)

        def unit_lo(dve, g, n):
            stage, b = n // GB % 4, n % GB
            bank = ps[:, RING + n % 2]
            wait(dve, conv_hi, g, n)
            if stage == 1:
                ins = dve.scalar_tensor_tensor(h1_s[:, b, 1], bank.rearrange("p (c d) -> p c d", c=C), 0.0,
                                               f(h1_s[:, b, 0]), ALU.max, ALU.subtract)
            elif stage == 3:
                ins = dve.scalar_tensor_tensor(h_s[:, 1, b], bank, 0.0, f(h_s[:, 0, b]), ALU.max, ALU.subtract)
            else:
                ins = dve.tensor_tensor(ax_s[:, b, 1], bank, f(ax_s[:, b, 0]), ALU.subtract)
            ins.then_inc(conv_lo.sem, 1)

        with ExitStack() as tmp:
            tb = lambda n, s, t=F32: tmp.enter_context(nc.sbuf_tensor(n, s, t))
            at = tb("d_at", [P, C, N])
            wg = tb("d_wg", [P, 2, D])
            wih = tb("d_wih", [P, SKIPS, 4 * D])
            whh = tb("d_whh", [P, SKIPS, 4 * D])
            bih = tb("d_bih", [P, SKIPS, 4])
            bhh = tb("d_bhh", [P, SKIPS, 4])
            brow = tb("d_brow", [96, 2, D])
            rsum = tb("d_rsum", [96, N])
            ones = tb("d_ones", [P, 96], F32R)
            small_in, adj_in, w_in = (tmp.enter_context(nc.semaphore(n)) for n in ("d_small_in", "d_adj_in", "d_w_in"))
            act_hi, dve_lo, pe_sum, cleared, halved = (tmp.enter_context(nc.semaphore(n)) for n in
                                              ("d_act_hi", "d_dve_lo", "d_pe_sum", "d_cleared", "d_halved"))
            block = tmp.enter_context(nc.Block())

            @block.sync
            def _(sp):
                sp.dma_start(at[:], d["adjT"].rearrange("(c p) m -> p c m", p=P)).then_inc(adj_in, 16)
                for r in range(3):
                    for layer in range(2):
                        sp.dma_start(brow[32 * r:32 * r + 1, layer], d[f"bg{layer}"].rearrange("(a n) -> a n", a=1)
                                     ).then_inc(small_in, 16)
                for layer in range(2):
                    sp.dma_start(wg[:, layer], d[f"Wg{layer}"]).then_inc(small_in, 16)
                sp.dma_start(bih[:], d["bih"]).then_inc(small_in, 16)
                sp.dma_start(bhh[:], d["bhh"]).then_inc(small_in, 16)
                sp.dma_start(ident[:], d["ident"]).then_inc(small_in, 16)
                sp.dma_start(wih[:], d["WihT"]).then_inc(w_in, 16)
                sp.dma_start(whh[:], d["WhhT"]).then_inc(w_in, 16)

            @block.gpsimd
            def _(pool):
                credit(pool, x_hi, x_lo)
                pool.memset(f(b_stack[:]), 0.0)
                pool.memset(f(r_stack[:]), 0.0).then_inc(cleared, 1)
                split(pool, 0, 0)

            @block.scalar
            def _(act):
                credit(act, conv_hi)
                act.wait_ge(adj_in, 16)
                act.copy(at_s[:, 0], at[:]).then_inc(act_hi, 1)
                for u in range(2 * GB):
                    unit_hi(act, 0, u)
                act.wait_ge(w_in, 32)
                act.copy(wih_s[:, 0, 0], wih[:, 0])
                act.wait_ge(halved, 1)
                act.copy(wih_s[:, 0, 1:], wih[:, 1:])
                act.copy(whh_s[:, 0], whh[:]).then_inc(act_hi, 1)
                for u in range(2 * GB, OUT_STAGE):
                    unit_hi(act, 0, u)

            @block.vector
            def _(dve):
                credit(dve, conv_lo)
                dve.memset(f(ones[:]), 1.0)
                dve.wait_ge(adj_in, 16)
                dve.wait_ge(act_hi, 1)
                dve.tensor_tensor(at_s[:, 1], at[:], f(at_s[:, 0]), ALU.subtract).then_inc(dve_lo, 1)
                dve.wait_ge(small_in, 11 * 16)
                dve.tensor_copy(wg_s[:, 0], wg[:])
                dve.tensor_copy(ident_r[:], ident[:])
                dve.tensor_tensor(gate_b[:], bih[:], bhh[:], ALU.add).then_inc(dve_lo, 1)
                dve.wait_ge(cleared, 1)
                for r in range(3):
                    last = dve.tensor_copy(b_stack[32 * r:32 * r + 1], brow[32 * r:32 * r + 1])
                last.then_inc(dve_lo, 1)
                unit_lo(dve, 0, 0)
                dve.wait_ge(dve_lo, 3)
                dve.tensor_tensor(wg_s[:, 1], wg[:], f(wg_s[:, 0]), ALU.subtract)
                for gate in "ifo":
                    dve.tensor_scalar(gate_b[:, :, GATE[gate]], gate_b[:, :, GATE[gate]], 0.5, None, ALU.mult)
                dve.tensor_tensor(b_stack[64:65], brow[64:65], f(b_stack[64:65]), ALU.subtract)
                for u in range(1, GB - 1):
                    unit_lo(dve, 0, u)
                dve.wait_ge(pe_sum, 1)
                dve.tensor_copy(rsum[:], ps[0:96, 0])
                for r in range(3):
                    last = dve.tensor_copy(r_stack[32 * r:32 * r + 1], ps[32 * r:32 * r + 1, 0])
                last.then_inc(dve_lo, 1)
                dve.wait_ge(dve_lo, 4)
                dve.tensor_tensor(r_stack[32:33], rsum[32:33], f(r_stack[32:33]), ALU.subtract).then_inc(dve_lo, 1)
                for u in range(GB - 1, 2 * GB):
                    unit_lo(dve, 0, u)
                dve.wait_ge(w_in, 32)
                dve.tensor_scalar(wih[:, 1:], wih[:, 1:], 0.5, None, ALU.mult)
                dve.tensor_scalar(whh[:], whh[:], 0.5, None, ALU.mult).then_inc(halved, 1)
                for u in range(2 * GB, OUT_STAGE):
                    unit_lo(dve, 0, u)
                dve.wait_ge(act_hi, 2)
                dve.tensor_tensor(wih_s[:, 1], wih[:], f(wih_s[:, 0]), ALU.subtract)
                dve.tensor_tensor(whh_s[:, 1], whh[:], f(whh_s[:, 0]), ALU.subtract)

            @block.tensor
            def _(pe):
                credit(pe, conv_ready)
                pe.wait_ge(dve_lo, 1)
                for u in range(OUT_STAGE):
                    if u == GB - 2:
                        for c in range(C):
                            for h in range(2):
                                last = pe.matmul(ps[0:96, 0], ones[:], at_s[:, h, c], start=c + h == 0,
                                                 stop=(c, h) == (C - 1, 1))
                        last.then_inc(pe_sum, 1)
                    if u == GB:
                        pe.wait_ge(dve_lo, 5)
                    unit(pe, 0, u)

        h_s = sb("d_h_split", [P, 2, GB, N], F32R)
        cell_s = sb("d_cell_split", [P, 2, 2, N], F32R)
        gates = sb("d_gates", [P, 2, 4, N])
        state = sb("d_state", [P, 2, N])
        ig = sb("d_ig", [P, 2, N])
        fc = sb("d_fc", [P, 2, N])
        tc = sb("d_tc", [P, 2, N])
        h2 = sb("d_h2", [P, 2, N])
        norm = Norm(nc, ctx, "ln1", GB, aside)
        gate_ready, gate_tanh = count("d_gate_ready", GATES), count("d_gate_tanh", GATES)
        LATER = sum(1 for t in LSTM if t[1])
        ig_done, fc_done = count("d_ig_done", LATER), count("d_fc_done", LATER)
        state_done, state_tanh, h2_done, h2_hi, h2_lo = (
            count("d_" + n, K) for n in ("state_done", "state_tanh", "h2_done", "h2_hi", "h2_lo"))
        turned = count("d_turned", GB)
        block = ctx.enter_context(nc.Block())
        @block.gpsimd
        def _(pool):
            norm.start_pool(pool)

            def roots(g):
                for b in range(GB):
                    norm.pool_root(pool, g, b)

            with pool.Fori(0, NG - 1) as g:
                split(pool, g, 1)
                roots(g)
            roots(NG - 1)

        @block.scalar
        def _(act):
            credit(act, gate_tanh, state_tanh)

            def gate_tanhs(g, k, which):
                p, s, q, _, names = LSTM[k]
                for gate in which:
                    if gate in names:
                        n = gate_number(k, gate)
                        wait(act, gate_ready, g, n)
                        act.activation(gates[:, k % 2, GATE[gate], 0:columns(k)], ps[:, n % RING, 0:columns(k)],
                                       ACT.Tanh, bias=gate_b[:, p - 1, GATE[gate]:GATE[gate] + 1],
                                       scale=1.0 if gate == "g" else 0.5).then_inc(gate_tanh.sem, 1)

            def state_tanhs(g, k):
                wait(act, state_done, g, k)
                act.activation(tc[:, k % 2, 0:columns(k)], state[:, k % 2, 0:columns(k)], ACT.Tanh,
                               scale=0.5).then_inc(state_tanh.sem, 1)

            def body(g, ahead):
                unit_hi(act, g, OUT_STAGE)
                for k in range(K):
                    if k < GB - 1:
                        unit_hi(act, g, OUT_STAGE + k + 1)
                    if k >= GB:
                        state_tanhs(g, k - 1)
                    if ahead and k in UNITS_AT:
                        unit_hi(act, g, 4 * GB + UNITS_AT[k])
                    wait(act, h2_done, g, k - 2)
                    gate_tanhs(g, k, "ig")
                    if 0 < k < GB:
                        state_tanhs(g, k - 1)
                    gate_tanhs(g, k, "fo")
                state_tanhs(g, K - 1)
                if ahead:
                    for b in range(GB):
                        for u in TAIL[b]:
                            unit_hi(act, g, 4 * GB + u)

            with act.Fori(0, NG - 1) as g:
                body(g, True)
            body(NG - 1, False)

        @block.vector
        def _(dve):
            credit(dve, ig_done, fc_done, state_done, h2_done, h2_hi, h2_lo)
            norm.start_dve(dve)

            def output(g, k):
                p, s, q, _, _ = LSTM[k]
                w = columns(k)
                gk, hk = gates[:, k % 2], h2[:, k % 2, 0:w]
                hi, lo = ((flat(cell_s[:, k % 2, 0], k), flat(cell_s[:, k % 2, 1], k)) if s < p - 1 else
                          (windows(h_s[:, 0], k), windows(h_s[:, 1], k)))
                wait(dve, gate_tanh, g, gate_number(k, "o"))
                wait(dve, state_tanh, g, k)
                dve.scalar_tensor_tensor(hk, gk[:, 3, 0:w], 1.0, tc[:, k % 2, 0:w], ALU.add, ALU.mult
                                         ).then_inc(h2_done.sem, 1)
                wait(dve, h2_done, g, k)
                dve.tensor_copy(hi, flat(h2[:, k % 2], k)).then_inc(h2_hi.sem, 1)
                wait(dve, h2_hi, g, k)
                dve.tensor_tensor(lo, flat(h2[:, k % 2], k), f(hi), ALU.subtract).then_inc(h2_lo.sem, 1)

            def body(g, ahead):
                unit_lo(dve, g, OUT_STAGE)
                for k in range(K):
                    p, s, q, _, _ = LSTM[k]
                    w = columns(k)
                    gk = gates[:, k % 2]
                    if k < GB - 1:
                        unit_lo(dve, g, OUT_STAGE + k + 1)
                    if k >= GB:
                        output(g, k - 1)
                    if ahead and k in UNITS_AT:
                        unit_lo(dve, g, 4 * GB + UNITS_AT[k])
                    wait(dve, gate_tanh, g, gate_number(k, "g"))
                    target = ig[:, k % 2, 0:w] if s else state[:, k % 2, 0:w]
                    ins = dve.scalar_tensor_tensor(target, gk[:, 0, 0:w], 1.0, gk[:, 2, 0:w], ALU.add, ALU.mult)
                    ins.then_inc((ig_done if s else state_done).sem, 1)
                    if 0 < k < GB:
                        output(g, k - 1)
                    if s:
                        wait(dve, gate_tanh, g, gate_number(k, "f"))
                        dve.scalar_tensor_tensor(fc[:, k % 2, 0:w], gk[:, 1, 0:w], 1.0, state[:, k % 2, 0:w],
                                                 ALU.add, ALU.mult).then_inc(fc_done.sem, 1)
                        later = sum(1 for t in LSTM[:k] if t[1])
                        wait(dve, ig_done, g, later)
                        wait(dve, fc_done, g, later)
                        dve.scalar_tensor_tensor(state[:, k % 2, 0:w], fc[:, k % 2, 0:w], 0.5, ig[:, k % 2, 0:w],
                                                 ALU.mult, ALU.add).then_inc(state_done.sem, 1)
                output(g, K - 1)
                for b in range(GB + 1):
                    if b < GB:
                        wait(dve, turned, g, b)
                        wait(dve, norm.normed, g, b - 2)
                        dve.scalar_tensor_tensor(norm.sum[:, b % 2].rearrange("p c d -> p (c d)"), ps[:, b], 0.5,
                                                 x[:, bass.ds(g * GB + b, 1)].rearrange("p a c d -> p (a c d)"),
                                                 ALU.mult, ALU.add).then_inc(norm.summed.sem, 1)
                        norm.dve_stats(dve, g, b)
                        if ahead:
                            for u in TAIL[b]:
                                unit_lo(dve, g, 4 * GB + u)
                    if b >= 1:
                        norm.dve_apply(dve, g, b - 1,
                                       lambda c: x[:, bass.ds(g * GB + (b - 1), 1), c].rearrange("p a d -> p (a d)"))

            with dve.Fori(0, NG - 1) as g:
                body(g, True)
            body(NG - 1, False)

        @block.tensor
        def _(pe):
            credit(pe, gate_ready, turned)

            def body(g, ahead):
                unit(pe, g, OUT_STAGE)
                for k in range(K):
                    p, s, q, _, names = LSTM[k]
                    if k < GB - 1:
                        unit(pe, g, OUT_STAGE + k + 1)
                    if s == 0 and ahead and k in UNITS_AT:
                        unit(pe, g, 4 * GB + UNITS_AT[k])
                    if p == 1:
                        wait(pe, conv_lo, g, OUT_STAGE + q)
                    elif s == 0:
                        wait(pe, h2_lo, g, 2 * q + 1 if p == 2 else k - 2)
                    for gate in names:
                        n = gate_number(k, gate)
                        cols = slice(GATE[gate] * D, (GATE[gate] + 1) * D)
                        out = ps[:, n % RING, 0:columns(k)]
                        out = out if p == 1 else out.rearrange("p (b w) -> p b w", b=2)
                        if n < GB:
                            wait(pe, norm.summed, g, n - GB)
                        else:
                            wait(pe, gate_tanh, g, n - RING)
                        last = products(pe, out, [wih_s[:, h, p - 1, cols] for h in range(2)],
                                        [windows(h_s[:, h], k) for h in range(2)], True, s == 0)
                        if s == 0:
                            last.then_inc(gate_ready.sem, 1)
                    if s:
                        if ahead and k in UNITS_AT:
                            unit(pe, g, 4 * GB + UNITS_AT[k])
                        wait(pe, h2_lo, g, k - 2)
                        for gate in names:
                            n = gate_number(k, gate)
                            cols = slice(GATE[gate] * D, (GATE[gate] + 1) * D)
                            products(pe, ps[:, n % RING, 0:columns(k)],
                                     [whh_s[:, h, p - 1, cols] for h in range(2)],
                                     [cell_s[:, k % 2, h, 0:columns(k)] for h in range(2)], False, True
                                     ).then_inc(gate_ready.sem, 1)
                for b in range(GB):
                    if b % 2 == 0:
                        wait(pe, h2_lo, g, K - 2 + b // 2)
                    for c in range(C):
                        cols = slice(c * P, (c + 1) * P)
                        for h in range(2):
                            last = pe.matmul(ps[:, b, cols], h_s[:, h, b, cols], ident_r[:], start=h == 0, stop=h == 1)
                    last.then_inc(turned.sem, 1)
                    if ahead:
                        for u in TAIL[b]:
                            unit(pe, g, 4 * GB + u)

            with pe.Fori(0, NG - 1) as g:
                body(g, True)
            body(NG - 1, False)


def edge_attention(nc, d, x):
    with ExitStack() as ctx:
        sb = lambda n, s, t=F32: ctx.enter_context(nc.sbuf_tensor(n, s, t))
        BH = BATCH * HEADS
        gather = sb("e_gather", [P, C, 2, EDGES], F32R)
        scatter = sb("e_scatter", [P, EC, N], F32R)
        w_s = sb("e_w_split", [P, 2, 3, D], F32R)
        a_blocks = sb("e_a_blocks", [P, HEADS])
        log_adj = sb("e_log_adj", [P, EC])
        breaks = sb("e_breaks", [BH, EDGES + 1])
        inside = sb("e_inside", [BH, EDGES])
        ident = sb("e_ident", [P, P])
        v_all = sb("e_v_all", [P, BATCH, EC, D])
        e_all = sb("e_e_all", [P, EC, BH])

        with ExitStack() as tmp:
            tb = lambda n, s, t=F32: tmp.enter_context(nc.sbuf_tensor(n, s, t))
            sem = lambda n: tmp.enter_context(nc.semaphore(n))
            adj = tb("e_adj", [P, C, N])
            w = tb("e_w", [P, 3, D])
            a_col = tb("e_a_col", [P, 1])
            head_mask = tb("e_head_mask", [P, HEADS])
            iota = tb("e_iota", [P, N])
            node = tb("e_node", [P, C])
            ends_i = tb("e_ends_i", [P, EC, 2], I32)
            src_i = tb("e_src_i", [P, EDGES], I32)
            ends = tb("e_ends", [P, EC, 2])
            src_row = tb("e_src_row", [P, EDGES])
            key_row = tb("e_key_row", [P, EDGES])
            key_col = tb("e_key_col", [P, EC])
            less = tb("e_less", [P, EC, EDGES])
            rank = tb("e_rank", [P, EC])
            order = tb("e_order", [P, EC, EDGES])
            wide = tb("e_wide", [P, EC, 2, P])
            row = tb("e_row", [P, 2, EDGES])
            col = tb("e_col", [P, EC, 2])
            src_hot = tb("e_src_hot", [P, C, EDGES])
            dst_hot_t = tb("e_dst_hot_t", [P, EC, N])
            picked = tb("e_picked", [P, EC, N])
            a0 = tb("e_a0", [P, EC])
            new = tb("e_new", [BH, EDGES])
            ps = tmp.enter_context(nc.psum_tensor("e_ps", [P, 4, N], F32))
            adj_in, small_in, pe_done, step, ln_done = (sem("e_adj_in"), sem("e_small_in"), sem("e_pe_done"),
                                                        sem("e_step"), sem("e_ln_done"))
            block = tmp.enter_context(nc.Block())

            @block.sync
            def _(sp):
                sp.dma_start(ends_i[:], d["edge_ends"]).then_inc(small_in, 16)
                sp.dma_start(src_i[:], d["src"].rearrange("(a e) -> a e", a=1).to_broadcast([P, EDGES])).then_inc(small_in, 16)
                sp.dma_start(iota[:], d["iota"]).then_inc(small_in, 16)
                sp.dma_start(node[:], d["node"]).then_inc(small_in, 16)
                sp.dma_start(head_mask[:], d["head_mask"]).then_inc(small_in, 16)
                sp.dma_start(a_col[:], d["a"]).then_inc(small_in, 16)
                sp.dma_start(ident[:], d["ident"]).then_inc(small_in, 16)
                for i, name in enumerate(("W_linT", "W_valT", "W_outT")):
                    sp.dma_start(w[:, i], d[name]).then_inc(small_in, 16)
                sp.dma_start(adj[:], d["adj"].rearrange("(c p) m -> p c m", p=P)).then_inc(adj_in, 16)

            @block.scalar
            def _(act):
                act.wait_ge(step, 10)
                act.activation(log_adj[:], a0[:], ACT.Ln).then_inc(ln_done, 1)

            @block.vector
            def _(dve):
                def then(ins, n):
                    ins.then_inc(step, 1)
                    dve.wait_ge(step, n)

                dve.wait_ge(small_in, 10 * 16)
                dve.tensor_copy(w_s[:, 0], w[:])
                dve.tensor_scalar(a_blocks[:], head_mask[:], a_col[:], None, ALU.mult)
                dve.tensor_copy(ends[:], ends_i[:])
                then(dve.tensor_copy(src_row[:], src_i[:]), 1)
                dve.tensor_tensor(w_s[:, 1], w[:], f(w_s[:, 0]), ALU.subtract)
                dve.scalar_tensor_tensor(key_row[:], src_row[:], float(EDGES), iota[:, 0:EDGES], ALU.mult, ALU.add)
                for i in range(2):
                    for c in range(EC):
                        dve.tensor_scalar(wide[:, c, i], ident[:], 0.0, ends[:, c, i:i + 1], ALU.mult, ALU.add)
                then(dve.scalar_tensor_tensor(key_col[:], ends[:, :, 0], float(EDGES), node[:, 0:EC],
                                              ALU.mult, ALU.add), 2)
                for c in range(EC):
                    last = dve.tensor_scalar(less[:, c], key_row[:], key_col[:, c:c + 1], None, ALU.is_lt)
                then(last, 3)
                then(dve.tensor_reduce(rank[:], less[:], AX.X, ALU.add), 4)
                for c in range(EC):
                    last = dve.tensor_scalar(order[:, c], iota[:, 0:EDGES], rank[:, c:c + 1], None, ALU.is_equal)
                then(last, 5)
                dve.wait_ge(pe_done, 2)
                dve.tensor_copy(row[:], ps[:, 0].rearrange("p (i e) -> p i e", i=2))
                then(dve.tensor_copy(col[:], ps[:, 1, 0:2 * EC].rearrange("p (c i) -> p c i", c=EC)), 6)
                for c in range(C):
                    dve.tensor_scalar(src_hot[:, c], row[:, 0], node[:, c:c + 1], None, ALU.is_equal)
                    dve.tensor_scalar(gather[:, c, 1], row[:, 1], node[:, c:c + 1], None, ALU.is_equal)
                for c in range(EC):
                    dve.tensor_scalar(scatter[:, c], iota[:], col[:, c, 0:1], None, ALU.is_equal)
                    dve.tensor_scalar(dst_hot_t[:, c], iota[:], col[:, c, 1:2], None, ALU.is_equal)
                dve.memset(breaks[:], BIG)
                then(dve.tensor_tensor(new[:, 1:EDGES], row[0:BH, 0, 1:EDGES], row[0:BH, 0, 0:EDGES - 1],
                                       ALU.not_equal), 7)
                dve.tensor_tensor(gather[:, :, 0], src_hot[:], f(gather[:, :, 1]), ALU.add)
                dve.tensor_scalar(breaks[:, 1:EDGES], new[:, 1:EDGES], BIG, None, ALU.mult)
                dve.memset(inside[:, 0:1], 0.0)
                dve.tensor_scalar(inside[:, 1:EDGES], new[:, 1:EDGES], -1.0, 1.0, ALU.mult, ALU.add)
                dve.wait_ge(pe_done, 3)
                then(dve.tensor_tensor(picked[:], ps[:, 2:4], dst_hot_t[:], ALU.mult), 8)
                then(dve.tensor_reduce(a0[:], picked[:], AX.X, ALU.add), 9)
                dve.tensor_scalar(a0[:], a0[:], 1e-8, None, ALU.add).then_inc(step, 1)

            @block.tensor
            def _(pe):
                pe.wait_ge(step, 5)
                for i in range(2):
                    for c in range(EC):
                        last = pe.matmul(ps[:, 0, i * EDGES:(i + 1) * EDGES], wide[:, c, i], order[:, c],
                                         start=c == 0, stop=c == EC - 1)
                last.then_inc(pe_done, 1)
                for r in range(EC):
                    for c in range(EC):
                        last = pe.matmul(ps[:, 1, 2 * r:2 * r + 2], order[:, c, r * P:(r + 1) * P], ends[:, c],
                                         start=c == 0, stop=c == EC - 1)
                last.then_inc(pe_done, 1)
                pe.wait_ge(adj_in, 16)
                pe.wait_ge(step, 7)
                for r in range(EC):
                    for c in range(C):
                        last = pe.matmul(ps[:, 2 + r], src_hot[:, c, r * P:(r + 1) * P], adj[:, c],
                                         start=c == 0, stop=c == C - 1)
                last.then_inc(pe_done, 1)

        with ExitStack() as tmp:
            tb = lambda n, s, t=F32: tmp.enter_context(nc.sbuf_tensor(n, s, t))
            aside = tmp.enter_context(nc.semaphore("e_aside"))
            count = lambda n: Count(tmp.enter_context(nc.semaphore(n)), GB, aside)
            x_s = tb("e_x_split", [P, 2, GB, C, D], F32R)
            z_s = tb("e_z_split", [P, 2, 2, 2 * EDGES], F32R)
            q_sum = tb("e_q_sum", [P, 2, EDGES])
            lrelu = tb("e_lrelu", [P, 2, EDGES])
            ps = tmp.enter_context(nc.psum_tensor("e_banks", [P, 8, N], F32))
            x_hi, x_lo, z_ready, z_hi, z_lo, q_ready, q_copied, lrelu_done, v_ready, v_copied, e_ready, e_done = (
                count("e_" + n) for n in ("x_hi", "x_lo", "z_ready", "z_hi", "z_lo", "q_ready", "q_copied",
                                          "lrelu_done", "v_ready", "v_copied", "e_ready", "e_done"))
            block = tmp.enter_context(nc.Block())
            Z, Q, V, E = 0, 2, 4, 6

            @block.gpsimd
            def _(pool):
                credit(pool, x_hi, x_lo)
                with pool.Fori(0, NG) as g:
                    for b in range(GB):
                        src = x[:, bass.ds(g * GB + b, 1)].rearrange("p a c d -> p (a c) d")
                        wait_apart(pool, z_hi, g, b - GB)
                        pool.tensor_copy(x_s[:, 0, b], src).then_inc(x_hi.sem, 1)
                        wait_apart(pool, x_hi, g, b)
                        pool.tensor_tensor(x_s[:, 1, b], src, f(x_s[:, 0, b]), ALU.subtract).then_inc(x_lo.sem, 1)

            @block.scalar
            def _(act):
                credit(act, z_hi, q_copied, v_copied)
                with act.Fori(0, NG) as g:
                    for t in range(GB + 1):
                        if t < GB:
                            b = t
                            wait(act, z_ready, g, b)
                            wait(act, v_ready, g, b - 2)
                            act.copy(z_s[:, b % 2, 0], ps[:, Z + b % 2]).then_inc(z_hi.sem, 1)
                        if t >= 1:
                            b = t - 1
                            wait(act, q_ready, g, b)
                            wait(act, lrelu_done, g, b - 2)
                            act.copy(q_sum[:, b % 2], ps[:, Q + b % 2, 0:EDGES]).then_inc(q_copied.sem, 1)
                            wait(act, v_ready, g, b)
                            act.copy(v_all[:, bass.ds(g * GB + b, 1)].rearrange("p a c d -> p (a c d)"),
                                     ps[:, V + b % 2, 0:EC * D]).then_inc(v_copied.sem, 1)

            @block.vector
            def _(dve):
                credit(dve, z_lo, lrelu_done, e_done)
                with dve.Fori(0, NG) as g:
                    for t in range(GB + 2):
                        if t < GB:
                            b = t
                            wait(dve, z_hi, g, b)
                            dve.tensor_tensor(z_s[:, b % 2, 1], ps[:, Z + b % 2], f(z_s[:, b % 2, 0]),
                                              ALU.subtract).then_inc(z_lo.sem, 1)
                        if 1 <= t < GB + 1:
                            b = t - 1
                            wait(dve, q_copied, g, b)
                            wait(dve, e_ready, g, b - 2)
                            dve.scalar_tensor_tensor(lrelu[:, b % 2], q_sum[:, b % 2], 0.2, ps[:, Q + b % 2, 0:EDGES],
                                                     ALU.mult, ALU.max).then_inc(lrelu_done.sem, 1)
                        if t >= 2:
                            b = t - 2
                            wait(dve, e_ready, g, b)
                            for c in range(EC):
                                last = dve.tensor_scalar(e_all[:, c, bass.ds((g * GB + b) * HEADS, HEADS)],
                                                         ps[:, E + b % 2, c * HEADS:(c + 1) * HEADS],
                                                         log_adj[:, c:c + 1], None, ALU.add)
                            last.then_inc(e_done.sem, 1)

            @block.tensor
            def _(pe):
                credit(pe, z_ready, q_ready, v_ready, e_ready)
                with pe.Fori(0, NG) as g:
                    for t in range(GB + 2):
                        if t < GB:
                            b = t
                            wait(pe, x_lo, g, b)
                            wait(pe, z_lo, g, b - 2)
                            for c in range(C):
                                for h in range(2):
                                    last = pe.matmul(ps[:, Z + b % 2], x_s[:, h, b, c],
                                                     gather[:, c].rearrange("p i e -> p (i e)"),
                                                     start=c + h == 0, stop=(c, h) == (C - 1, 1))
                            last.then_inc(z_ready.sem, 1)
                        if 1 <= t < GB + 1:
                            b = t - 1
                            wait(pe, z_lo, g, b)
                            wait(pe, lrelu_done, g, b - 2)
                            products(pe, ps[:, Q + b % 2, 0:EDGES], [w_s[:, h, 0] for h in range(2)],
                                     [z_s[:, b % 2, h, 0:EDGES] for h in range(2)]).then_inc(q_ready.sem, 1)
                            wait(pe, v_copied, g, b - 2)
                            for c in range(EC):
                                last = products(pe, ps[:, V + b % 2, c * D:(c + 1) * D],
                                                [z_s[:, b % 2, h, EDGES + c * P:EDGES + (c + 1) * P] for h in range(2)],
                                                [w_s[:, h, 1] for h in range(2)])
                            last.then_inc(v_ready.sem, 1)
                        if t >= 2:
                            b = t - 2
                            wait(pe, lrelu_done, g, b)
                            wait(pe, e_done, g, b - 2)
                            for c in range(EC):
                                last = pe.matmul(ps[:, E + b % 2, c * HEADS:(c + 1) * HEADS],
                                                 lrelu[:, b % 2, c * P:(c + 1) * P], a_blocks[:], start=True, stop=True)
                            last.then_inc(e_ready.sem, 1)

        with ExitStack() as tmp:
            tb = lambda n, s: tmp.enter_context(nc.sbuf_tensor(n, s, F32))
            sem = lambda n: tmp.enter_context(nc.semaphore(n))
            e_t, run, top, shifted, ex, total, share = (tb("e_" + n, [BH, EDGES]) for n in
                                                        ("t", "run", "top", "shifted", "ex", "total", "share"))
            ps = tmp.enter_context(nc.psum_tensor("e_turn", [P, 2, N], F32))
            turned, step, ex_done, back = sem("e_turned"), sem("e_sstep"), sem("e_ex_done"), sem("e_back")
            block = tmp.enter_context(nc.Block())
            flip = lambda t, a, b: t[:, a:b][:, ::-1]

            @block.tensor
            def _(pe):
                for c in range(EC):
                    last = pe.transpose(ps[0:BH, 0, c * P:(c + 1) * P], e_all[:, c], ident[:])
                last.then_inc(turned, 1)
                pe.wait_ge(step, 8)
                for c in range(EC):
                    last = pe.transpose(ps[:, 1, c * BH:(c + 1) * BH], share[:, c * P:(c + 1) * P], ident[0:BH, 0:BH])
                last.then_inc(back, 1)

            @block.scalar
            def _(act):
                act.wait_ge(step, 4)
                act.activation(ex[:], shifted[:], ACT.Exp).then_inc(ex_done, 1)

            @block.vector
            def _(dve):
                def then(ins, n):
                    ins.then_inc(step, 1)
                    dve.wait_ge(step, n)

                dve.wait_ge(turned, 1)
                then(dve.tensor_copy(e_t[:], ps[0:BH, 0, 0:EDGES]), 1)
                then(dve.tensor_tensor_scan(run[:], breaks[:, 0:EDGES], e_t[:], BIG, ALU.add, ALU.max), 2)
                then(dve.tensor_tensor_scan(flip(top, 0, EDGES), flip(breaks, 1, EDGES + 1), flip(run, 0, EDGES), BIG,
                                            ALU.add, ALU.max), 3)
                dve.tensor_tensor(shifted[:], e_t[:], top[:], ALU.subtract).then_inc(step, 1)
                dve.wait_ge(ex_done, 1)
                then(dve.tensor_tensor_scan(run[:], inside[:], ex[:], 0.0, ALU.mult, ALU.add), 5)
                then(dve.tensor_tensor_scan(flip(total, 0, EDGES), flip(breaks, 1, EDGES + 1), flip(run, 0, EDGES), BIG,
                                            ALU.add, ALU.max), 6)
                then(dve.reciprocal(total[:], total[:]), 7)
                dve.tensor_tensor(share[:], ex[:], total[:], ALU.mult).then_inc(step, 1)
                dve.wait_ge(back, 1)
                dve.tensor_copy(e_all[:], ps[:, 1, 0:EC * BH].rearrange("p (c n) -> p c n", c=EC))

        with ExitStack() as tmp:
            tb = lambda n, s, t=F32: tmp.enter_context(nc.sbuf_tensor(n, s, t))
            aside = tmp.enter_context(nc.semaphore("y_aside"))
            count = lambda n: Count(tmp.enter_context(nc.semaphore(n)), GB, aside)
            av = tb("y_av", [P, 2, EC, D])
            av_s = tb("y_av_split", [P, 2, 2, EC, D], F32R)
            y_s = tb("y_y_split", [P, 2, 2, N], F32R)
            norm = Norm(nc, tmp, "ln2", GB, aside)
            ps = tmp.enter_context(nc.psum_tensor("y_banks", [P, 4, N], F32))
            av_done, av_hi, av_lo, y_ready, y_hi, y_lo, o_ready = (
                count("y_" + n) for n in ("av_done", "av_hi", "av_lo", "y_ready", "y_hi", "y_lo", "o_ready"))
            block = tmp.enter_context(nc.Block())

            @block.gpsimd
            def _(pool):
                norm.start_pool(pool)
                with pool.Fori(0, NG) as g:
                    for b in range(GB):
                        norm.pool_root(pool, g, b)

            @block.scalar
            def _(act):
                credit(act, av_hi, y_hi)
                with act.Fori(0, NG) as g:
                    for t in range(GB + 1):
                        if t < GB:
                            b = t
                            wait(act, av_done, g, b)
                            wait(act, y_ready, g, b - 2)
                            act.copy(av_s[:, b % 2, 0], av[:, b % 2]).then_inc(av_hi.sem, 1)
                        if t >= 1:
                            b = t - 1
                            wait(act, y_ready, g, b)
                            wait(act, o_ready, g, b - 2)
                            act.copy(y_s[:, b % 2, 0], ps[:, b % 2]).then_inc(y_hi.sem, 1)

            @block.vector
            def _(dve):
                credit(dve, av_done, av_lo, y_lo)
                norm.start_dve(dve)
                with dve.Fori(0, NG) as g:
                    for t in range(GB + 2):
                        if t < GB:
                            b = t
                            dve.tensor_tensor(
                                av[:, b % 2].rearrange("p c (h d) -> p c h d", h=HEADS),
                                v_all[:, bass.ds(g * GB + b, 1)].rearrange("p a c (h d) -> p (a c) h d", h=HEADS),
                                e_all[:, :, bass.ds((g * GB + b) * HEADS, HEADS)].unsqueeze(3)
                                .to_broadcast([P, EC, HEADS, DH]), ALU.mult).then_inc(av_done.sem, 1)
                            wait(dve, av_hi, g, b)
                            dve.tensor_tensor(av_s[:, b % 2, 1], av[:, b % 2], f(av_s[:, b % 2, 0]),
                                              ALU.subtract).then_inc(av_lo.sem, 1)
                        if 1 <= t < GB + 1:
                            b = t - 1
                            wait(dve, y_hi, g, b)
                            dve.tensor_tensor(y_s[:, b % 2, 1], ps[:, b % 2], f(y_s[:, b % 2, 0]),
                                              ALU.subtract).then_inc(y_lo.sem, 1)
                        if t >= 2:
                            b = t - 2
                            wait(dve, o_ready, g, b)
                            wait(dve, norm.normed, g, b - 2)
                            dve.tensor_tensor(norm.sum[:, b % 2].rearrange("p c d -> p (c d)"), ps[:, 2 + b % 2],
                                              x[:, bass.ds(g * GB + b, 1)].rearrange("p a c d -> p (a c d)"),
                                              ALU.add).then_inc(norm.summed.sem, 1)
                            norm.dve_stats(dve, g, b)
                            norm.dve_apply(dve, g, b, lambda c: x[:, bass.ds(g * GB + b, 1), c].rearrange("p a d -> p (a d)"))

            @block.tensor
            def _(pe):
                credit(pe, y_ready, o_ready)
                with pe.Fori(0, NG) as g:
                    for t in range(GB + 1):
                        if t < GB:
                            b = t
                            wait(pe, av_lo, g, b)
                            wait(pe, y_lo, g, b - 2)
                            for c in range(EC):
                                for h in range(2):
                                    last = pe.matmul(ps[:, b % 2], av_s[:, b % 2, h, c], scatter[:, c],
                                                     start=c + h == 0, stop=(c, h) == (EC - 1, 1))
                            last.then_inc(y_ready.sem, 1)
                        if t >= 1:
                            b = t - 1
                            wait(pe, y_lo, g, b)
                            wait(pe, norm.summed, g, b - 2)
                            for c in range(C):
                                cols = slice(c * P, (c + 1) * P)
                                last = products(pe, ps[:, 2 + b % 2, cols], [y_s[:, b % 2, h, cols] for h in range(2)],
                                                [w_s[:, h, 2] for h in range(2)])
                            last.then_inc(o_ready.sem, 1)


BODY = 2
TILES = HEADS * C
BT = BODY * TILES
BHD = BODY * HEADS
SPLIT = (True, False, True, False)


def is_split(t):
    return SPLIT[t // C % HEADS]


def evac_engine(t):
    return "dve" if is_split(t) or t % 2 else "act"


def number(t, test):
    per = sum(map(test, range(BT)))
    return (t // BT) * per + sum(map(test, range(t % BT)))


def evac_number(t, who):
    return number(t, lambda u: evac_engine(u) == who)


def self_attention(nc, d, x, out):
    with ExitStack() as ctx:
        sb = lambda n, s, t=F32: ctx.enter_context(nc.sbuf_tensor(n, s, t))
        sem = lambda n: ctx.enter_context(nc.semaphore(n))
        mask = sb("t_mask", [P, C, N])
        w_s = sb("t_w_split", [P, 2, 3 * D], F32R)
        ident = sb("t_ident", [P, P])
        eps = sb("t_eps", [P, C])
        with ExitStack() as tmp:
            w = tmp.enter_context(nc.sbuf_tensor("t_w", [P, 3 * D], F32))
            loaded = tmp.enter_context(nc.semaphore("t_loaded"))
            step = tmp.enter_context(nc.semaphore("t_step"))
            block = tmp.enter_context(nc.Block())

            @block.sync
            def _(sp):
                sp.dma_start(mask[:], d["adj"].rearrange("(c p) m -> p c m", p=P)).then_inc(loaded, 16)
                sp.dma_start(w[:], d["W_qkv"]).then_inc(loaded, 16)
                sp.dma_start(ident[:], d["ident"]).then_inc(loaded, 16)

            @block.vector
            def _(dve):
                dve.wait_ge(loaded, 48)
                dve.tensor_scalar(w[:, 0:D], w[:, 0:D], -float(DH) ** -0.5, None, ALU.mult)
                dve.tensor_scalar(mask[:], mask[:], 0.0, -BIG, ALU.is_equal, ALU.mult).then_inc(step, 1)
                dve.wait_ge(step, 1)
                dve.tensor_copy(w_s[:, 0], w[:])
                dve.tensor_reduce(eps[:], mask[:], AX.X, ALU.min).then_inc(step, 1)
                dve.wait_ge(step, 2)
                dve.tensor_tensor(w_s[:, 1], w[:], f(w_s[:, 0]), ALU.subtract)
                dve.tensor_scalar(eps[:], eps[:], -BIG, 0.0, ALU.mult, ALU.mult).then_inc(step, 1)
                dve.wait_ge(step, 3)
                dve.tensor_scalar(eps[:], eps[:], EPS, None, ALU.add)

        aside = sem("t_aside")
        count = lambda n, per: Count(sem("t_" + n), per, aside)
        x_s = sb("t_x_split", [P, BODY, 2, C, D], F32R)
        xt_s = sb("t_xt_split", [P, 2, N], F32R)
        qk = sb("t_qk", [P, 4, N], F32R)
        stack = sb("t_stack", [96, BODY, HEADS, 2, N], F32R)
        v_s = sb("t_v_split", [P, BODY, C, HEADS, 2 * DH], F32R)
        v_w = sb("t_v_whole", [P, BODY, C, HEADS, DH])
        masked = sb("t_masked", [P, 4, N])
        low = sb("t_low", [P, 4, 1])
        prob = sb("t_prob", [P, 4, N])
        total = sb("t_total", [P, BODY, HEADS, C])
        recip = sb("t_recip", [P, BODY, HEADS, C])
        pt_s = sb("t_pt_split", [P, 2, C, N], F32R)
        pt_w = sb("t_pt_whole", [P, C, N])
        o_t = sb("t_o_t", [2 * DH, 2, N])
        o_hi = sb("t_o_hi", [P, BODY, C, D])
        o_lo = sb("t_o_lo", [P, BODY, C, D])
        norm = Norm(nc, ctx, "ln3", BODY, aside, eps)
        ps = ctx.enter_context(nc.psum_tensor("t_banks", [P, 8, N], F32))
        S, T, O, M = 0, 2, 4, 6

        x_hi, x_lo, xt_ready, xt_hi, xt_lo = (count(n, BODY) for n in ("x_hi", "x_lo", "xt_ready", "xt_hi", "xt_lo"))
        qkv_ready, qkv_hi, qkv_lo = (count(n, 3 * BODY) for n in ("qkv_ready", "qkv_hi", "qkv_lo"))
        stacked = [count(f"stacked{j}", 16 * 3 * HEADS) for j in range(BODY)]
        s_ready, masked_done, exp_done, t_ready = (count(n, BT) for n in (
            "s_ready", "masked_done", "exp_done", "t_ready"))
        pt_hi = count("pt_hi", number(BT, is_split))
        evac = {w: count("pt_" + w, sum(evac_engine(t) == w for t in range(BT))) for w in ("dve", "act")}
        o_ready, o_copied, o_turned, rec_done, o_done = (count(n, BHD) for n in (
            "o_ready", "o_copied", "o_turned", "rec_done", "o_done"))
        parts_added = count("parts_added", BODY)
        stored = sem("t_stored")
        BODIES = BATCH // BODY
        TAIL = 16

        def run(eng, prologue, slot):
            prologue()

            def body(g, first, last):
                end = BT if last else 10 ** 6
                inside = lambda n, unit=1: (n >= 0 or not first) and n * unit < end
                for t in range(BT + (TAIL if last else 0)):
                    slot(g, t, inside)
            body(0, True, False)
            with eng.Fori(1, BODIES - 1) as g:
                body(g, False, False)
            body(BODIES - 1, False, True)

        def wait_evac(eng, g, t):
            who = evac_engine(t)
            wait(eng, evac[who], g, evac_number(t, who))

        def batch_of(g, n):
            return x[:, bass.ds(g * BODY + n, 1)] if not isinstance(g, int) else x[:, g * BODY + n:g * BODY + n + 1]

        def stack_count(n):
            return 16 * 3 * HEADS * (n // BODY + 1) - 1

        block = ctx.enter_context(nc.Block())

        @block.sync
        def _(sp):
            def restack(g, n):
                j = n % BODY
                wait_apart(sp, qkv_lo, g, 3 * n + 1)
                wait_apart(sp, s_ready, g, TILES * (n - BODY + 1) - 1)
                for h in range(HEADS):
                    rows = slice(h * DH, (h + 1) * DH)
                    for r, pick in enumerate((slice(0, 3, 2), slice(0, 4, 3), slice(1, 3))):
                        sp.dma_start(f(stack[r * DH:(r + 1) * DH, j, h]), f(qk[rows, pick])).then_inc(stacked[j].sem, 16)

            def start():
                credit(sp, *stacked)
                restack(0, 0)

            def slot(g, t, inside):
                if t % TILES == 6 and inside(t // TILES + 1, TILES):
                    restack(g, t // TILES + 1)
                if t % TILES == 15 and inside((t - 31) // TILES, TILES):
                    n = (t - 31) // TILES
                    wait_apart(sp, norm.normed, g, n)
                    dst = out[bass.ds(g * BODY + n, 1)] if not isinstance(g, int) else out[g * BODY + n:g * BODY + n + 1]
                    sp.dma_start(dst.rearrange("a (c p) d -> p (a c) d", p=P),
                                 batch_of(g, n).rearrange("p a c d -> p (a c) d")).then_inc(stored, 16)
            run(sp, start, slot)
            sp.wait_ge(stored, 16 * BATCH)

        @block.gpsimd
        def _(pool):
            def split(g, n):
                j, src = n % BODY, batch_of(g, n).rearrange("p a c d -> p (a c) d")
                wait_apart(pool, xt_hi, g, n - BODY)
                pool.tensor_copy(x_s[:, j, 0], src).then_inc(x_hi.sem, 1)
                wait_apart(pool, x_hi, g, n)
                pool.tensor_tensor(x_s[:, j, 1], src, f(x_s[:, j, 0]), ALU.subtract).then_inc(x_lo.sem, 1)

            def start():
                credit(pool, x_hi, x_lo, parts_added, norm.summed)
                norm.start_pool(pool)
                split(0, 0)
                split(0, 1)

            def slot(g, t, inside):
                if t % TILES == 8 and inside(t // TILES + 2, TILES):
                    split(g, t // TILES + 2)
                if t % TILES == 8 and inside((t - 24) // TILES, TILES):
                    n = (t - 24) // TILES
                    j = n % BODY
                    wait_apart(pool, o_done, g, HEADS * (n + 1) - 1)
                    for h in range(HEADS):
                        if SPLIT[h]:
                            cols = slice(h * DH, (h + 1) * DH)
                            last = pool.tensor_tensor(o_hi[:, j, :, cols], o_hi[:, j, :, cols], o_lo[:, j, :, cols], ALU.add)
                    last.then_inc(parts_added.sem, 1)
                    wait_apart(pool, norm.normed, g, n - 2)
                    wait_apart(pool, parts_added, g, n)
                    pool.tensor_tensor(norm.sum[:, j], batch_of(g, n).rearrange("p a c d -> p (a c) d"), o_hi[:, j],
                                       ALU.add).then_inc(norm.summed.sem, 1)
                    norm.pool_root(pool, g, n)
            run(pool, start, slot)

        @block.scalar
        def _(act):
            def exponent(g, t):
                wait(act, masked_done, g, t)
                wait(act, t_ready, g, t - 4)
                j, h, c = t // TILES % BODY, t // C % HEADS, t % C
                if c == 0:
                    wait(act, rec_done, g, t // C - BHD)
                act.activation(prob[:, t % 4], masked[:, t % 4], ACT.Exp, bias=low[:, t % 4], scale=-1.0,
                               accum_out=total[:, j, h, c:c + 1]).then_inc(exp_done.sem, 1)

            def turned_x(g, n):
                wait(act, xt_ready, g, n)
                wait(act, qkv_ready, g, 3 * n - 1)
                act.copy(xt_s[:, 0], ps[:, M]).then_inc(xt_hi.sem, 1)

            def q_k_high(g, n):
                wait(act, stacked[(n - 1) % BODY], g, stack_count(n - 1))
                for i in range(2):
                    wait(act, qkv_ready, g, 3 * n + i)
                    act.copy(qk[:, 2 * i], ps[:, M + i]).then_inc(qkv_hi.sem, 1)

            def v_high(g, n):
                j = n % BODY
                wait(act, qkv_ready, g, 3 * n + 2)
                wait(act, o_ready, g, HEADS * (n - 1) - 1)
                bank = ps[:, M].rearrange("p (c h d) -> p c h d", c=C, h=HEADS)
                act.copy(v_w[:, j], bank)
                act.copy(v_s[:, j, :, :, 0:DH], bank).then_inc(qkv_hi.sem, 1)

            def start():
                credit(act, exp_done, xt_hi, qkv_hi, pt_hi, evac["act"], o_copied)
                turned_x(0, 0)
                q_k_high(0, 0)
                v_high(0, 0)
                exponent(0, 0)

            def slot(g, t, inside):
                if inside(t + 1):
                    exponent(g, t + 1)
                if inside(t):
                    c = t % C
                    cols = slice(c * P, (c + 1) * P)
                    bank = ps[:, T + t % 2].rearrange("p (c i) -> p c i", c=C)
                    if is_split(t):
                        wait(act, t_ready, g, t)
                        if c == 0:
                            wait(act, o_ready, g, t // C - 2)
                        act.copy(pt_s[:, 0, :, cols], bank).then_inc(pt_hi.sem, 1)
                    elif evac_engine(t) == "act":
                        wait(act, t_ready, g, t)
                        wait(act, o_ready, g, t // C - 2)
                        act.copy(pt_w[:, :, cols], bank).then_inc(evac["act"].sem, 1)
                if t % C == 1 and inside((t - 9) // C, C):
                    n = (t - 9) // C
                    wait(act, o_ready, g, n)
                    wait(act, o_turned, g, n - 2)
                    rows = 2 * DH if SPLIT[n % HEADS] else DH
                    act.copy(o_t[0:rows, n % 2], ps[0:rows, O + n % 2]).then_inc(o_copied.sem, 1)
                if inside(t // TILES + 1, TILES):
                    for at, what in ((2, turned_x), (4, q_k_high), (6, v_high)):
                        if t % TILES == at:
                            what(g, t // TILES + 1)
            run(act, start, slot)

        @block.vector
        def _(dve):
            def mask_scores(g, t):
                wait_apart(dve, s_ready, g, t)
                wait_apart(dve, exp_done, g, t - 4)
                dve.tensor_tensor_reduce(masked[:, t % 4], ps[:, S + t % 2], mask[:, t % C], 1.0, -BIG, ALU.add, ALU.min,
                                         low[:, t % 4]).then_inc(masked_done.sem, 1)

            def turned_x(g, n):
                wait(dve, xt_ready, g, n)
                wait(dve, qkv_ready, g, 3 * n - 1)
                dve.tensor_copy(xt_s[:, 1], ps[:, M + 1]).then_inc(xt_lo.sem, 1)

            def q_k_low(g, n):
                for i in range(2):
                    wait(dve, qkv_hi, g, 3 * n + i)
                    dve.tensor_tensor(qk[:, 2 * i + 1], ps[:, M + i], f(qk[:, 2 * i]), ALU.subtract
                                      ).then_inc(qkv_lo.sem, 1)

            def v_low(g, n):
                j = n % BODY
                wait(dve, qkv_hi, g, 3 * n + 2)
                dve.tensor_tensor(v_s[:, j, :, :, DH:], ps[:, M].rearrange("p (c h d) -> p c h d", c=C, h=HEADS),
                                  f(v_s[:, j, :, :, 0:DH]), ALU.subtract).then_inc(qkv_lo.sem, 1)

            def start():
                credit(dve, masked_done, xt_lo, qkv_lo, evac["dve"], rec_done, o_done)
                credit(dve, norm.counted, norm.averaged, norm.normed)
                turned_x(0, 0)
                q_k_low(0, 0)
                v_low(0, 0)
                mask_scores(0, 0)
                mask_scores(0, 1)

            def slot(g, t, inside):
                if inside(t + 2):
                    mask_scores(g, t + 2)
                if inside(t) and evac_engine(t) == "dve":
                    c = t % C
                    cols = slice(c * P, (c + 1) * P)
                    bank = ps[:, T + t % 2].rearrange("p (c i) -> p c i", c=C)
                    if is_split(t):
                        wait(dve, pt_hi, g, number(t, is_split))
                        dve.tensor_tensor(pt_s[:, 1, :, cols], bank, f(pt_s[:, 0, :, cols]), ALU.subtract
                                          ).then_inc(evac["dve"].sem, 1)
                    else:
                        wait(dve, t_ready, g, t)
                        wait(dve, o_ready, g, t // C - 2)
                        dve.tensor_copy(pt_w[:, :, cols], bank).then_inc(evac["dve"].sem, 1)
                if t % C == 3 and inside((t - 11) // C, C):
                    n = (t - 11) // C
                    j, h = n // HEADS % BODY, n % HEADS
                    if h == 0:
                        wait(dve, parts_added, g, n // HEADS - 2)
                        wait(dve, norm.summed, g, n // HEADS - 2)
                    wait(dve, exp_done, g, C * n + C - 1)
                    dve.reciprocal(recip[:, j, h], total[:, j, h]).then_inc(rec_done.sem, 1)
                    wait(dve, rec_done, g, n)
                    wait(dve, o_turned, g, n)
                    bank = ps[:, O + n % 2, 0:C * 2 * DH].rearrange("p (c d) -> p c d", c=C)
                    scale = recip[:, j, h].unsqueeze(2).to_broadcast([P, C, DH])
                    cols = slice(h * DH, (h + 1) * DH)
                    ins = dve.tensor_tensor(o_hi[:, j, :, cols], bank[:, :, 0:DH], scale, ALU.mult)
                    if SPLIT[h]:
                        ins = dve.tensor_tensor(o_lo[:, j, :, cols], bank[:, :, DH:], scale, ALU.mult)
                    ins.then_inc(o_done.sem, 1)
                if t % TILES == 10 and inside((t - 26) // TILES, TILES):
                    norm.dve_stats(dve, g, (t - 26) // TILES)
                if t % TILES == 14 and inside((t - 30) // TILES, TILES):
                    n = (t - 30) // TILES
                    norm.dve_apply(dve, g, n, lambda c: batch_of(g, n)[:, :, c].rearrange("p a d -> p (a d)"))
                if inside(t // TILES + 1, TILES):
                    for at, what in ((2, turned_x), (4, q_k_low), (6, v_low)):
                        if t % TILES == at:
                            what(g, t // TILES + 1)
            run(dve, start, slot)

        @block.tensor
        def _(pe):
            def scores(g, t):
                j, h, c = t // TILES % BODY, t // C % HEADS, t % C
                if t % TILES == 0:
                    wait(pe, stacked[j], g, stack_count(t // TILES))
                wait(pe, masked_done, g, t - 2)
                pe.matmul(ps[:, S + t % 2], stack[:, j, h, 0, c * P:(c + 1) * P], stack[:, j, h, 1],
                          start=True, stop=True).then_inc(s_ready.sem, 1)

            def turn_x(g, n):
                j = n % BODY
                wait(pe, x_lo, g, n)
                wait(pe, qkv_lo, g, 3 * n - 1)
                for part in range(2):
                    for c in range(C):
                        last = pe.transpose(ps[:, M + part, c * P:(c + 1) * P], f(x_s[:, j, part, c]), ident[:])
                last.then_inc(xt_ready.sem, 1)

            def q_k(g, n):
                wait(pe, xt_hi, g, n)
                wait(pe, xt_lo, g, n)
                for i in range(2):
                    products(pe, ps[:, M + i], [w_s[:, h, i * D:(i + 1) * D] for h in range(2)],
                             [xt_s[:, h] for h in range(2)]).then_inc(qkv_ready.sem, 1)

            def v(g, n):
                wait(pe, qkv_lo, g, 3 * n)
                for c in range(C):
                    cols = slice(c * P, (c + 1) * P)
                    last = products(pe, ps[:, M, cols], [xt_s[:, h, cols] for h in range(2)],
                                    [w_s[:, h, 2 * D:] for h in range(2)])
                last.then_inc(qkv_ready.sem, 1)

            def start():
                credit(pe, s_ready, xt_ready, qkv_ready, t_ready, o_ready, o_turned)
                turn_x(0, 0)
                q_k(0, 0)
                v(0, 0)
                scores(0, 0)
                scores(0, 1)

            def slot(g, t, inside):
                if inside(t + 2):
                    scores(g, t + 2)
                if inside((t - 5) // C, C):
                    n, c = (t - 5) // C, (t - 5) % C
                    j, h = n // HEADS % BODY, n % HEADS
                    if c == 0:
                        for u in range(C * n + 2, C * n + 4):
                            wait_evac(pe, g, u)
                        wait(pe, o_done, g, n - 2)
                        if h == 0:
                            wait(pe, qkv_lo, g, 3 * (n // HEADS) + 2)
                    if SPLIT[h]:
                        for part in range(2):
                            last = pe.matmul(ps[0:2 * DH, O + n % 2], v_s[:, j, c, h], pt_s[:, part, c],
                                             start=c + part == 0, stop=(c, part) == (C - 1, 1))
                    else:
                        last = pe.matmul(ps[0:DH, O + n % 2], v_w[:, j, c, h], pt_w[:, c],
                                         start=c == 0, stop=c == C - 1)
                    if c == C - 1:
                        last.then_inc(o_ready.sem, 1)
                if inside(t):
                    wait(pe, exp_done, g, t)
                    wait_evac(pe, g, t - 2)
                    for c in range(C):
                        last = pe.transpose(ps[:, T + t % 2, c * P:(c + 1) * P], prob[:, t % 4, c * P:(c + 1) * P],
                                            ident[:])
                    last.then_inc(t_ready.sem, 1)
                if t % C == 2 and inside((t - 10) // C, C):
                    n = (t - 10) // C
                    wait_apart(pe, o_copied, g, n)
                    rows = 2 * DH if SPLIT[n % HEADS] else DH
                    for c in range(C):
                        last = pe.transpose(ps[:, O + n % 2, c * 2 * DH:c * 2 * DH + rows],
                                            o_t[0:rows, n % 2, c * P:(c + 1) * P], ident[0:rows, 0:rows])
                    last.then_inc(o_turned.sem, 1)
                if inside(t // TILES + 1, TILES):
                    for at, what in ((1, turn_x), (3, q_k), (5, v)):
                        if t % TILES == at:
                            what(g, t // TILES + 1)
            run(pe, start, slot)


def build(nc, d, out):
    with ExitStack() as ctx:
        x = ctx.enter_context(nc.sbuf_tensor("x_all", [P, BATCH, C, D], F32))
        with ExitStack() as first:
            sb = lambda n, s, t=F32R: first.enter_context(nc.sbuf_tensor(n, s, t))
            keep = (sb("at_split", [P, 2, C, N]), sb("a2t_split", [P, 2, C, N]), sb("ct_split", [P, 2, C, N]),
                    sb("c2t_split", [P, 2, C, N]), sb("g_split", [P, 2, 3, 3, D]), sb("v_sum", [P, C, D], F32), x)
            diffusion_setup(nc, d, keep)
            diffusion(nc, d, keep)
        dilated(nc, d, x)
        edge_attention(nc, d, x)
        self_attention(nc, d, x, out)


def kernel(**inputs):
    import numpy as np
    import concourse.bacc as bacc
    from concourse.bass_utils import run_bass_kernel_spmd

    a = {k: np.ascontiguousarray(v) for k, v in inputs.items()}
    flip = lambda v: np.ascontiguousarray(np.swapaxes(v, -1, -2))
    cols = lambda v: np.ascontiguousarray(v.reshape(-1, P).T)
    by_input = lambda w: np.ascontiguousarray(w.transpose(2, 0, 1))
    by_gate = lambda b: np.ascontiguousarray(b.reshape(SKIPS, 4, D).transpose(2, 0, 1))
    laid = {
        "x": a["x"], "xT": flip(a["x"]), "adj": a["adj"], "adjT": flip(a["adj"]),
        "alpha": a["L0_gnn_alpha_train"], "alpha_cols": cols(a["L0_gnn_alpha_train"]), "wT": flip(a["L0_gnn_w"]), "d": a["L0_gnn_d"],
        "fc_w": a["L0_gnn_fc_in_w"], "fc_b": a["L0_gnn_fc_in_b"],
        "Wg0": a["L1_gnn_Wg0"], "bg0": a["L1_gnn_bg0"], "Wg1": a["L1_gnn_Wg1"], "bg1": a["L1_gnn_bg1"],
        "WihT": by_input(a["L1_gnn_Wih"]), "WhhT": by_input(a["L1_gnn_Whh"]),
        "bih": by_gate(a["L1_gnn_bih"]), "bhh": by_gate(a["L1_gnn_bhh"]),
        "W_linT": flip(a["L2_gnn_W_lin"]), "W_valT": flip(a["L2_gnn_W_val"]), "W_outT": flip(a["L2_gnn_W_out"]),
        "a": a["L2_gnn_a"].reshape(D, 1), "src": a["L2_gnn_src"],
        "edge_ends": np.ascontiguousarray(np.stack([cols(a["L2_gnn_src"]), cols(a["L2_gnn_dst"])], -1)),
        "iota": np.tile(np.arange(N, dtype=np.float32), (P, 1)),
        "node": cols(np.arange(N, dtype=np.float32)),
        "head_mask": np.repeat(np.eye(HEADS, dtype=np.float32), DH, axis=0),
        "W_qkv": a["L3_gnn_W"],
        "ident": np.eye(P, dtype=np.float32),
    }
    nc = bacc.Bacc("TRN2", target_bir_lowering=False, num_devices=1)
    d, arrays = {}, {}
    for name, v in laid.items():
        arrays[f"in_{name}"] = v
        d[name] = nc.dram_tensor(f"in_{name}", v.shape, mybir.dt.from_np(v.dtype), kind="ExternalInput").ap()
    out = nc.dram_tensor("out", (BATCH, N, D), F32, kind="ExternalOutput").ap()
    build(nc, d, out)
    return run_bass_kernel_spmd(nc, [arrays], core_ids=[0]).results[0]["out"]
```

```python
from contextlib import ExitStack
from math import comb

import concourse.bass as bass
from concourse import mybir

F32 = mybir.dt.float32
F32R = mybir.dt.float32r
I32 = mybir.dt.int32
ALU = mybir.AluOpType
ACT = mybir.ActivationFunctionType
AX = mybir.AxisListType

P = 128
BATCH = 16
N = 512
D = 128
C = N // P
GB = 4
NG = BATCH // GB
STEPS = 8
DT = 1.0 / STEPS
EPS = 1e-5
SKIPS = 4
EDGES = 256
EC = EDGES // P
HEADS = 4
DH = D // HEADS
BIG = -3.0e38


class Count:

    def __init__(self, sem, per, aside=None):
        self.sem, self.per, self.aside = sem, per, aside

    def at(self, g, n):
        return g * self.per + (self.per + n + 1)


def credit(eng, *counts):
    for c in counts:
        eng.sem_inc(c.sem, c.per)


def wait(eng, c, g, n):
    eng.wait_ge(c.sem, c.at(g, n))


def wait_apart(eng, c, g, n):
    eng.wait_ge(c.sem, c.at(g, n))
    eng.sem_inc(c.aside, 1)


def staggered(eng, stages):
    def slots(g, ts, first, final):
        for t in ts:
            for lag, do in stages:
                if not (first and t < lag) and not (final and t - lag >= GB):
                    do(g, t - lag)

    slots(0, range(GB), True, False)
    with eng.Fori(1, NG) as g:
        slots(g, range(GB), False, False)
    slots(NG - 1, range(GB, GB + max(lag for lag, _ in stages)), False, True)


def f(ap):
    return ap.bitcast(F32)


def products(pe, out, lhs, rhs, start=True, stop=True):
    pe.matmul(out, lhs[0], rhs[0], start=start, stop=False)
    pe.matmul(out, lhs[0], rhs[1], start=False, stop=False)
    return pe.matmul(out, lhs[1], rhs[0], start=False, stop=stop)


class Norm:

    def __init__(self, nc, ctx, name, per, aside, eps=None, slots=2):
        sb = lambda n, s: ctx.enter_context(nc.sbuf_tensor(f"{name}_{n}", s, F32))
        self.slots, self.eps = slots, eps
        self.sum = sb("sum", [P, slots, C, D])
        self.stats = sb("stats", [P, slots, C, 6])
        self.mean_var = sb("mean_var", [P, slots, C, 2])
        self.var_eps = sb("var_eps", [P, slots, C])
        self.rstd = sb("rstd", [P, slots, C])
        self.power = sb("power", [P, C])
        c = lambda n: Count(ctx.enter_context(nc.semaphore(f"{name}_{n}")), per, aside)
        self.summed, self.counted, self.averaged = c("summed"), c("counted"), c("averaged")
        self.eps_added, self.rooted, self.normed = c("eps_added"), c("rooted"), c("normed")

    def dve_stats(self, dve, g, n):
        k = n % self.slots
        wait(dve, self.summed, g, n)
        for c in range(C):
            last = dve.bn_stats(self.stats[:, k, c, :], self.sum[:, k, c, :])
        last.then_inc(self.counted.sem, 1)
        wait_apart(dve, self.counted, g, n)
        for c in range(C):
            last = dve.bn_aggr(self.mean_var[:, k, c, :], self.stats[:, k, c, :])
        last.then_inc(self.averaged.sem, 1)

    def pool_root(self, pool, g, n):
        k = n % self.slots
        wait_apart(pool, self.averaged, g, n)
        if self.eps is None:
            ins = pool.tensor_scalar(self.var_eps[:, k, :], self.mean_var[:, k, :, 1], EPS, None, ALU.add)
        else:
            ins = pool.tensor_tensor(self.var_eps[:, k, :], self.mean_var[:, k, :, 1], self.eps[:], ALU.add)
        ins.then_inc(self.eps_added.sem, 1)
        wait_apart(pool, self.eps_added, g, n)
        pool.tensor_tensor(self.rstd[:, k, :], self.var_eps[:, k, :], self.power[:],
                           ALU.pow).then_inc(self.rooted.sem, 1)

    def dve_apply(self, dve, g, n, out):
        k = n % self.slots
        wait(dve, self.rooted, g, n)
        for c in range(C):
            last = dve.tensor_scalar(out(c), self.sum[:, k, c, :], self.mean_var[:, k, c, 0:1],
                                     self.rstd[:, k, c:c + 1], ALU.subtract, ALU.mult)
        last.then_inc(self.normed.sem, 1)

    def start_dve(self, dve):
        credit(dve, self.summed, self.counted, self.averaged, self.normed)

    def start_pool(self, pool):
        credit(pool, self.eps_added, self.rooted)
        pool.memset(self.power[:], -0.5)


def diffusion_setup(nc, d, keep):
    at_s, a2t_s, ct_s, c2t_s, g_s, v_sum, x = keep
    with ExitStack() as ctx:
        sb = lambda n, s, t=F32: ctx.enter_context(nc.sbuf_tensor(n, s, t))
        sem = lambda n: ctx.enter_context(nc.semaphore(n))
        adj = sb("s_adj", [P, C, N])
        adjt = sb("s_adjt", [P, C, N])
        a_s = sb("s_a_split", [P, 2, C, N], F32R)
        pair = sb("s_pair", [P, C, N])
        al_row = sb("s_al_row", [P, N])
        al_col = sb("s_al_col", [P, C])
        be_col = sb("s_be_col", [P, C])
        wt = sb("s_wt", [P, D]); dw = sb("s_dw", [P, D]); dcol = sb("s_dcol", [P, 1])
        fcw = sb("s_fcw", [P, D]); bcol = sb("s_bcol", [P, 1]); bwide = sb("s_bwide", [P, D])
        ident = sb("s_ident", [P, P])
        wp = sb("s_wp", [P, STEPS + 1, D])
        tk = sb("s_tk", [P, STEPS + 1, D])
        ck = sb("s_ck", [P, STEPS + 1, D])
        colsum = sb("s_colsum", [P, 2, N])
        s_all = sb("s_sj", [P, C, 3, D])
        ps_a = ctx.enter_context(nc.psum_tensor("s_ps_a", [P, 4, 512], F32))
        ps_w = ctx.enter_context(nc.psum_tensor("s_ps_w", [P, 4, 512], F32))

        adj_in, small_in, x_in = sem("s_adj_in"), sem("s_small_in"), sem("s_x_in")
        act_alpha, act_hi, dve_lo = sem("s_act_alpha"), sem("s_act_hi"), sem("s_dve_lo")
        dve_step, pe_a, pe_w, dve_w, dve_s = (sem("s_dve_step"), sem("s_pe_a"), sem("s_pe_w"),
                                              sem("s_dve_w"), sem("s_dve_s"))
        pe_t, act_a = sem("s_pe_t"), sem("s_act_a")
        block = ctx.enter_context(nc.Block())
        rows = lambda a: a.rearrange("(c p) m -> p c m", p=P)

        @block.sync
        def _(sp):
            sp.dma_start(al_row[:], d["alpha"].rearrange("(a n) -> a n", a=1).to_broadcast([P, N])).then_inc(small_in, 16)
            sp.dma_start(al_col[:], d["alpha_cols"]).then_inc(small_in, 16)
            sp.dma_start(wt[:], d["wT"]).then_inc(small_in, 16)
            sp.dma_start(dcol[:], d["d"].rearrange("(p a) -> p a", a=1)).then_inc(small_in, 16)
            sp.dma_start(fcw[:], d["fc_w"]).then_inc(small_in, 16)
            sp.dma_start(bcol[:], d["fc_b"].rearrange("(p a) -> p a", a=1)).then_inc(small_in, 16)
            sp.dma_start(ident[:], d["ident"]).then_inc(small_in, 16)
            sp.dma_start(adjt[:], rows(d["adjT"])).then_inc(adj_in, 16)
            sp.dma_start(adj[:], rows(d["adj"])).then_inc(adj_in, 16)
            for b in range(BATCH):
                sp.dma_start(x[:, b], rows(d["x"][b])).then_inc(x_in, 16)
            sp.wait_ge(x_in, 16 * BATCH)

        @block.scalar
        def _(act):
            act.wait_ge(small_in, 7 * 16)
            act.activation(al_row[:], al_row[:], ACT.Tanh, scale=0.5)
            act.activation(al_col[:], al_col[:], ACT.Tanh, scale=0.5).then_inc(act_alpha, 1)
            act.wait_ge(dve_step, 3)
            act.copy(at_s[:, 0], adjt[:]).then_inc(act_hi, 1)
            act.wait_ge(dve_step, 5)
            act.copy(a_s[:, 0], adj[:]).then_inc(act_hi, 1)
            for c in range(C):
                act.wait_ge(pe_a, c + 1)
                act.copy(a2t_s[:, 0, c], ps_a[:, c]).then_inc(act_hi, 1)
            for c in range(C):
                act.wait_ge(pe_a, C + c + 1)
                act.copy(pair[:, c], ps_a[:, c]).then_inc(act_a, 1)
                act.copy(ct_s[:, 0, c], ps_a[:, c]).then_inc(act_hi, 1)
            for c in range(C):
                act.wait_ge(pe_t, c + 1)
                act.copy(a_s[:, 0, c], ps_a[:, c]).then_inc(act_hi, 1)
            for c in range(C):
                act.wait_ge(pe_a, 2 * C + c + 1)
                act.copy(c2t_s[:, 0, c], ps_a[:, c]).then_inc(act_hi, 1)

        @block.vector
        def _(dve):
            dve.wait_ge(act_alpha, 1)
            dve.tensor_scalar(al_row[:], al_row[:], DT / 4, DT / 4, ALU.mult, ALU.add)
            dve.tensor_scalar(al_col[:], al_col[:], DT / 4, DT / 4, ALU.mult, ALU.add).then_inc(dve_step, 1)
            dve.wait_ge(dve_step, 1)
            dve.tensor_scalar(be_col[:], al_col[:], -1.0, 1.0 - DT, ALU.mult, ALU.add)
            dve.wait_ge(adj_in, 32)
            for c in range(C):
                last = dve.tensor_tensor(adjt[:, c], adjt[:, c], al_row[:], ALU.mult)
            last.then_inc(dve_step, 1)
            dve.wait_ge(dve_step, 2)
            for c in range(C):
                blk = adjt[:, c, c * P:(c + 1) * P]
                last = dve.scalar_tensor_tensor(blk, ident[:], be_col[:, c:c + 1], blk, ALU.mult, ALU.add)
            last.then_inc(dve_step, 1)
            for c in range(C):
                last = dve.tensor_scalar(adj[:, c], adj[:, c], al_col[:, c:c + 1], None, ALU.mult)
            last.then_inc(dve_step, 1)
            dve.wait_ge(dve_step, 4)
            for c in range(C):
                blk = adj[:, c, c * P:(c + 1) * P]
                last = dve.scalar_tensor_tensor(blk, ident[:], be_col[:, c:c + 1], blk, ALU.mult, ALU.add)
            last.then_inc(dve_step, 1)
            dve.tensor_scalar(dcol[:], dcol[:], 0.0, 1.0, ALU.max, ALU.min).then_inc(dve_w, 1)
            dve.wait_ge(dve_w, 1)
            dve.tensor_scalar(dw[:], wt[:], dcol[:], None, ALU.mult)
            dve.tensor_copy(wp[:, 0], ident[:])
            dve.tensor_scalar(bwide[:], ident[:], 0.0, bcol[:], ALU.mult, ALU.add).then_inc(dve_w, 1)
            dve.wait_ge(act_hi, 1)
            dve.tensor_tensor(at_s[:, 1], adjt[:], f(at_s[:, 0]), ALU.subtract).then_inc(dve_lo, 1)
            dve.wait_ge(act_hi, 2)
            dve.tensor_tensor(a_s[:, 1], adj[:], f(a_s[:, 0]), ALU.subtract).then_inc(dve_lo, 1)
            for n, (lo, k) in enumerate(((1, 1), (2, 1), (3, 2), (5, 4))):
                dve.wait_ge(pe_w, n + 1)
                dve.tensor_scalar(wp[:, lo:lo + k], ps_w[:, 0, 0:k * D].rearrange("p (k d) -> p k d", k=k),
                                  DT if n == 0 else 1.0, None, ALU.mult).then_inc(dve_w, 1)
            for c in range(C):
                dve.wait_ge(act_hi, 2 + c + 1)
                dve.tensor_tensor(a2t_s[:, 1, c], ps_a[:, c], f(a2t_s[:, 0, c]), ALU.subtract).then_inc(dve_lo, 1)
            dve.wait_ge(dve_w, 6)
            for s in range(STEPS):
                for k in range(STEPS - s):
                    if s == 0:
                        last = dve.tensor_scalar(tk[:, k], wp[:, 0], DT, None, ALU.mult)
                    else:
                        last = dve.scalar_tensor_tensor(tk[:, k], wp[:, s], DT * comb(k + s, k), tk[:, k],
                                                        ALU.mult, ALU.add)
                last.then_inc(dve_s, 1)
                dve.wait_ge(dve_s, s + 1)
            dve.wait_ge(pe_w, 6)
            for q in range(STEPS + 1):
                k = STEPS - q
                src = ps_w[:, 1 + q // 4, (q % 4) * D:(q % 4 + 1) * D]
                if k == STEPS:
                    last = dve.tensor_copy(tk[:, k], src)
                else:
                    last = dve.scalar_tensor_tensor(tk[:, k], src, float(comb(STEPS, k)), tk[:, k], ALU.mult, ALU.add)
            last.then_inc(dve_w, 1)
            dve.wait_ge(dve_w, 7)
            for j in range(3):
                last = dve.tensor_copy(g_s[:, 0, :, j], tk[:, 3 * j:3 * j + 3])
            last.then_inc(dve_w, 1)
            dve.wait_ge(dve_w, 8)
            for j in range(3):
                last = dve.tensor_tensor(g_s[:, 1, :, j], tk[:, 3 * j:3 * j + 3], f(g_s[:, 0, :, j]), ALU.subtract)
            last.then_inc(dve_w, 1)
            dve.wait_ge(pe_w, 7)
            for q in range(STEPS + 1):
                k = STEPS - q
                src = ps_w[:, 1 + q // 4, (q % 4) * D:(q % 4 + 1) * D]
                last = dve.tensor_scalar(ck[:, k], src, float(comb(STEPS, k)), None, ALU.mult)
            last.then_inc(dve_w, 1)
            for c in range(C):
                dve.wait_ge(act_hi, 6 + c + 1)
                dve.tensor_tensor(ct_s[:, 1, c], ps_a[:, c], f(ct_s[:, 0, c]), ALU.subtract).then_inc(dve_lo, 1)
            for i, part in enumerate((at_s, a2t_s)):
                last = dve.tensor_reduce(colsum[:, i], f(part[:, 0]).rearrange("p c n -> p n c"), AX.X, ALU.add)
            last.then_inc(dve_w, 1)
            for c in range(C):
                dve.wait_ge(act_hi, 10 + c + 1)
                dve.tensor_tensor(a_s[:, 1, c], ps_a[:, c], f(a_s[:, 0, c]), ALU.subtract).then_inc(dve_lo, 1)
            for c in range(C):
                dve.wait_ge(act_hi, 14 + c + 1)
                dve.tensor_tensor(c2t_s[:, 1, c], ps_a[:, c], f(c2t_s[:, 0, c]), ALU.subtract).then_inc(dve_lo, 1)
            for i, part in enumerate((at_s, a2t_s)):
                for c in range(C):
                    dve.wait_ge(dve_w, 11 + i * C + c)
                    dve.tensor_tensor(colsum[:, i], colsum[:, i], f(part[:, 1, c]), ALU.add).then_inc(dve_w, 1)
            for c in range(C):
                dve.wait_ge(pe_w, 8 + c)
                dve.tensor_tensor(s_all[:, c], ps_w[:, c % 2, 0:3 * D].rearrange("p (j d) -> p j d", j=3),
                                  ck[:, 0:STEPS + 1:3], ALU.add).then_inc(dve_s, 1)
            for c in range(C):
                dve.wait_ge(pe_w, 12 + c)
                dve.tensor_tensor(v_sum[:, c], ps_w[:, 2 + c % 2, 0:D], s_all[:, c, 0], ALU.add).then_inc(dve_s, 1)

        @block.tensor
        def _(pe):
            pe.wait_ge(dve_w, 2)
            pe.matmul(ps_w[:, 0, 0:D], dw[:], wt[:], start=True, stop=True).then_inc(pe_w, 1)
            pe.wait_ge(dve_w, 3)
            pe.matmul(ps_w[:, 0, 0:D], wp[:, 1], wp[:, 1], start=True, stop=True).then_inc(pe_w, 1)
            pe.wait_ge(dve_w, 4)
            pe.matmul(ps_w[:, 0, 0:2 * D], wp[:, 2], wp[:, 1:3], start=True, stop=True).then_inc(pe_w, 1)
            pe.wait_ge(dve_w, 5)
            pe.matmul(ps_w[:, 0, 0:4 * D], wp[:, 4], wp[:, 1:5], start=True, stop=True).then_inc(pe_w, 1)
            pe.wait_ge(dve_lo, 2)
            for m in range(C):
                for k in range(C):
                    last = products(pe, ps_a[:, m], [a_s[:, h, k, m * P:(m + 1) * P] for h in range(2)],
                                    [at_s[:, h, k] for h in range(2)], k == 0, k == C - 1)
                last.then_inc(pe_a, 1)
            pe.wait_ge(dve_w, 6)
            for bank, lo, k in ((1, 0, 4), (2, 4, 4), (3, 8, 1)):
                last = pe.matmul(ps_w[:, bank, 0:k * D], fcw[:], wp[:, lo:lo + k], start=True, stop=True)
            last.then_inc(pe_w, 2)
            pe.wait_ge(dve_w, 7)
            for bank, lo, k in ((1, 0, 4), (2, 4, 4), (3, 8, 1)):
                last = pe.matmul(ps_w[:, bank, 0:k * D], bwide[:], wp[:, lo:lo + k], start=True, stop=True)
            last.then_inc(pe_w, 1)
            pe.wait_ge(dve_lo, 2 + C)
            for m in range(C):
                for k in range(C):
                    last = products(pe, ps_a[:, m], [a_s[:, h, k, m * P:(m + 1) * P] for h in range(2)],
                                    [a2t_s[:, h, k] for h in range(2)], k == 0, k == C - 1)
                last.then_inc(pe_a, 1)
            pe.wait_ge(act_a, C)
            pe.wait_ge(dve_lo, 2 + 2 * C)
            for m in range(C):
                for k in range(C):
                    last = pe.transpose(ps_a[:, m, k * P:(k + 1) * P], pair[:, k, m * P:(m + 1) * P], ident[:])
                last.then_inc(pe_t, 1)
            pe.wait_ge(dve_lo, 2 + 3 * C)
            for m in range(C):
                for k in range(C):
                    last = products(pe, ps_a[:, m], [a_s[:, h, k, m * P:(m + 1) * P] for h in range(2)],
                                    [ct_s[:, h, k] for h in range(2)], k == 0, k == C - 1)
                last.then_inc(pe_a, 1)
            pe.wait_ge(dve_lo, 2 + 4 * C)
            pe.wait_ge(dve_w, 11 + 2 * C)
            for c in range(C):
                if c >= 2:
                    pe.wait_ge(dve_s, STEPS + c - 1)
                for i in range(2):
                    last = pe.matmul(ps_w[:, c % 2, 0:3 * D], colsum[:, i, c * P:(c + 1) * P],
                                     ck[:, i + 1:STEPS + 1:3], start=i == 0, stop=i == 1)
                last.then_inc(pe_w, 1)
            pe.wait_ge(dve_s, STEPS + C)
            for c in range(C):
                if c >= 2:
                    pe.wait_ge(dve_s, STEPS + C + c - 1)
                for j, part in ((1, ct_s), (2, c2t_s)):
                    for k in range(C):
                        for h in range(2):
                            last = pe.matmul(ps_w[:, 2 + c % 2, 0:D], f(part[:, h, k, c * P:(c + 1) * P]), s_all[:, k, j],
                                             start=(j, k, h) == (1, 0, 0), stop=(j, k, h) == (2, C - 1, 1))
                last.then_inc(pe_w, 1)


def diffusion(nc, d, keep):
    at_s, a2t_s, ct_s, c2t_s, g_s, v_sum, x = keep
    with ExitStack() as ctx:
        sb = lambda n, s, t=F32: ctx.enter_context(nc.sbuf_tensor(n, s, t))
        count = lambda n, per: Count(ctx.enter_context(nc.semaphore(n)), per, aside)
        x_s = sb("x_split", [P, 2, GB, C, D], F32R)
        xt = sb("xt", [P, 2, N])
        base_s = sb("base_split", [P, 2, 3, 2, N], F32R)
        x_v = sb("x_plus_v", [P, GB, C, D])
        rest = sb("rest", [P, C, GB, D])
        z_s = sb("z_split", [P, 2, 2, C, GB, D], F32R)
        aside = ctx.enter_context(nc.semaphore("aside"))
        norm = Norm(nc, ctx, "ln0", C, aside)
        ps_base = ctx.enter_context(nc.psum_tensor("ps_base", [P, 2, 2, N], F32))
        ps_z = ctx.enter_context(nc.psum_tensor("ps_z", [P, 2, N], F32))
        ps_out = ctx.enter_context(nc.psum_tensor("ps_out", [P, 2, N], F32))

        xt_in = [count(f"xt_in{q}", 16 * GB // 2) for q in range(2)]
        x_hi, x_lo, xt_hi, xt_lo, xv_done = (count(n, GB) for n in ("x_hi", "x_lo", "xt_hi", "xt_lo", "xv_done"))
        base_ready, base_hi, base_lo = (count(n, 2 * GB) for n in ("base_ready", "base_hi", "base_lo"))
        z_ready, z_hi, z_lo, rest_done = (count(n, C * GB) for n in ("z_ready", "z_hi", "z_lo", "rest_done"))
        out_ready = count("out_ready", C)
        block = ctx.enter_context(nc.Block())

        @block.sync
        def _(sp):
            for q in range(2):
                credit(sp, xt_in[q])
            with sp.Fori(0, NG) as g:
                for b in range(GB):
                    wait(sp, xt_lo, g, b - 2)
                    sp.dma_start(xt[:, b % 2], d["xT"][bass.ds(g * GB + b, 1)].rearrange("a d n -> (a d) n")
                                 ).then_inc(xt_in[b % 2].sem, 16)

        @block.gpsimd
        def _(pool):
            credit(pool, x_hi, x_lo, xt_hi, xt_lo, xv_done)
            norm.start_pool(pool)
            rows = lambda g, b: x[:, bass.ds(g * GB + b, 1)].rearrange("p a c d -> p (a c) d")

            def split(g, n):
                b = n % GB
                wait_apart(pool, base_lo, g, 2 * (n - GB) + 1)
                pool.tensor_copy(x_s[:, 0, b], rows(g, n)).then_inc(x_hi.sem, 1)
                wait_apart(pool, x_hi, g, n)
                pool.tensor_tensor(x_s[:, 1, b], rows(g, n), f(x_s[:, 0, b]), ALU.subtract).then_inc(x_lo.sem, 1)

            def split_t(g, n):
                b = n % GB
                wait_apart(pool, xt_in[b % 2], g, 16 * (n // 2) + 15)
                wait_apart(pool, z_lo, g, C * (n - 2) + C - 1)
                pool.tensor_copy(base_s[:, b % 2, 0, 0], xt[:, b % 2]).then_inc(xt_hi.sem, 1)
                wait_apart(pool, xt_hi, g, n)
                pool.tensor_tensor(base_s[:, b % 2, 0, 1], xt[:, b % 2], f(base_s[:, b % 2, 0, 0]),
                                   ALU.subtract).then_inc(xt_lo.sem, 1)
                wait_apart(pool, rest_done, g, C * (n - GB) + C - 1)
                pool.tensor_tensor(x_v[:, b], rows(g, n), v_sum[:], ALU.add).then_inc(xv_done.sem, 1)

            def roots(g):
                for c in range(C):
                    norm.pool_root(pool, g, c)

            split(0, 0)
            split(0, 1)
            split_t(0, 0)
            split(0, 2)
            split_t(0, 1)
            split(0, 3)
            with pool.Fori(0, NG - 1) as g:
                for b in range(GB):
                    split(g, GB + b)
                    split_t(g, 2 + b)
                roots(g)
            split_t(NG - 1, 2)
            split_t(NG - 1, 3)
            roots(NG - 1)

        @block.scalar
        def _(act):
            credit(act, base_hi, z_hi)
            with act.Fori(0, NG) as g:
                def base(b):
                    for i in range(2):
                        wait(act, base_ready, g, 2 * b + i)
                        wait(act, z_lo, g, C * (b - 2) + C - 1)
                        act.copy(base_s[:, b % 2, i + 1, 0], ps_base[:, b % 2, i]).then_inc(base_hi.sem, 1)
                base(0)
                for b in range(GB):
                    if b + 1 < GB:
                        base(b + 1)
                    if b == 0:
                        wait(act, out_ready, g, -1)
                    for c in range(C):
                        wait(act, z_ready, g, C * b + c)
                        act.copy(z_s[:, :, 0, c, b], ps_z[:, c % 2, D:3 * D].rearrange("p (j d) -> p j d", j=2)
                                 ).then_inc(z_hi.sem, 1)

        @block.vector
        def _(dve):
            credit(dve, base_lo, z_lo, rest_done)
            norm.start_dve(dve)
            with dve.Fori(0, NG) as g:
                def base(b):
                    for i in range(2):
                        wait(dve, base_hi, g, 2 * b + i)
                        dve.tensor_tensor(base_s[:, b % 2, i + 1, 1], ps_base[:, b % 2, i],
                                          f(base_s[:, b % 2, i + 1, 0]), ALU.subtract).then_inc(base_lo.sem, 1)
                base(0)
                for b in range(GB):
                    if b + 1 < GB:
                        base(b + 1)
                    wait(dve, xv_done, g, b)
                    for c in range(C):
                        wait(dve, z_hi, g, C * b + c)
                        dve.tensor_tensor(rest[:, c, b], ps_z[:, c % 2, 0:D], x_v[:, b, c],
                                          ALU.add).then_inc(rest_done.sem, 1)
                        dve.tensor_tensor(z_s[:, :, 1, c, b], ps_z[:, c % 2, D:3 * D].rearrange("p (j d) -> p j d", j=2),
                                          f(z_s[:, :, 0, c, b]), ALU.subtract).then_inc(z_lo.sem, 1)
                for c in range(C):
                    wait(dve, out_ready, g, c)
                    wait(dve, norm.normed, g, c - 2)
                    wait(dve, rest_done, g, C * GB - 1)
                    dve.tensor_tensor(norm.sum[:, c % 2], ps_out[:, c % 2].rearrange("p (b d) -> p b d", b=GB),
                                      rest[:, c], ALU.add).then_inc(norm.summed.sem, 1)
                    norm.dve_stats(dve, g, c)
                    norm.dve_apply(dve, g, c, lambda b: x[:, bass.ds(g * GB + b, 1), c].rearrange("p a d -> p (a d)"))

        @block.tensor
        def _(pe):
            credit(pe, base_ready, z_ready, out_ready)
            with pe.Fori(0, NG) as g:
                def base(b):
                    wait(pe, x_lo, g, b)
                    for i, m in enumerate((at_s, a2t_s)):
                        wait(pe, base_lo, g, 2 * (b - 2) + i)
                        for c in range(C):
                            last = products(pe, ps_base[:, b % 2, i], [x_s[:, h, b, c] for h in range(2)],
                                            [m[:, h, c] for h in range(2)], c == 0, c == C - 1)
                        last.then_inc(base_ready.sem, 1)
                base(0)
                for b in range(GB):
                    if b + 1 < GB:
                        base(b + 1)
                    wait(pe, xt_lo, g, b)
                    wait(pe, base_lo, g, 2 * b + 1)
                    for c in range(C):
                        wait(pe, z_lo, g, C * b + c - 2)
                        for i in range(3):
                            last = products(pe, ps_z[:, c % 2, 0:3 * D],
                                            [base_s[:, b % 2, i, h, c * P:(c + 1) * P] for h in range(2)],
                                            [g_s[:, h, i] for h in range(2)], i == 0, i == 2)
                        last.then_inc(z_ready.sem, 1)
                wait(pe, z_lo, g, C * GB - 1)
                for c in range(C):
                    wait(pe, norm.summed, g, c - 2)
                    for j, m in enumerate((ct_s, c2t_s)):
                        for k in range(C):
                            last = products(pe, ps_out[:, c % 2], [m[:, h, k, c * P:(c + 1) * P] for h in range(2)],
                                            [z_s[:, j, h, k] for h in range(2)], j + k == 0, (j, k) == (1, C - 1))
                    last.then_inc(out_ready.sem, 1)


def lstm_steps():
    steps = [(1, 0, b, N, "igo") for b in range(GB)]
    for p in range(2, SKIPS + 1):
        steps += [(p, s, q, N // p, "igfo" if s else "igo") for s in range(p) for q in range(2)]
    return steps


LSTM = lstm_steps()
GATE = {"i": 0, "f": 1, "g": 2, "o": 3}
FIRST_GATE = [sum(len(t[4]) for t in LSTM[:k]) for k in range(len(LSTM) + 1)]


def gate_number(k, gate):
    return FIRST_GATE[k] + LSTM[k][4].index(gate)


def windows(tile, k):
    p, s, q, w, _ = LSTM[k]
    if p == 1:
        return tile[:, q]
    return tile[:, 2 * q:2 * q + 2, s:s + p * (w - 1) + 1:p]


def flat(tile, k):
    p, s, q, w, _ = LSTM[k]
    if p == 1:
        return tile
    return tile[:, 0:2 * w].rearrange("p (b w) -> p b w", b=2)


def columns(k):
    return LSTM[k][3] * (1 if LSTM[k][0] == 1 else 2)


def dilated(nc, d, x):
    with ExitStack() as ctx:
        sb = lambda n, s, t=F32: ctx.enter_context(nc.sbuf_tensor(n, s, t))
        sem = lambda n: ctx.enter_context(nc.semaphore(n))
        at_s = sb("d_at_split", [P, 2, C, N], F32R)
        wg_s = sb("d_wg_split", [P, 2, 2, D], F32R)
        wih_s = sb("d_wih_split", [P, 2, SKIPS, 4 * D], F32R)
        whh_s = sb("d_whh_split", [P, 2, SKIPS, 4 * D], F32R)
        gate_b = sb("d_gate_bias", [P, SKIPS, 4])
        ident = sb("d_ident", [P, P])
        ident_r = sb("d_ident_r", [P, P], F32R)
        b_stack = sb("d_b_stack", [96, 2, D], F32R)
        r_stack = sb("d_r_stack", [96, N], F32R)
        x_s = sb("d_x_split", [P, 2, GB, C, D], F32R)
        ax_s = sb("d_ax_split", [P, GB, 2, N], F32R)
        h1_s = sb("d_h1_split", [P, GB, 2, C, D], F32R)
        ps = ctx.enter_context(nc.psum_tensor("d_banks", [P, 8, N], F32))
        K, GATES = len(LSTM), FIRST_GATE[-1]
        aside = sem("d_aside")
        count = lambda n, per: Count(sem(n), per, aside)
        count = lambda n, per: Count(sem(n), per, aside)
        x_hi, x_lo = count("d_x_hi", GB), count("d_x_lo", GB)
        conv_ready, conv_hi, conv_lo = (count(n, 4 * GB) for n in ("d_conv_ready", "d_conv_hi", "d_conv_lo"))
        RING = 6
        assert GATES % RING == 0 and K == 22
        UNITS_AT = {6: 0, 8: 1, 10: 2, 12: 3, 14: 4, 16: 5, 18: 6, 20: 7}
        TAIL = ((8,), (9,), (10,), (11,))
        OUT_STAGE = 3 * GB

        def split(pool, g, ahead):
            for b in range(GB):
                src = x[:, bass.ds(g * GB + (ahead * GB + b), 1)].rearrange("p a c d -> p (a c) d")
                wait_apart(pool, conv_hi, g, b - 4 * GB * (1 - ahead))
                pool.tensor_copy(x_s[:, 0, b], src).then_inc(x_hi.sem, 1)
                wait_apart(pool, x_hi, g, b + GB * ahead)
                pool.tensor_tensor(x_s[:, 1, b], src, f(x_s[:, 0, b]), ALU.subtract).then_inc(x_lo.sem, 1)

        def unit(pe, g, n):
            stage, b = n // GB % 4, n % GB
            bank = ps[:, RING + n % 2]
            if stage == 0:
                wait(pe, x_lo, g, n // (4 * GB) * GB + b)
            wait(pe, conv_lo, g, n - 2)
            if stage == 0:
                for c in range(C):
                    last = products(pe, bank, [x_s[:, h, b, c] for h in range(2)],
                                    [at_s[:, h, c] for h in range(2)], c == 0, c == C - 1)
            elif stage == 1:
                for c in range(C):
                    cols = slice(c * P, (c + 1) * P)
                    products(pe, bank[:, cols], [ax_s[:, b, h, cols] for h in range(2)],
                             [wg_s[:, h, 0] for h in range(2)], True, False)
                    last = pe.matmul(bank[:, cols], r_stack[:, cols], b_stack[:, 0], start=False, stop=True)
            elif stage == 2:
                for c in range(C):
                    last = products(pe, bank, [h1_s[:, b, h, c] for h in range(2)],
                                    [at_s[:, h, c] for h in range(2)], c == 0, c == C - 1)
            else:
                products(pe, bank, [wg_s[:, h, 1] for h in range(2)],
                         [ax_s[:, b, h] for h in range(2)], True, False)
                last = pe.matmul(bank, b_stack[:, 1], r_stack[:], start=False, stop=True)
            last.then_inc(conv_ready.sem, 1)

        def unit_hi(act, g, n):
            stage, b = n // GB % 4, n % GB
            bank = ps[:, RING + n % 2]
            wait(act, conv_ready, g, n)
            if stage == 1:
                act.activation(h1_s[:, b, 0], bank.rearrange("p (c d) -> p c d", c=C), ACT.Relu
                               ).then_inc(conv_hi.sem, 1)
            elif stage == 3:
                act.activation(h_s[:, 0, b], bank, ACT.Relu).then_inc(conv_hi.sem, 1)
            else:
                act.copy(ax_s[:, b, 0], bank).then_inc(conv_hi.sem, 1)

        def unit_lo(dve, g, n):
            stage, b = n // GB % 4, n % GB
            bank = ps[:, RING + n % 2]
            wait(dve, conv_hi, g, n)
            if stage == 1:
                ins = dve.scalar_tensor_tensor(h1_s[:, b, 1], bank.rearrange("p (c d) -> p c d", c=C), 0.0,
                                               f(h1_s[:, b, 0]), ALU.max, ALU.subtract)
            elif stage == 3:
                ins = dve.scalar_tensor_tensor(h_s[:, 1, b], bank, 0.0, f(h_s[:, 0, b]), ALU.max, ALU.subtract)
            else:
                ins = dve.tensor_tensor(ax_s[:, b, 1], bank, f(ax_s[:, b, 0]), ALU.subtract)
            ins.then_inc(conv_lo.sem, 1)

        with ExitStack() as tmp:
            tb = lambda n, s, t=F32: tmp.enter_context(nc.sbuf_tensor(n, s, t))
            at = tb("d_at", [P, C, N])
            wg = tb("d_wg", [P, 2, D])
            wih = tb("d_wih", [P, SKIPS, 4 * D])
            whh = tb("d_whh", [P, SKIPS, 4 * D])
            bih = tb("d_bih", [P, SKIPS, 4])
            bhh = tb("d_bhh", [P, SKIPS, 4])
            brow = tb("d_brow", [96, 2, D])
            rsum = tb("d_rsum", [96, N])
            ones = tb("d_ones", [P, 96], F32R)
            small_in, adj_in, w_in = (tmp.enter_context(nc.semaphore(n)) for n in ("d_small_in", "d_adj_in", "d_w_in"))
            act_hi, dve_lo, pe_sum, cleared, halved = (tmp.enter_context(nc.semaphore(n)) for n in
                                              ("d_act_hi", "d_dve_lo", "d_pe_sum", "d_cleared", "d_halved"))
            block = tmp.enter_context(nc.Block())

            @block.sync
            def _(sp):
                sp.dma_start(at[:], d["adjT"].rearrange("(c p) m -> p c m", p=P)).then_inc(adj_in, 16)
                for r in range(3):
                    for layer in range(2):
                        sp.dma_start(brow[32 * r:32 * r + 1, layer], d[f"bg{layer}"].rearrange("(a n) -> a n", a=1)
                                     ).then_inc(small_in, 16)
                for layer in range(2):
                    sp.dma_start(wg[:, layer], d[f"Wg{layer}"]).then_inc(small_in, 16)
                sp.dma_start(bih[:], d["bih"]).then_inc(small_in, 16)
                sp.dma_start(bhh[:], d["bhh"]).then_inc(small_in, 16)
                sp.dma_start(ident[:], d["ident"]).then_inc(small_in, 16)
                sp.dma_start(wih[:], d["WihT"]).then_inc(w_in, 16)
                sp.dma_start(whh[:], d["WhhT"]).then_inc(w_in, 16)

            @block.gpsimd
            def _(pool):
                credit(pool, x_hi, x_lo)
                pool.memset(f(b_stack[:]), 0.0)
                pool.memset(f(r_stack[:]), 0.0).then_inc(cleared, 1)
                split(pool, 0, 0)

            @block.scalar
            def _(act):
                credit(act, conv_hi)
                act.wait_ge(adj_in, 16)
                act.copy(at_s[:, 0], at[:]).then_inc(act_hi, 1)
                for u in range(2 * GB):
                    unit_hi(act, 0, u)
                act.wait_ge(w_in, 32)
                act.copy(wih_s[:, 0, 0], wih[:, 0])
                act.wait_ge(halved, 1)
                act.copy(wih_s[:, 0, 1:], wih[:, 1:])
                act.copy(whh_s[:, 0], whh[:]).then_inc(act_hi, 1)
                for u in range(2 * GB, OUT_STAGE):
                    unit_hi(act, 0, u)

            @block.vector
            def _(dve):
                credit(dve, conv_lo)
                dve.memset(f(ones[:]), 1.0)
                dve.wait_ge(adj_in, 16)
                dve.wait_ge(act_hi, 1)
                dve.tensor_tensor(at_s[:, 1], at[:], f(at_s[:, 0]), ALU.subtract).then_inc(dve_lo, 1)
                dve.wait_ge(small_in, 11 * 16)
                dve.tensor_copy(wg_s[:, 0], wg[:])
                dve.tensor_copy(ident_r[:], ident[:])
                dve.tensor_tensor(gate_b[:], bih[:], bhh[:], ALU.add).then_inc(dve_lo, 1)
                dve.wait_ge(cleared, 1)
                for r in range(3):
                    last = dve.tensor_copy(b_stack[32 * r:32 * r + 1], brow[32 * r:32 * r + 1])
                last.then_inc(dve_lo, 1)
                unit_lo(dve, 0, 0)
                dve.wait_ge(dve_lo, 3)
                dve.tensor_tensor(wg_s[:, 1], wg[:], f(wg_s[:, 0]), ALU.subtract)
                for gate in "ifo":
                    dve.tensor_scalar(gate_b[:, :, GATE[gate]], gate_b[:, :, GATE[gate]], 0.5, None, ALU.mult)
                dve.tensor_tensor(b_stack[64:65], brow[64:65], f(b_stack[64:65]), ALU.subtract)
                for u in range(1, GB - 1):
                    unit_lo(dve, 0, u)
                dve.wait_ge(pe_sum, 1)
                dve.tensor_copy(rsum[:], ps[0:96, 0])
                for r in range(3):
                    last = dve.tensor_copy(r_stack[32 * r:32 * r + 1], ps[32 * r:32 * r + 1, 0])
                last.then_inc(dve_lo, 1)
                dve.wait_ge(dve_lo, 4)
                dve.tensor_tensor(r_stack[32:33], rsum[32:33], f(r_stack[32:33]), ALU.subtract).then_inc(dve_lo, 1)
                for u in range(GB - 1, 2 * GB):
                    unit_lo(dve, 0, u)
                dve.wait_ge(w_in, 32)
                dve.tensor_scalar(wih[:, 1:], wih[:, 1:], 0.5, None, ALU.mult)
                dve.tensor_scalar(whh[:], whh[:], 0.5, None, ALU.mult).then_inc(halved, 1)
                for u in range(2 * GB, OUT_STAGE):
                    unit_lo(dve, 0, u)
                dve.wait_ge(act_hi, 2)
                dve.tensor_tensor(wih_s[:, 1], wih[:], f(wih_s[:, 0]), ALU.subtract)
                dve.tensor_tensor(whh_s[:, 1], whh[:], f(whh_s[:, 0]), ALU.subtract)

            @block.tensor
            def _(pe):
                credit(pe, conv_ready)
                pe.wait_ge(dve_lo, 1)
                for u in range(OUT_STAGE):
                    if u == GB - 2:
                        for c in range(C):
                            for h in range(2):
                                last = pe.matmul(ps[0:96, 0], ones[:], at_s[:, h, c], start=c + h == 0,
                                                 stop=(c, h) == (C - 1, 1))
                        last.then_inc(pe_sum, 1)
                    if u == GB:
                        pe.wait_ge(dve_lo, 5)
                    unit(pe, 0, u)

        h_s = sb("d_h_split", [P, 2, GB, N], F32R)
        cell_s = sb("d_cell_split", [P, 2, 2, N], F32R)
        gates = sb("d_gates", [P, 2, 4, N])
        state = sb("d_state", [P, 2, N])
        ig = sb("d_ig", [P, 2, N])
        fc = sb("d_fc", [P, 2, N])
        tc = sb("d_tc", [P, 2, N])
        h2 = sb("d_h2", [P, 2, N])
        norm = Norm(nc, ctx, "ln1", GB, aside)
        gate_ready, gate_tanh = count("d_gate_ready", GATES), count("d_gate_tanh", GATES)
        LATER = sum(1 for t in LSTM if t[1])
        ig_done, fc_done = count("d_ig_done", LATER), count("d_fc_done", LATER)
        state_done, state_tanh, h2_done, h2_hi, h2_lo = (
            count("d_" + n, K) for n in ("state_done", "state_tanh", "h2_done", "h2_hi", "h2_lo"))
        turned = count("d_turned", GB)
        block = ctx.enter_context(nc.Block())
        @block.gpsimd
        def _(pool):
            norm.start_pool(pool)

            def roots(g):
                for b in range(GB):
                    norm.pool_root(pool, g, b)

            with pool.Fori(0, NG - 1) as g:
                split(pool, g, 1)
                roots(g)
            roots(NG - 1)

        @block.scalar
        def _(act):
            credit(act, gate_tanh, state_tanh)

            def gate_tanhs(g, k, which):
                p, s, q, _, names = LSTM[k]
                for gate in which:
                    if gate in names:
                        n = gate_number(k, gate)
                        wait(act, gate_ready, g, n)
                        act.activation(gates[:, k % 2, GATE[gate], 0:columns(k)], ps[:, n % RING, 0:columns(k)],
                                       ACT.Tanh, bias=gate_b[:, p - 1, GATE[gate]:GATE[gate] + 1],
                                       scale=1.0 if gate == "g" else 0.5).then_inc(gate_tanh.sem, 1)

            def state_tanhs(g, k):
                wait(act, state_done, g, k)
                act.activation(tc[:, k % 2, 0:columns(k)], state[:, k % 2, 0:columns(k)], ACT.Tanh,
                               scale=0.5).then_inc(state_tanh.sem, 1)

            def body(g, ahead):
                unit_hi(act, g, OUT_STAGE)
                for k in range(K):
                    if k < GB - 1:
                        unit_hi(act, g, OUT_STAGE + k + 1)
                    if k >= GB:
                        state_tanhs(g, k - 1)
                    if ahead and k in UNITS_AT:
                        unit_hi(act, g, 4 * GB + UNITS_AT[k])
                    wait(act, h2_done, g, k - 2)
                    gate_tanhs(g, k, "ig")
                    if 0 < k < GB:
                        state_tanhs(g, k - 1)
                    gate_tanhs(g, k, "fo")
                state_tanhs(g, K - 1)
                if ahead:
                    for b in range(GB):
                        for u in TAIL[b]:
                            unit_hi(act, g, 4 * GB + u)

            with act.Fori(0, NG - 1) as g:
                body(g, True)
            body(NG - 1, False)

        @block.vector
        def _(dve):
            credit(dve, ig_done, fc_done, state_done, h2_done, h2_hi, h2_lo)
            norm.start_dve(dve)

            def output(g, k):
                p, s, q, _, _ = LSTM[k]
                w = columns(k)
                gk, hk = gates[:, k % 2], h2[:, k % 2, 0:w]
                hi, lo = ((flat(cell_s[:, k % 2, 0], k), flat(cell_s[:, k % 2, 1], k)) if s < p - 1 else
                          (windows(h_s[:, 0], k), windows(h_s[:, 1], k)))
                wait(dve, gate_tanh, g, gate_number(k, "o"))
                wait(dve, state_tanh, g, k)
                dve.scalar_tensor_tensor(hk, gk[:, 3, 0:w], 1.0, tc[:, k % 2, 0:w], ALU.add, ALU.mult
                                         ).then_inc(h2_done.sem, 1)
                wait(dve, h2_done, g, k)
                dve.tensor_copy(hi, flat(h2[:, k % 2], k)).then_inc(h2_hi.sem, 1)
                wait(dve, h2_hi, g, k)
                dve.tensor_tensor(lo, flat(h2[:, k % 2], k), f(hi), ALU.subtract).then_inc(h2_lo.sem, 1)

            def body(g, ahead):
                unit_lo(dve, g, OUT_STAGE)
                for k in range(K):
                    p, s, q, _, _ = LSTM[k]
                    w = columns(k)
                    gk = gates[:, k % 2]
                    if k < GB - 1:
                        unit_lo(dve, g, OUT_STAGE + k + 1)
                    if k >= GB:
                        output(g, k - 1)
                    if ahead and k in UNITS_AT:
                        unit_lo(dve, g, 4 * GB + UNITS_AT[k])
                    wait(dve, gate_tanh, g, gate_number(k, "g"))
                    target = ig[:, k % 2, 0:w] if s else state[:, k % 2, 0:w]
                    ins = dve.scalar_tensor_tensor(target, gk[:, 0, 0:w], 1.0, gk[:, 2, 0:w], ALU.add, ALU.mult)
                    ins.then_inc((ig_done if s else state_done).sem, 1)
                    if 0 < k < GB:
                        output(g, k - 1)
                    if s:
                        wait(dve, gate_tanh, g, gate_number(k, "f"))
                        dve.scalar_tensor_tensor(fc[:, k % 2, 0:w], gk[:, 1, 0:w], 1.0, state[:, k % 2, 0:w],
                                                 ALU.add, ALU.mult).then_inc(fc_done.sem, 1)
                        later = sum(1 for t in LSTM[:k] if t[1])
                        wait(dve, ig_done, g, later)
                        wait(dve, fc_done, g, later)
                        dve.scalar_tensor_tensor(state[:, k % 2, 0:w], fc[:, k % 2, 0:w], 0.5, ig[:, k % 2, 0:w],
                                                 ALU.mult, ALU.add).then_inc(state_done.sem, 1)
                output(g, K - 1)
                for b in range(GB + 1):
                    if b < GB:
                        wait(dve, turned, g, b)
                        wait(dve, norm.normed, g, b - 2)
                        dve.scalar_tensor_tensor(norm.sum[:, b % 2].rearrange("p c d -> p (c d)"), ps[:, b], 0.5,
                                                 x[:, bass.ds(g * GB + b, 1)].rearrange("p a c d -> p (a c d)"),
                                                 ALU.mult, ALU.add).then_inc(norm.summed.sem, 1)
                        norm.dve_stats(dve, g, b)
                        if ahead:
                            for u in TAIL[b]:
                                unit_lo(dve, g, 4 * GB + u)
                    if b >= 1:
                        norm.dve_apply(dve, g, b - 1,
                                       lambda c: x[:, bass.ds(g * GB + (b - 1), 1), c].rearrange("p a d -> p (a d)"))

            with dve.Fori(0, NG - 1) as g:
                body(g, True)
            body(NG - 1, False)

        @block.tensor
        def _(pe):
            credit(pe, gate_ready, turned)

            def body(g, ahead):
                unit(pe, g, OUT_STAGE)
                for k in range(K):
                    p, s, q, _, names = LSTM[k]
                    if k < GB - 1:
                        unit(pe, g, OUT_STAGE + k + 1)
                    if s == 0 and ahead and k in UNITS_AT:
                        unit(pe, g, 4 * GB + UNITS_AT[k])
                    if p == 1:
                        wait(pe, conv_lo, g, OUT_STAGE + q)
                    elif s == 0:
                        wait(pe, h2_lo, g, 2 * q + 1 if p == 2 else k - 2)
                    for gate in names:
                        n = gate_number(k, gate)
                        cols = slice(GATE[gate] * D, (GATE[gate] + 1) * D)
                        out = ps[:, n % RING, 0:columns(k)]
                        out = out if p == 1 else out.rearrange("p (b w) -> p b w", b=2)
                        if n < GB:
                            wait(pe, norm.summed, g, n - GB)
                        else:
                            wait(pe, gate_tanh, g, n - RING)
                        last = products(pe, out, [wih_s[:, h, p - 1, cols] for h in range(2)],
                                        [windows(h_s[:, h], k) for h in range(2)], True, s == 0)
                        if s == 0:
                            last.then_inc(gate_ready.sem, 1)
                    if s:
                        if ahead and k in UNITS_AT:
                            unit(pe, g, 4 * GB + UNITS_AT[k])
                        wait(pe, h2_lo, g, k - 2)
                        for gate in names:
                            n = gate_number(k, gate)
                            cols = slice(GATE[gate] * D, (GATE[gate] + 1) * D)
                            products(pe, ps[:, n % RING, 0:columns(k)],
                                     [whh_s[:, h, p - 1, cols] for h in range(2)],
                                     [cell_s[:, k % 2, h, 0:columns(k)] for h in range(2)], False, True
                                     ).then_inc(gate_ready.sem, 1)
                for b in range(GB):
                    if b % 2 == 0:
                        wait(pe, h2_lo, g, K - 2 + b // 2)
                    for c in range(C):
                        cols = slice(c * P, (c + 1) * P)
                        for h in range(2):
                            last = pe.matmul(ps[:, b, cols], h_s[:, h, b, cols], ident_r[:], start=h == 0, stop=h == 1)
                    last.then_inc(turned.sem, 1)
                    if ahead:
                        for u in TAIL[b]:
                            unit(pe, g, 4 * GB + u)

            with pe.Fori(0, NG - 1) as g:
                body(g, True)
            body(NG - 1, False)


def edge_attention(nc, d, x):
    with ExitStack() as ctx:
        sb = lambda n, s, t=F32: ctx.enter_context(nc.sbuf_tensor(n, s, t))
        BH = BATCH * HEADS
        gather = sb("e_gather", [P, C, 2, EDGES], F32R)
        scatter = sb("e_scatter", [P, EC, N], F32R)
        w_s = sb("e_w_split", [P, 2, 3, D], F32R)
        a_blocks = sb("e_a_blocks", [P, HEADS])
        log_adj = sb("e_log_adj", [P, EC])
        breaks = sb("e_breaks", [BH, EDGES + 1])
        inside = sb("e_inside", [BH, EDGES])
        ident = sb("e_ident", [P, P])
        v_all = sb("e_v_all", [P, BATCH, EC, D])
        e_all = sb("e_e_all", [P, EC, BH])
        src_hot = sb("e_src_hot", [P, C, EDGES], F32R)
        dst_hot_t = sb("e_dst_hot_t", [P, EC, N])
        adj_s = sb("e_adj_split", [P, 2, C, N], F32R)
        x_s = sb("e_x_split", [P, 2, GB, C, D], F32R)
        aside = ctx.enter_context(nc.semaphore("e_aside"))
        x_hi, x_lo, z_hi = (Count(ctx.enter_context(nc.semaphore(n)), GB, aside) for n in ("e_x_hi", "e_x_lo", "e_z_hi"))
        x_rows = lambda g, n: x[:, bass.ds(g * GB + n, 1)].rearrange("p a c d -> p (a c) d")

        def x_high(act, g, n):
            act.copy(x_s[:, 0, n % GB], x_rows(g, n)).then_inc(x_hi.sem, 1)

        def x_low(pool, g, n):
            wait_apart(pool, x_hi, g, n)
            pool.tensor_tensor(x_s[:, 1, n % GB], x_rows(g, n), f(x_s[:, 0, n % GB]), ALU.subtract).then_inc(x_lo.sem, 1)

        with ExitStack() as tmp:
            tb = lambda n, s, t=F32: tmp.enter_context(nc.sbuf_tensor(n, s, t))
            sem = lambda n: tmp.enter_context(nc.semaphore(n))
            adj = tb("e_adj", [P, C, N])
            w = tb("e_w", [P, 3, D])
            a_col = tb("e_a_col", [P, 1])
            head_mask = tb("e_head_mask", [P, HEADS])
            iota = tb("e_iota", [P, N])
            node = tb("e_node", [P, C])
            ends_i = tb("e_ends_i", [P, EC, 2], I32)
            src_i = tb("e_src_i", [P, EDGES], I32)
            ends = tb("e_ends", [P, EC, 2])
            src_row = tb("e_src_row", [P, EDGES])
            key_row = tb("e_key_row", [P, EDGES])
            key_col = tb("e_key_col", [P, EC])
            ends_r = tb("e_ends_r", [P, EC, 2], F32R)
            less = tb("e_less", [P, EC, EDGES])
            rank = tb("e_rank", [P, EC])
            order = tb("e_order", [P, EC, EDGES], F32R)
            wide = tb("e_wide", [P, EC, 2, P], F32R)
            row = tb("e_row", [P, 2, EDGES])
            col = tb("e_col", [P, EC, 2])
            new = tb("e_new", [BH, EDGES])
            ps = tmp.enter_context(nc.psum_tensor("e_ps", [P, 2, N], F32))
            adj_in, ends_in, small_in, pe_done, step, adj_hi = (sem("e_adj_in"), sem("e_ends_in"), sem("e_small_in"),
                                                                sem("e_pe_done"), sem("e_step"), sem("e_adj_hi"))
            block = tmp.enter_context(nc.Block())

            @block.sync
            def _(sp):
                sp.dma_start(src_i[:], d["src"].rearrange("(a e) -> a e", a=1).to_broadcast([P, EDGES])).then_inc(ends_in, 16)
                sp.dma_start(ends_i[:], d["edge_ends"]).then_inc(ends_in, 16)
                sp.dma_start(iota[:], d["iota"]).then_inc(ends_in, 16)
                sp.dma_start(node[:], d["node"]).then_inc(ends_in, 16)
                sp.dma_start(ident[:], d["ident"]).then_inc(ends_in, 16)
                sp.dma_start(head_mask[:], d["head_mask"]).then_inc(small_in, 16)
                sp.dma_start(a_col[:], d["a"]).then_inc(small_in, 16)
                for i, name in enumerate(("W_linT", "W_valT", "W_outT")):
                    sp.dma_start(w[:, i], d[name]).then_inc(small_in, 16)
                sp.dma_start(adj[:], d["adj"].rearrange("(c p) m -> p c m", p=P)).then_inc(adj_in, 16)

            @block.scalar
            def _(act):
                credit(act, x_hi)
                for b in range(GB):
                    x_high(act, 0, b)
                act.wait_ge(adj_in, 16)
                act.copy(adj_s[:, 0], adj[:]).then_inc(adj_hi, 1)

            @block.gpsimd
            def _(pool):
                credit(pool, x_lo)
                pool.memset(breaks[:], BIG)
                pool.memset(inside[:, 0:1], 0.0)
                for b in range(GB):
                    x_low(pool, 0, b)
                pool.wait_ge(adj_hi, 1)
                pool.tensor_tensor(adj_s[:, 1], adj[:], f(adj_s[:, 0]), ALU.subtract)

            @block.vector
            def _(dve):
                def then(ins, n):
                    ins.then_inc(step, 1)
                    dve.wait_ge(step, n)

                dve.wait_ge(ends_in, 5 * 16)
                dve.tensor_copy(ends[:], ends_i[:])
                then(dve.tensor_copy(src_row[:], src_i[:]), 1)
                dve.tensor_copy(ends_r[:], ends[:])
                dve.scalar_tensor_tensor(key_row[:], src_row[:], float(EDGES), iota[:, 0:EDGES], ALU.mult, ALU.add)
                then(dve.scalar_tensor_tensor(key_col[:], ends[:, :, 0], float(EDGES), node[:, 0:EC],
                                              ALU.mult, ALU.add), 2)
                for c in range(EC):
                    last = dve.tensor_scalar(less[:, c], key_row[:], key_col[:, c:c + 1], None, ALU.is_lt)
                then(last, 3)
                then(dve.tensor_reduce(rank[:], less[:], AX.X, ALU.add), 4)
                for c in range(EC):
                    dve.tensor_scalar(order[:, c], iota[:, 0:EDGES], rank[:, c:c + 1], None, ALU.is_equal)
                for c in range(EC):
                    for i in range(2):
                        last = dve.tensor_scalar(wide[:, c, i], ident[:], 0.0, ends[:, c, i:i + 1], ALU.mult, ALU.add)
                last.then_inc(step, 1)
                dve.wait_ge(small_in, 5 * 16)
                dve.tensor_scalar(a_blocks[:], head_mask[:], a_col[:], None, ALU.mult)
                dve.tensor_copy(w_s[:, 0], w[:]).then_inc(step, 1)
                dve.wait_ge(pe_done, 2)
                dve.tensor_copy(row[:], ps[:, 0].rearrange("p (i e) -> p i e", i=2))
                then(dve.tensor_copy(col[:], ps[:, 1, 0:2 * EC].rearrange("p (c i) -> p c i", c=EC)), 7)
                for c in range(C):
                    dve.tensor_scalar(gather[:, c, 1], row[:, 1], node[:, c:c + 1], None, ALU.is_equal)
                    last = dve.tensor_scalar(src_hot[:, c], row[:, 0], node[:, c:c + 1], None, ALU.is_equal)
                then(last, 8)
                dve.tensor_tensor(gather[:, :, 0], f(src_hot[:]), f(gather[:, :, 1]), ALU.add)
                for c in range(EC):
                    dve.tensor_scalar(dst_hot_t[:, c], iota[:], col[:, c, 1:2], None, ALU.is_equal)
                    dve.tensor_scalar(scatter[:, c], iota[:], col[:, c, 0:1], None, ALU.is_equal)
                dve.tensor_tensor(w_s[:, 1], w[:], f(w_s[:, 0]), ALU.subtract)
                then(dve.tensor_tensor(new[:, 1:EDGES], row[0:BH, 0, 1:EDGES], row[0:BH, 0, 0:EDGES - 1],
                                       ALU.not_equal), 9)
                dve.tensor_scalar(inside[:, 1:EDGES], new[:, 1:EDGES], -1.0, 1.0, ALU.mult, ALU.add)
                dve.wait_ge(x_lo.sem, GB + 1)
                dve.tensor_scalar(breaks[:, 1:EDGES], new[:, 1:EDGES], BIG, None, ALU.mult)

            @block.tensor
            def _(pe):
                pe.wait_ge(step, 5)
                for i in range(2):
                    for c in range(EC):
                        last = pe.matmul(ps[:, 0, i * EDGES:(i + 1) * EDGES], wide[:, c, i], order[:, c],
                                         start=c == 0, stop=c == EC - 1)
                last.then_inc(pe_done, 1)
                for r in range(EC):
                    for c in range(EC):
                        last = pe.matmul(ps[:, 1, 2 * r:2 * r + 2], order[:, c, r * P:(r + 1) * P], ends_r[:, c],
                                         start=c == 0, stop=c == EC - 1)
                last.then_inc(pe_done, 1)

        with ExitStack() as tmp:
            tb = lambda n, s, t=F32: tmp.enter_context(nc.sbuf_tensor(n, s, t))
            count = lambda n: Count(tmp.enter_context(nc.semaphore(n)), GB, aside)
            picked = tb("e_picked", [P, EC, N])
            a0 = tb("e_a0", [P, EC])
            z_s = tb("e_z_split", [P, 2, 2, 2 * EDGES], F32R)
            q_sum = tb("e_q_sum", [P, 2, EDGES])
            lrelu = tb("e_lrelu", [P, 2, EDGES])
            ps = tmp.enter_context(nc.psum_tensor("e_banks", [P, 8, N], F32))
            z_ready, z_lo, q_ready, q_copied, lrelu_done, v_ready, v_copied, e_ready, e_done = (
                count("e_" + n) for n in ("z_ready", "z_lo", "q_ready", "q_copied",
                                          "lrelu_done", "v_ready", "v_copied", "e_ready", "e_done"))
            adj_rows, step = (tmp.enter_context(nc.semaphore(n)) for n in ("e_adj_rows", "e_pick_step"))
            block = tmp.enter_context(nc.Block())
            Z, Q, V, E = 0, 2, 4, 6

            @block.gpsimd
            def _(pool):
                with pool.Fori(0, NG - 1) as g:
                    for b in range(GB):
                        x_low(pool, g, GB + b)

            @block.scalar
            def _(act):
                credit(act, z_hi, q_copied, v_copied)

                def z_high(g, n):
                    wait(act, z_ready, g, n)
                    wait(act, v_ready, g, n - 2)
                    act.copy(z_s[:, n % 2, 0], ps[:, Z + n % 2]).then_inc(z_hi.sem, 1)

                def copies(g, n):
                    wait(act, q_ready, g, n)
                    wait(act, lrelu_done, g, n - 2)
                    act.copy(q_sum[:, n % 2], ps[:, Q + n % 2, 0:EDGES]).then_inc(q_copied.sem, 1)
                    wait(act, v_ready, g, n)
                    act.copy(v_all[:, bass.ds(g * GB + n, 1)].rearrange("p a c d -> p (a c d)"),
                             ps[:, V + n % 2, 0:EC * D]).then_inc(v_copied.sem, 1)

                def body(g, first, final):
                    for b in range(GB):
                        z_high(g, b)
                        if not final:
                            x_high(act, g, GB + b)
                        if b or not first:
                            copies(g, b - 1)
                body(0, True, False)
                with act.Fori(1, NG - 1) as g:
                    body(g, False, False)
                body(NG - 1, False, True)
                copies(NG - 1, GB - 1)
                act.wait_ge(step, 3)
                act.activation(log_adj[:], a0[:], ACT.Ln)

            @block.vector
            def _(dve):
                credit(dve, z_lo, lrelu_done, e_done)
                dve.wait_ge(adj_rows, 1)
                dve.tensor_tensor(picked[:], ps[:, Q:Q + 2], dst_hot_t[:], ALU.mult).then_inc(step, 1)
                dve.wait_ge(step, 1)
                dve.tensor_reduce(a0[:], picked[:], AX.X, ALU.add).then_inc(step, 1)
                dve.wait_ge(step, 2)
                dve.tensor_scalar(a0[:], a0[:], 1e-8, None, ALU.add).then_inc(step, 1)

                def z_low(g, n):
                    wait(dve, z_hi, g, n)
                    dve.tensor_tensor(z_s[:, n % 2, 1], ps[:, Z + n % 2], f(z_s[:, n % 2, 0]),
                                      ALU.subtract).then_inc(z_lo.sem, 1)

                def leaky(g, n):
                    wait(dve, q_copied, g, n)
                    wait(dve, e_ready, g, n - 2)
                    dve.scalar_tensor_tensor(lrelu[:, n % 2], q_sum[:, n % 2], 0.2, ps[:, Q + n % 2, 0:EDGES],
                                             ALU.mult, ALU.max).then_inc(lrelu_done.sem, 1)

                def logits(g, n):
                    wait(dve, e_ready, g, n)
                    dve.tensor_copy(e_all[:, :, bass.ds((g * GB + n) * HEADS, HEADS)],
                                    ps[:, E + n % 2, 0:EC * HEADS].rearrange("p (c h) -> p c h", c=EC)
                                    ).then_inc(e_done.sem, 1)
                staggered(dve, ((0, z_low), (1, leaky), (2, logits)))

            @block.tensor
            def _(pe):
                credit(pe, z_ready, q_ready, v_ready, e_ready)
                for r in range(EC):
                    for c in range(C):
                        for h in range(2):
                            last = pe.matmul(ps[:, Q + r], src_hot[:, c, r * P:(r + 1) * P], adj_s[:, h, c],
                                             start=c + h == 0, stop=(c, h) == (C - 1, 1))
                last.then_inc(adj_rows, 1)

                def gathers(g, n):
                    wait(pe, x_lo, g, n)
                    wait(pe, z_lo, g, n - 2)
                    for c in range(C):
                        for h in range(2):
                            last = pe.matmul(ps[:, Z + n % 2], x_s[:, h, n % GB, c],
                                             gather[:, c].rearrange("p i e -> p (i e)"),
                                             start=c + h == 0, stop=(c, h) == (C - 1, 1))
                    last.then_inc(z_ready.sem, 1)

                def images(g, n):
                    wait(pe, z_lo, g, n)
                    wait(pe, lrelu_done, g, n - 2)
                    products(pe, ps[:, Q + n % 2, 0:EDGES], [w_s[:, h, 0] for h in range(2)],
                             [z_s[:, n % 2, h, 0:EDGES] for h in range(2)]).then_inc(q_ready.sem, 1)
                    wait(pe, v_copied, g, n - 2)
                    for c in range(EC):
                        last = products(pe, ps[:, V + n % 2, c * D:(c + 1) * D],
                                        [z_s[:, n % 2, h, EDGES + c * P:EDGES + (c + 1) * P] for h in range(2)],
                                        [w_s[:, h, 1] for h in range(2)])
                    last.then_inc(v_ready.sem, 1)

                def weigh(g, n):
                    wait(pe, lrelu_done, g, n)
                    wait(pe, e_done, g, n - 2)
                    for c in range(EC):
                        last = pe.matmul(ps[:, E + n % 2, c * HEADS:(c + 1) * HEADS],
                                         lrelu[:, n % 2, c * P:(c + 1) * P], a_blocks[:], start=True, stop=True)
                    last.then_inc(e_ready.sem, 1)
                staggered(pe, ((0, gathers), (1, images), (2, weigh)))

        with ExitStack() as tmp:
            tb = lambda n, s: tmp.enter_context(nc.sbuf_tensor(n, s, F32))
            sem = lambda n: tmp.enter_context(nc.semaphore(n))
            e_t, run, top, shifted, ex, total, share = (tb("e_" + n, [BH, EDGES]) for n in
                                                        ("t", "run", "top", "shifted", "ex", "total", "share"))
            ps = tmp.enter_context(nc.psum_tensor("e_turn", [P, 2, N], F32))
            logged, turned, step, ex_done, back = (sem("e_logged"), sem("e_turned"), sem("e_sstep"), sem("e_ex_done"),
                                                   sem("e_back"))
            block = tmp.enter_context(nc.Block())
            flip = lambda t, a, b: t[:, a:b][:, ::-1]

            @block.tensor
            def _(pe):
                pe.wait_ge(logged, 1)
                for c in range(EC):
                    last = pe.transpose(ps[0:BH, 0, c * P:(c + 1) * P], e_all[:, c], ident[:])
                last.then_inc(turned, 1)
                pe.wait_ge(step, 8)
                for c in range(EC):
                    last = pe.transpose(ps[:, 1, c * BH:(c + 1) * BH], share[:, c * P:(c + 1) * P], ident[0:BH, 0:BH])
                last.then_inc(back, 1)

            @block.scalar
            def _(act):
                act.wait_ge(step, 4)
                act.activation(ex[:], shifted[:], ACT.Exp).then_inc(ex_done, 1)

            @block.vector
            def _(dve):
                def then(ins, n):
                    ins.then_inc(step, 1)
                    dve.wait_ge(step, n)

                for c in range(EC):
                    last = dve.tensor_scalar(e_all[:, c], e_all[:, c], log_adj[:, c:c + 1], None, ALU.add)
                last.then_inc(logged, 1)
                dve.wait_ge(turned, 1)
                then(dve.tensor_copy(e_t[:], ps[0:BH, 0, 0:EDGES]), 1)
                then(dve.tensor_tensor_scan(run[:], breaks[:, 0:EDGES], e_t[:], BIG, ALU.add, ALU.max), 2)
                then(dve.tensor_tensor_scan(flip(top, 0, EDGES), flip(breaks, 1, EDGES + 1), flip(run, 0, EDGES), BIG,
                                            ALU.add, ALU.max), 3)
                dve.tensor_tensor(shifted[:], e_t[:], top[:], ALU.subtract).then_inc(step, 1)
                dve.wait_ge(ex_done, 1)
                then(dve.tensor_tensor_scan(run[:], inside[:], ex[:], 0.0, ALU.mult, ALU.add), 5)
                then(dve.tensor_tensor_scan(flip(total, 0, EDGES), flip(breaks, 1, EDGES + 1), flip(run, 0, EDGES), BIG,
                                            ALU.add, ALU.max), 6)
                then(dve.reciprocal(total[:], total[:]), 7)
                dve.tensor_tensor(share[:], ex[:], total[:], ALU.mult).then_inc(step, 1)
                dve.wait_ge(back, 1)
                dve.tensor_copy(e_all[:], ps[:, 1, 0:EC * BH].rearrange("p (c n) -> p c n", c=EC))

        with ExitStack() as tmp:
            tb = lambda n, s, t=F32: tmp.enter_context(nc.sbuf_tensor(n, s, t))
            aside = tmp.enter_context(nc.semaphore("y_aside"))
            count = lambda n: Count(tmp.enter_context(nc.semaphore(n)), GB, aside)
            av = tb("y_av", [P, 2, EC, D])
            av_s = tb("y_av_split", [P, 2, 2, EC, D], F32R)
            y_s = tb("y_y_split", [P, 2, 2, N], F32R)
            norm = Norm(nc, tmp, "ln2", GB, aside)
            ps = tmp.enter_context(nc.psum_tensor("y_banks", [P, 4, N], F32))
            av_done, av_hi, av_lo, y_ready, y_hi, y_lo, o_ready = (
                count("y_" + n) for n in ("av_done", "av_hi", "av_lo", "y_ready", "y_hi", "y_lo", "o_ready"))
            block = tmp.enter_context(nc.Block())

            rows = lambda g, n: x[:, bass.ds(g * GB + n, 1)]

            @block.gpsimd
            def _(pool):
                credit(pool, av_done)
                norm.start_pool(pool)

                def weighted(g, n):
                    wait_apart(pool, av_lo, g, n - 2)
                    pool.tensor_tensor(
                        av[:, n % 2].rearrange("p c (h d) -> p c h d", h=HEADS),
                        v_all[:, bass.ds(g * GB + n, 1)].rearrange("p a c (h d) -> p (a c) h d", h=HEADS),
                        e_all[:, :, bass.ds((g * GB + n) * HEADS, HEADS)].unsqueeze(3)
                        .to_broadcast([P, EC, HEADS, DH]), ALU.mult).then_inc(av_done.sem, 1)

                staggered(pool, ((0, weighted), (3, lambda g, n: norm.pool_root(pool, g, n))))

            @block.scalar
            def _(act):
                credit(act, av_hi, y_hi)

                def av_high(g, n):
                    wait(act, av_done, g, n)
                    wait(act, y_ready, g, n - 2)
                    act.copy(av_s[:, n % 2, 0], av[:, n % 2]).then_inc(av_hi.sem, 1)

                def y_high(g, n):
                    wait(act, y_ready, g, n)
                    wait(act, o_ready, g, n - 2)
                    act.copy(y_s[:, n % 2, 0], ps[:, n % 2]).then_inc(y_hi.sem, 1)
                staggered(act, ((1, av_high), (2, y_high)))

            @block.vector
            def _(dve):
                credit(dve, av_lo, y_lo)
                norm.start_dve(dve)

                def av_low(g, n):
                    wait(dve, av_hi, g, n)
                    dve.tensor_tensor(av_s[:, n % 2, 1], av[:, n % 2], f(av_s[:, n % 2, 0]),
                                      ALU.subtract).then_inc(av_lo.sem, 1)

                def y_low(g, n):
                    wait(dve, y_hi, g, n)
                    dve.tensor_tensor(y_s[:, n % 2, 1], ps[:, n % 2], f(y_s[:, n % 2, 0]),
                                      ALU.subtract).then_inc(y_lo.sem, 1)

                def statistics(g, n):
                    wait(dve, o_ready, g, n)
                    wait(dve, norm.normed, g, n - 2)
                    dve.tensor_tensor(norm.sum[:, n % 2].rearrange("p c d -> p (c d)"), ps[:, 2 + n % 2],
                                      rows(g, n).rearrange("p a c d -> p (a c d)"), ALU.add).then_inc(norm.summed.sem, 1)
                    norm.dve_stats(dve, g, n)

                def apply(g, n):
                    norm.dve_apply(dve, g, n, lambda c: rows(g, n)[:, :, c].rearrange("p a d -> p (a d)"))
                staggered(dve, ((1, av_low), (2, y_low), (3, statistics), (4, apply)))

            @block.tensor
            def _(pe):
                credit(pe, y_ready, o_ready)

                def to_sources(g, n):
                    wait(pe, av_lo, g, n)
                    wait(pe, y_lo, g, n - 2)
                    for c in range(EC):
                        for h in range(2):
                            last = pe.matmul(ps[:, n % 2], av_s[:, n % 2, h, c], scatter[:, c],
                                             start=c + h == 0, stop=(c, h) == (EC - 1, 1))
                    last.then_inc(y_ready.sem, 1)

                def output(g, n):
                    wait(pe, y_lo, g, n)
                    wait(pe, norm.summed, g, n - 2)
                    for c in range(C):
                        cols = slice(c * P, (c + 1) * P)
                        last = products(pe, ps[:, 2 + n % 2, cols], [y_s[:, n % 2, h, cols] for h in range(2)],
                                        [w_s[:, h, 2] for h in range(2)])
                    last.then_inc(o_ready.sem, 1)
                staggered(pe, ((1, to_sources), (2, output)))


BODY = 2
TILES = HEADS * C
BT = BODY * TILES
BHD = BODY * HEADS
SPLIT = (True, False, True, False)


def is_split(t):
    return SPLIT[t // C % HEADS]


def evac_engine(t):
    return "dve" if is_split(t) or t % 2 else "act"


def number(t, test):
    per = sum(map(test, range(BT)))
    return (t // BT) * per + sum(map(test, range(t % BT)))


def evac_number(t, who):
    return number(t, lambda u: evac_engine(u) == who)


def self_attention(nc, d, x, out):
    with ExitStack() as ctx:
        sb = lambda n, s, t=F32: ctx.enter_context(nc.sbuf_tensor(n, s, t))
        sem = lambda n: ctx.enter_context(nc.semaphore(n))
        mask = sb("t_mask", [P, C, N])
        w_s = sb("t_w_split", [P, 2, 3 * D], F32R)
        ident = sb("t_ident", [P, P])
        eps = sb("t_eps", [P, C])
        with ExitStack() as tmp:
            w = tmp.enter_context(nc.sbuf_tensor("t_w", [P, 3 * D], F32))
            loaded = tmp.enter_context(nc.semaphore("t_loaded"))
            step = tmp.enter_context(nc.semaphore("t_step"))
            block = tmp.enter_context(nc.Block())

            @block.sync
            def _(sp):
                sp.dma_start(mask[:], d["adj"].rearrange("(c p) m -> p c m", p=P)).then_inc(loaded, 16)
                sp.dma_start(w[:], d["W_qkv"]).then_inc(loaded, 16)
                sp.dma_start(ident[:], d["ident"]).then_inc(loaded, 16)

            @block.vector
            def _(dve):
                dve.wait_ge(loaded, 48)
                dve.tensor_scalar(w[:, 0:D], w[:, 0:D], -float(DH) ** -0.5, None, ALU.mult)
                dve.tensor_scalar(mask[:], mask[:], 0.0, -BIG, ALU.is_equal, ALU.mult).then_inc(step, 1)
                dve.wait_ge(step, 1)
                dve.tensor_copy(w_s[:, 0], w[:])
                dve.tensor_reduce(eps[:], mask[:], AX.X, ALU.min).then_inc(step, 1)
                dve.wait_ge(step, 2)
                dve.tensor_tensor(w_s[:, 1], w[:], f(w_s[:, 0]), ALU.subtract)
                dve.tensor_scalar(eps[:], eps[:], -BIG, 0.0, ALU.mult, ALU.mult).then_inc(step, 1)
                dve.wait_ge(step, 3)
                dve.tensor_scalar(eps[:], eps[:], EPS, None, ALU.add)

        aside = sem("t_aside")
        count = lambda n, per: Count(sem("t_" + n), per, aside)
        x_s = sb("t_x_split", [P, BODY, 2, C, D], F32R)
        xt_s = sb("t_xt_split", [P, 2, N], F32R)
        qk = sb("t_qk", [P, 4, N], F32R)
        stack = sb("t_stack", [96, BODY, HEADS, 2, N], F32R)
        v_s = sb("t_v_split", [P, BODY, C, HEADS, 2 * DH], F32R)
        v_w = sb("t_v_whole", [P, BODY, C, HEADS, DH])
        masked = sb("t_masked", [P, 4, N])
        low = sb("t_low", [P, 4, 1])
        prob = sb("t_prob", [P, 4, N])
        total = sb("t_total", [P, BODY, HEADS, C])
        recip = sb("t_recip", [P, BODY, HEADS, C])
        pt_s = sb("t_pt_split", [P, 2, C, N], F32R)
        pt_w = sb("t_pt_whole", [P, C, N])
        o_t = sb("t_o_t", [2 * DH, 2, N])
        o_hi = sb("t_o_hi", [P, BODY, C, D])
        o_lo = sb("t_o_lo", [P, BODY, C, D])
        norm = Norm(nc, ctx, "ln3", BODY, aside, eps)
        ps = ctx.enter_context(nc.psum_tensor("t_banks", [P, 8, N], F32))
        S, T, O, M = 0, 2, 4, 6

        x_hi, x_lo, xt_ready, xt_hi, xt_lo = (count(n, BODY) for n in ("x_hi", "x_lo", "xt_ready", "xt_hi", "xt_lo"))
        qkv_ready, qkv_hi, qkv_lo = (count(n, 3 * BODY) for n in ("qkv_ready", "qkv_hi", "qkv_lo"))
        stacked = [count(f"stacked{j}", 16 * 3 * HEADS) for j in range(BODY)]
        s_ready, masked_done, exp_done, t_ready = (count(n, BT) for n in (
            "s_ready", "masked_done", "exp_done", "t_ready"))
        pt_hi = count("pt_hi", number(BT, is_split))
        evac = {w: count("pt_" + w, sum(evac_engine(t) == w for t in range(BT))) for w in ("dve", "act")}
        o_ready, o_copied, o_turned, rec_done, o_done = (count(n, BHD) for n in (
            "o_ready", "o_copied", "o_turned", "rec_done", "o_done"))
        parts_added = count("parts_added", BODY)
        stored = sem("t_stored")
        BODIES = BATCH // BODY
        TAIL = 16

        def run(eng, prologue, slot):
            prologue()

            def body(g, first, last):
                end = BT if last else 10 ** 6
                inside = lambda n, unit=1: (n >= 0 or not first) and n * unit < end
                for t in range(BT + (TAIL if last else 0)):
                    slot(g, t, inside)
            body(0, True, False)
            with eng.Fori(1, BODIES - 1) as g:
                body(g, False, False)
            body(BODIES - 1, False, True)

        def wait_evac(eng, g, t):
            who = evac_engine(t)
            wait(eng, evac[who], g, evac_number(t, who))

        def batch_of(g, n):
            return x[:, bass.ds(g * BODY + n, 1)] if not isinstance(g, int) else x[:, g * BODY + n:g * BODY + n + 1]

        def stack_count(n):
            return 16 * 3 * HEADS * (n // BODY + 1) - 1

        block = ctx.enter_context(nc.Block())

        @block.sync
        def _(sp):
            def restack(g, n):
                j = n % BODY
                wait_apart(sp, qkv_lo, g, 3 * n + 1)
                wait_apart(sp, s_ready, g, TILES * (n - BODY + 1) - 1)
                for h in range(HEADS):
                    rows = slice(h * DH, (h + 1) * DH)
                    for r, pick in enumerate((slice(0, 3, 2), slice(0, 4, 3), slice(1, 3))):
                        sp.dma_start(f(stack[r * DH:(r + 1) * DH, j, h]), f(qk[rows, pick])).then_inc(stacked[j].sem, 16)

            def start():
                credit(sp, *stacked)
                restack(0, 0)

            def slot(g, t, inside):
                if t % TILES == 6 and inside(t // TILES + 1, TILES):
                    restack(g, t // TILES + 1)
                if t % TILES == 15 and inside((t - 31) // TILES, TILES):
                    n = (t - 31) // TILES
                    wait_apart(sp, norm.normed, g, n)
                    dst = out[bass.ds(g * BODY + n, 1)] if not isinstance(g, int) else out[g * BODY + n:g * BODY + n + 1]
                    sp.dma_start(dst.rearrange("a (c p) d -> p (a c) d", p=P),
                                 batch_of(g, n).rearrange("p a c d -> p (a c) d")).then_inc(stored, 16)
            run(sp, start, slot)
            sp.wait_ge(stored, 16 * BATCH)

        @block.gpsimd
        def _(pool):
            def split(g, n):
                j, src = n % BODY, batch_of(g, n).rearrange("p a c d -> p (a c) d")
                wait_apart(pool, xt_hi, g, n - BODY)
                pool.tensor_copy(x_s[:, j, 0], src).then_inc(x_hi.sem, 1)
                wait_apart(pool, x_hi, g, n)
                pool.tensor_tensor(x_s[:, j, 1], src, f(x_s[:, j, 0]), ALU.subtract).then_inc(x_lo.sem, 1)

            def start():
                credit(pool, x_hi, x_lo, parts_added, norm.summed)
                norm.start_pool(pool)
                split(0, 0)
                split(0, 1)

            def slot(g, t, inside):
                if t % TILES == 8 and inside(t // TILES + 2, TILES):
                    split(g, t // TILES + 2)
                if t % TILES == 8 and inside((t - 24) // TILES, TILES):
                    n = (t - 24) // TILES
                    j = n % BODY
                    wait_apart(pool, o_done, g, HEADS * (n + 1) - 1)
                    for h in range(HEADS):
                        if SPLIT[h]:
                            cols = slice(h * DH, (h + 1) * DH)
                            last = pool.tensor_tensor(o_hi[:, j, :, cols], o_hi[:, j, :, cols], o_lo[:, j, :, cols], ALU.add)
                    last.then_inc(parts_added.sem, 1)
                    wait_apart(pool, norm.normed, g, n - 2)
                    wait_apart(pool, parts_added, g, n)
                    pool.tensor_tensor(norm.sum[:, j], batch_of(g, n).rearrange("p a c d -> p (a c) d"), o_hi[:, j],
                                       ALU.add).then_inc(norm.summed.sem, 1)
                    norm.pool_root(pool, g, n)
            run(pool, start, slot)

        @block.scalar
        def _(act):
            def exponent(g, t):
                wait(act, masked_done, g, t)
                wait(act, t_ready, g, t - 4)
                j, h, c = t // TILES % BODY, t // C % HEADS, t % C
                if c == 0:
                    wait(act, rec_done, g, t // C - BHD)
                act.activation(prob[:, t % 4], masked[:, t % 4], ACT.Exp, bias=low[:, t % 4], scale=-1.0,
                               accum_out=total[:, j, h, c:c + 1]).then_inc(exp_done.sem, 1)

            def turned_x(g, n):
                wait(act, xt_ready, g, n)
                wait(act, qkv_ready, g, 3 * n - 1)
                act.copy(xt_s[:, 0], ps[:, M]).then_inc(xt_hi.sem, 1)

            def q_k_high(g, n):
                wait(act, stacked[(n - 1) % BODY], g, stack_count(n - 1))
                for i in range(2):
                    wait(act, qkv_ready, g, 3 * n + i)
                    act.copy(qk[:, 2 * i], ps[:, M + i]).then_inc(qkv_hi.sem, 1)

            def v_high(g, n):
                j = n % BODY
                wait(act, qkv_ready, g, 3 * n + 2)
                wait(act, o_ready, g, HEADS * (n - 1) - 1)
                bank = ps[:, M].rearrange("p (c h d) -> p c h d", c=C, h=HEADS)
                act.copy(v_w[:, j], bank)
                act.copy(v_s[:, j, :, :, 0:DH], bank).then_inc(qkv_hi.sem, 1)

            def start():
                credit(act, exp_done, xt_hi, qkv_hi, pt_hi, evac["act"], o_copied)
                turned_x(0, 0)
                q_k_high(0, 0)
                v_high(0, 0)
                exponent(0, 0)

            def slot(g, t, inside):
                if inside(t + 1):
                    exponent(g, t + 1)
                if inside(t):
                    c = t % C
                    cols = slice(c * P, (c + 1) * P)
                    bank = ps[:, T + t % 2].rearrange("p (c i) -> p c i", c=C)
                    if is_split(t):
                        wait(act, t_ready, g, t)
                        if c == 0:
                            wait(act, o_ready, g, t // C - 2)
                        act.copy(pt_s[:, 0, :, cols], bank).then_inc(pt_hi.sem, 1)
                    elif evac_engine(t) == "act":
                        wait(act, t_ready, g, t)
                        wait(act, o_ready, g, t // C - 2)
                        act.copy(pt_w[:, :, cols], bank).then_inc(evac["act"].sem, 1)
                if t % C == 1 and inside((t - 9) // C, C):
                    n = (t - 9) // C
                    wait(act, o_ready, g, n)
                    wait(act, o_turned, g, n - 2)
                    rows = 2 * DH if SPLIT[n % HEADS] else DH
                    act.copy(o_t[0:rows, n % 2], ps[0:rows, O + n % 2]).then_inc(o_copied.sem, 1)
                if inside(t // TILES + 1, TILES):
                    for at, what in ((2, turned_x), (4, q_k_high), (6, v_high)):
                        if t % TILES == at:
                            what(g, t // TILES + 1)
            run(act, start, slot)

        @block.vector
        def _(dve):
            def mask_scores(g, t):
                wait_apart(dve, s_ready, g, t)
                wait_apart(dve, exp_done, g, t - 4)
                dve.tensor_tensor_reduce(masked[:, t % 4], ps[:, S + t % 2], mask[:, t % C], 1.0, -BIG, ALU.add, ALU.min,
                                         low[:, t % 4]).then_inc(masked_done.sem, 1)

            def turned_x(g, n):
                wait(dve, xt_ready, g, n)
                wait(dve, qkv_ready, g, 3 * n - 1)
                dve.tensor_copy(xt_s[:, 1], ps[:, M + 1]).then_inc(xt_lo.sem, 1)

            def q_k_low(g, n):
                for i in range(2):
                    wait(dve, qkv_hi, g, 3 * n + i)
                    dve.tensor_tensor(qk[:, 2 * i + 1], ps[:, M + i], f(qk[:, 2 * i]), ALU.subtract
                                      ).then_inc(qkv_lo.sem, 1)

            def v_low(g, n):
                j = n % BODY
                wait(dve, qkv_hi, g, 3 * n + 2)
                dve.tensor_tensor(v_s[:, j, :, :, DH:], ps[:, M].rearrange("p (c h d) -> p c h d", c=C, h=HEADS),
                                  f(v_s[:, j, :, :, 0:DH]), ALU.subtract).then_inc(qkv_lo.sem, 1)

            def start():
                credit(dve, masked_done, xt_lo, qkv_lo, evac["dve"], rec_done, o_done)
                credit(dve, norm.counted, norm.averaged, norm.normed)
                turned_x(0, 0)
                q_k_low(0, 0)
                v_low(0, 0)
                mask_scores(0, 0)
                mask_scores(0, 1)

            def slot(g, t, inside):
                if inside(t + 2):
                    mask_scores(g, t + 2)
                if inside(t) and evac_engine(t) == "dve":
                    c = t % C
                    cols = slice(c * P, (c + 1) * P)
                    bank = ps[:, T + t % 2].rearrange("p (c i) -> p c i", c=C)
                    if is_split(t):
                        wait(dve, pt_hi, g, number(t, is_split))
                        dve.tensor_tensor(pt_s[:, 1, :, cols], bank, f(pt_s[:, 0, :, cols]), ALU.subtract
                                          ).then_inc(evac["dve"].sem, 1)
                    else:
                        wait(dve, t_ready, g, t)
                        wait(dve, o_ready, g, t // C - 2)
                        dve.tensor_copy(pt_w[:, :, cols], bank).then_inc(evac["dve"].sem, 1)
                if t % C == 3 and inside((t - 11) // C, C):
                    n = (t - 11) // C
                    j, h = n // HEADS % BODY, n % HEADS
                    if h == 0:
                        wait(dve, parts_added, g, n // HEADS - 2)
                        wait(dve, norm.summed, g, n // HEADS - 2)
                    wait(dve, exp_done, g, C * n + C - 1)
                    dve.reciprocal(recip[:, j, h], total[:, j, h]).then_inc(rec_done.sem, 1)
                    wait(dve, rec_done, g, n)
                    wait(dve, o_turned, g, n)
                    bank = ps[:, O + n % 2, 0:C * 2 * DH].rearrange("p (c d) -> p c d", c=C)
                    scale = recip[:, j, h].unsqueeze(2).to_broadcast([P, C, DH])
                    cols = slice(h * DH, (h + 1) * DH)
                    ins = dve.tensor_tensor(o_hi[:, j, :, cols], bank[:, :, 0:DH], scale, ALU.mult)
                    if SPLIT[h]:
                        ins = dve.tensor_tensor(o_lo[:, j, :, cols], bank[:, :, DH:], scale, ALU.mult)
                    ins.then_inc(o_done.sem, 1)
                if t % TILES == 10 and inside((t - 26) // TILES, TILES):
                    norm.dve_stats(dve, g, (t - 26) // TILES)
                if t % TILES == 14 and inside((t - 30) // TILES, TILES):
                    n = (t - 30) // TILES
                    norm.dve_apply(dve, g, n, lambda c: batch_of(g, n)[:, :, c].rearrange("p a d -> p (a d)"))
                if inside(t // TILES + 1, TILES):
                    for at, what in ((2, turned_x), (4, q_k_low), (6, v_low)):
                        if t % TILES == at:
                            what(g, t // TILES + 1)
            run(dve, start, slot)

        @block.tensor
        def _(pe):
            def scores(g, t):
                j, h, c = t // TILES % BODY, t // C % HEADS, t % C
                if t % TILES == 0:
                    wait(pe, stacked[j], g, stack_count(t // TILES))
                wait(pe, masked_done, g, t - 2)
                pe.matmul(ps[:, S + t % 2], stack[:, j, h, 0, c * P:(c + 1) * P], stack[:, j, h, 1],
                          start=True, stop=True).then_inc(s_ready.sem, 1)

            def turn_x(g, n):
                j = n % BODY
                wait(pe, x_lo, g, n)
                wait(pe, qkv_lo, g, 3 * n - 1)
                for part in range(2):
                    for c in range(C):
                        last = pe.transpose(ps[:, M + part, c * P:(c + 1) * P], f(x_s[:, j, part, c]), ident[:])
                last.then_inc(xt_ready.sem, 1)

            def q_k(g, n):
                wait(pe, xt_hi, g, n)
                wait(pe, xt_lo, g, n)
                for i in range(2):
                    products(pe, ps[:, M + i], [w_s[:, h, i * D:(i + 1) * D] for h in range(2)],
                             [xt_s[:, h] for h in range(2)]).then_inc(qkv_ready.sem, 1)

            def v(g, n):
                wait(pe, qkv_lo, g, 3 * n)
                for c in range(C):
                    cols = slice(c * P, (c + 1) * P)
                    last = products(pe, ps[:, M, cols], [xt_s[:, h, cols] for h in range(2)],
                                    [w_s[:, h, 2 * D:] for h in range(2)])
                last.then_inc(qkv_ready.sem, 1)

            def start():
                credit(pe, s_ready, xt_ready, qkv_ready, t_ready, o_ready, o_turned)
                turn_x(0, 0)
                q_k(0, 0)
                v(0, 0)
                scores(0, 0)
                scores(0, 1)

            def slot(g, t, inside):
                if inside(t + 2):
                    scores(g, t + 2)
                if inside((t - 5) // C, C):
                    n, c = (t - 5) // C, (t - 5) % C
                    j, h = n // HEADS % BODY, n % HEADS
                    if c == 0:
                        for u in range(C * n + 2, C * n + 4):
                            wait_evac(pe, g, u)
                        wait(pe, o_done, g, n - 2)
                        if h == 0:
                            wait(pe, qkv_lo, g, 3 * (n // HEADS) + 2)
                    if SPLIT[h]:
                        for part in range(2):
                            last = pe.matmul(ps[0:2 * DH, O + n % 2], v_s[:, j, c, h], pt_s[:, part, c],
                                             start=c + part == 0, stop=(c, part) == (C - 1, 1))
                    else:
                        last = pe.matmul(ps[0:DH, O + n % 2], v_w[:, j, c, h], pt_w[:, c],
                                         start=c == 0, stop=c == C - 1)
                    if c == C - 1:
                        last.then_inc(o_ready.sem, 1)
                if inside(t):
                    wait(pe, exp_done, g, t)
                    wait_evac(pe, g, t - 2)
                    for c in range(C):
                        last = pe.transpose(ps[:, T + t % 2, c * P:(c + 1) * P], prob[:, t % 4, c * P:(c + 1) * P],
                                            ident[:])
                    last.then_inc(t_ready.sem, 1)
                if t % C == 2 and inside((t - 10) // C, C):
                    n = (t - 10) // C
                    wait_apart(pe, o_copied, g, n)
                    rows = 2 * DH if SPLIT[n % HEADS] else DH
                    for c in range(C):
                        last = pe.transpose(ps[:, O + n % 2, c * 2 * DH:c * 2 * DH + rows],
                                            o_t[0:rows, n % 2, c * P:(c + 1) * P], ident[0:rows, 0:rows])
                    last.then_inc(o_turned.sem, 1)
                if inside(t // TILES + 1, TILES):
                    for at, what in ((1, turn_x), (3, q_k), (5, v)):
                        if t % TILES == at:
                            what(g, t // TILES + 1)
            run(pe, start, slot)


def build(nc, d, out):
    with ExitStack() as ctx:
        x = ctx.enter_context(nc.sbuf_tensor("x_all", [P, BATCH, C, D], F32))
        with ExitStack() as first:
            sb = lambda n, s, t=F32R: first.enter_context(nc.sbuf_tensor(n, s, t))
            keep = (sb("at_split", [P, 2, C, N]), sb("a2t_split", [P, 2, C, N]), sb("ct_split", [P, 2, C, N]),
                    sb("c2t_split", [P, 2, C, N]), sb("g_split", [P, 2, 3, 3, D]), sb("v_sum", [P, C, D], F32), x)
            diffusion_setup(nc, d, keep)
            diffusion(nc, d, keep)
        dilated(nc, d, x)
        edge_attention(nc, d, x)
        self_attention(nc, d, x, out)


def kernel(**inputs):
    import numpy as np
    import concourse.bacc as bacc
    from concourse.bass_utils import run_bass_kernel_spmd

    a = {k: np.ascontiguousarray(v) for k, v in inputs.items()}
    flip = lambda v: np.ascontiguousarray(np.swapaxes(v, -1, -2))
    cols = lambda v: np.ascontiguousarray(v.reshape(-1, P).T)
    by_input = lambda w: np.ascontiguousarray(w.transpose(2, 0, 1))
    by_gate = lambda b: np.ascontiguousarray(b.reshape(SKIPS, 4, D).transpose(2, 0, 1))
    laid = {
        "x": a["x"], "xT": flip(a["x"]), "adj": a["adj"], "adjT": flip(a["adj"]),
        "alpha": a["L0_gnn_alpha_train"], "alpha_cols": cols(a["L0_gnn_alpha_train"]), "wT": flip(a["L0_gnn_w"]), "d": a["L0_gnn_d"],
        "fc_w": a["L0_gnn_fc_in_w"], "fc_b": a["L0_gnn_fc_in_b"],
        "Wg0": a["L1_gnn_Wg0"], "bg0": a["L1_gnn_bg0"], "Wg1": a["L1_gnn_Wg1"], "bg1": a["L1_gnn_bg1"],
        "WihT": by_input(a["L1_gnn_Wih"]), "WhhT": by_input(a["L1_gnn_Whh"]),
        "bih": by_gate(a["L1_gnn_bih"]), "bhh": by_gate(a["L1_gnn_bhh"]),
        "W_linT": flip(a["L2_gnn_W_lin"]), "W_valT": flip(a["L2_gnn_W_val"]), "W_outT": flip(a["L2_gnn_W_out"]),
        "a": a["L2_gnn_a"].reshape(D, 1), "src": a["L2_gnn_src"],
        "edge_ends": np.ascontiguousarray(np.stack([cols(a["L2_gnn_src"]), cols(a["L2_gnn_dst"])], -1)),
        "iota": np.tile(np.arange(N, dtype=np.float32), (P, 1)),
        "node": cols(np.arange(N, dtype=np.float32)),
        "head_mask": np.repeat(np.eye(HEADS, dtype=np.float32), DH, axis=0),
        "W_qkv": a["L3_gnn_W"],
        "ident": np.eye(P, dtype=np.float32),
    }
    nc = bacc.Bacc("TRN2", target_bir_lowering=False, num_devices=1)
    d, arrays = {}, {}
    for name, v in laid.items():
        arrays[f"in_{name}"] = v
        d[name] = nc.dram_tensor(f"in_{name}", v.shape, mybir.dt.from_np(v.dtype), kind="ExternalInput").ap()
    out = nc.dram_tensor("out", (BATCH, N, D), F32, kind="ExternalOutput").ap()
    build(nc, d, out)
    return run_bass_kernel_spmd(nc, [arrays], core_ids=[0]).results[0]["out"]
```

```python
from contextlib import ExitStack
from math import comb

import concourse.bass as bass
from concourse import mybir

F32 = mybir.dt.float32
F32R = mybir.dt.float32r
I32 = mybir.dt.int32
ALU = mybir.AluOpType
ACT = mybir.ActivationFunctionType
AX = mybir.AxisListType

P = 128
BATCH = 16
N = 512
D = 128
C = N // P
GB = 4
NG = BATCH // GB
STEPS = 8
DT = 1.0 / STEPS
EPS = 1e-5
SKIPS = 4
EDGES = 256
EC = EDGES // P
HEADS = 4
DH = D // HEADS
BIG = -3.0e38


class Count:

    def __init__(self, sem, per, aside=None):
        self.sem, self.per, self.aside = sem, per, aside

    def at(self, g, n):
        return g * self.per + (self.per + n + 1)


def credit(eng, *counts):
    for c in counts:
        eng.sem_inc(c.sem, c.per)


def wait(eng, c, g, n):
    eng.wait_ge(c.sem, c.at(g, n))


def wait_apart(eng, c, g, n):
    eng.wait_ge(c.sem, c.at(g, n))
    eng.sem_inc(c.aside, 1)


def staggered(eng, stages):
    def slots(g, ts, first, final):
        for t in ts:
            for lag, do in stages:
                if not (first and t < lag) and not (final and t - lag >= GB):
                    do(g, t - lag)

    slots(0, range(GB), True, False)
    with eng.Fori(1, NG) as g:
        slots(g, range(GB), False, False)
    slots(NG - 1, range(GB, GB + max(lag for lag, _ in stages)), False, True)


def f(ap):
    return ap.bitcast(F32)


def products(pe, out, lhs, rhs, start=True, stop=True):
    pe.matmul(out, lhs[0], rhs[0], start=start, stop=False)
    pe.matmul(out, lhs[0], rhs[1], start=False, stop=False)
    return pe.matmul(out, lhs[1], rhs[0], start=False, stop=stop)


class Norm:

    def __init__(self, nc, ctx, name, per, aside, eps=None, slots=2):
        sb = lambda n, s: ctx.enter_context(nc.sbuf_tensor(f"{name}_{n}", s, F32))
        self.slots, self.eps = slots, eps
        self.sum = sb("sum", [P, slots, C, D])
        self.stats = sb("stats", [P, slots, C, 6])
        self.mean_var = sb("mean_var", [P, slots, C, 2])
        self.var_eps = sb("var_eps", [P, slots, C])
        self.rstd = sb("rstd", [P, slots, C])
        self.power = sb("power", [P, C])
        c = lambda n: Count(ctx.enter_context(nc.semaphore(f"{name}_{n}")), per, aside)
        self.summed, self.counted, self.averaged = c("summed"), c("counted"), c("averaged")
        self.eps_added, self.rooted, self.normed = c("eps_added"), c("rooted"), c("normed")

    def dve_stats(self, dve, g, n):
        k = n % self.slots
        wait(dve, self.summed, g, n)
        for c in range(C):
            last = dve.bn_stats(self.stats[:, k, c, :], self.sum[:, k, c, :])
        last.then_inc(self.counted.sem, 1)
        wait_apart(dve, self.counted, g, n)
        for c in range(C):
            last = dve.bn_aggr(self.mean_var[:, k, c, :], self.stats[:, k, c, :])
        last.then_inc(self.averaged.sem, 1)

    def pool_root(self, pool, g, n):
        k = n % self.slots
        wait_apart(pool, self.averaged, g, n)
        if self.eps is None:
            ins = pool.tensor_scalar(self.var_eps[:, k, :], self.mean_var[:, k, :, 1], EPS, None, ALU.add)
        else:
            ins = pool.tensor_tensor(self.var_eps[:, k, :], self.mean_var[:, k, :, 1], self.eps[:], ALU.add)
        ins.then_inc(self.eps_added.sem, 1)
        wait_apart(pool, self.eps_added, g, n)
        pool.tensor_tensor(self.rstd[:, k, :], self.var_eps[:, k, :], self.power[:],
                           ALU.pow).then_inc(self.rooted.sem, 1)

    def dve_apply(self, dve, g, n, out):
        k = n % self.slots
        wait(dve, self.rooted, g, n)
        for c in range(C):
            last = dve.tensor_scalar(out(c), self.sum[:, k, c, :], self.mean_var[:, k, c, 0:1],
                                     self.rstd[:, k, c:c + 1], ALU.subtract, ALU.mult)
        last.then_inc(self.normed.sem, 1)

    def start_dve(self, dve):
        credit(dve, self.summed, self.counted, self.averaged, self.normed)

    def start_pool(self, pool):
        credit(pool, self.eps_added, self.rooted)
        pool.memset(self.power[:], -0.5)


def diffusion_setup(nc, d, keep):
    at_s, a2t_s, ct_s, c2t_s, g_s, v_sum, x = keep
    with ExitStack() as ctx:
        sb = lambda n, s, t=F32: ctx.enter_context(nc.sbuf_tensor(n, s, t))
        sem = lambda n: ctx.enter_context(nc.semaphore(n))
        adj = sb("s_adj", [P, C, N])
        adjt = sb("s_adjt", [P, C, N])
        a_s = sb("s_a_split", [P, 2, C, N], F32R)
        pair = sb("s_pair", [P, C, N])
        al_row = sb("s_al_row", [P, N])
        al_col = sb("s_al_col", [P, C])
        be_col = sb("s_be_col", [P, C])
        wt = sb("s_wt", [P, D]); dw = sb("s_dw", [P, D]); dcol = sb("s_dcol", [P, 1])
        fcw = sb("s_fcw", [P, D]); bcol = sb("s_bcol", [P, 1]); bwide = sb("s_bwide", [P, D])
        ident = sb("s_ident", [P, P])
        wp = sb("s_wp", [P, STEPS + 1, D])
        tk = sb("s_tk", [P, STEPS + 1, D])
        ck = sb("s_ck", [P, STEPS + 1, D])
        colsum = sb("s_colsum", [P, 2, N])
        s_all = sb("s_sj", [P, C, 3, D])
        s_s = sb("s_sj_split", [P, 2, C, 2, D], F32R)
        ps_a = ctx.enter_context(nc.psum_tensor("s_ps_a", [P, 4, 512], F32))
        ps_w = ctx.enter_context(nc.psum_tensor("s_ps_w", [P, 4, 512], F32))

        act_scaled = sem("s_act_scaled")
        bias_in = sem("s_bias_in")
        adj_in, small_in, x_in = sem("s_adj_in"), sem("s_small_in"), sem("s_x_in")
        act_alpha, act_hi, dve_lo = sem("s_act_alpha"), sem("s_act_hi"), sem("s_dve_lo")
        dve_step, pe_a, pe_w, dve_w, dve_s = (sem("s_dve_step"), sem("s_pe_a"), sem("s_pe_w"),
                                              sem("s_dve_w"), sem("s_dve_s"))
        pe_t, act_a = sem("s_pe_t"), sem("s_act_a")
        block = ctx.enter_context(nc.Block())
        rows = lambda a: a.rearrange("(c p) m -> p c m", p=P)

        @block.sync
        def _(sp):
            sp.dma_start(al_row[:], d["alpha"].rearrange("(a n) -> a n", a=1).to_broadcast([P, N])).then_inc(small_in, 16)
            sp.dma_start(al_col[:], d["alpha_cols"]).then_inc(small_in, 16)
            sp.dma_start(wt[:], d["wT"]).then_inc(small_in, 16)
            sp.dma_start(dcol[:], d["d"].rearrange("(p a) -> p a", a=1)).then_inc(small_in, 16)
            sp.dma_start(ident[:], d["ident"]).then_inc(small_in, 16)
            sp.dma_start(adjt[:], rows(d["adjT"])).then_inc(adj_in, 16)
            sp.dma_start(adj[:], rows(d["adj"])).then_inc(adj_in, 16)
            sp.dma_start(fcw[:], d["fc_w"]).then_inc(bias_in, 16)
            sp.dma_start(bcol[:], d["fc_b"].rearrange("(p a) -> p a", a=1)).then_inc(bias_in, 16)
            for b in range(BATCH):
                sp.dma_start(x[:, b], rows(d["x"][b])).then_inc(x_in, 16)
            sp.wait_ge(x_in, 16 * BATCH)

        @block.scalar
        def _(act):
            act.wait_ge(small_in, 5 * 16)
            act.activation(al_row[:], al_row[:], ACT.Tanh, scale=0.5)
            act.activation(al_col[:], al_col[:], ACT.Tanh, scale=0.5).then_inc(act_alpha, 1)
            act.wait_ge(dve_step, 1)
            act.wait_ge(adj_in, 32)
            for c in range(C):
                last = act.activation(adj[:, c], adj[:, c], ACT.Copy, scale=al_col[:, c:c + 1])
            last.then_inc(act_scaled, 1)
            act.wait_ge(dve_step, 3)
            act.copy(at_s[:, 0], adjt[:]).then_inc(act_hi, 1)
            act.wait_ge(dve_step, 4)
            act.copy(a_s[:, 0], adj[:]).then_inc(act_hi, 1)
            for c in range(C):
                act.wait_ge(pe_a, c + 1)
                act.copy(a2t_s[:, 0, c], ps_a[:, c]).then_inc(act_hi, 1)
            for c in range(C):
                act.wait_ge(pe_a, C + c + 1)
                act.copy(pair[:, c], ps_a[:, c]).then_inc(act_a, 1)
                act.copy(ct_s[:, 0, c], ps_a[:, c]).then_inc(act_hi, 1)
            for c in range(C):
                act.wait_ge(pe_t, c + 1)
                act.copy(a_s[:, 0, c], ps_a[:, c]).then_inc(act_hi, 1)
            for c in range(C):
                act.wait_ge(pe_a, 2 * C + c + 1)
                act.copy(c2t_s[:, 0, c], ps_a[:, c]).then_inc(act_hi, 1)

        @block.vector
        def _(dve):
            dve.wait_ge(act_alpha, 1)
            dve.tensor_scalar(al_row[:], al_row[:], DT / 4, DT / 4, ALU.mult, ALU.add)
            dve.tensor_scalar(al_col[:], al_col[:], DT / 4, DT / 4, ALU.mult, ALU.add).then_inc(dve_step, 1)
            dve.wait_ge(dve_step, 1)
            dve.tensor_scalar(be_col[:], al_col[:], -1.0, 1.0 - DT, ALU.mult, ALU.add)
            dve.tensor_scalar(dcol[:], dcol[:], 0.0, 1.0, ALU.max, ALU.min).then_inc(dve_w, 1)
            dve.wait_ge(dve_w, 1)
            dve.tensor_scalar(dw[:], wt[:], dcol[:], None, ALU.mult)
            dve.tensor_copy(wp[:, 0], ident[:]).then_inc(dve_w, 1)
            def powers_of_w(n, lo, k):
                dve.wait_ge(pe_w, n + 1)
                dve.tensor_scalar(wp[:, lo:lo + k], ps_w[:, 0, 0:k * D].rearrange("p (k d) -> p k d", k=k),
                                  DT if n == 0 else 1.0, None, ALU.mult).then_inc(dve_w, 1)

            powers_of_w(0, 1, 1)
            powers_of_w(1, 2, 1)
            powers_of_w(2, 3, 2)
            dve.wait_ge(adj_in, 32)
            for c in range(C):
                last = dve.tensor_tensor(adjt[:, c], adjt[:, c], al_row[:], ALU.mult)
            last.then_inc(dve_step, 1)
            dve.wait_ge(dve_step, 2)
            for c in range(C):
                blk = adjt[:, c, c * P:(c + 1) * P]
                last = dve.scalar_tensor_tensor(blk, ident[:], be_col[:, c:c + 1], blk, ALU.mult, ALU.add)
            last.then_inc(dve_step, 1)
            dve.wait_ge(act_scaled, 1)
            for c in range(C):
                blk = adj[:, c, c * P:(c + 1) * P]
                last = dve.scalar_tensor_tensor(blk, ident[:], be_col[:, c:c + 1], blk, ALU.mult, ALU.add)
            last.then_inc(dve_step, 1)
            dve.wait_ge(bias_in, 32)
            dve.tensor_scalar(bwide[:], ident[:], 0.0, bcol[:], ALU.mult, ALU.add)
            powers_of_w(3, 5, 4)
            dve.wait_ge(act_hi, 1)
            dve.tensor_tensor(at_s[:, 1], adjt[:], f(at_s[:, 0]), ALU.subtract).then_inc(dve_lo, 1)
            dve.wait_ge(act_hi, 2)
            dve.tensor_tensor(a_s[:, 1], adj[:], f(a_s[:, 0]), ALU.subtract).then_inc(dve_lo, 1)
            dve.wait_ge(dve_w, 6)
            for s in range(STEPS):
                for k in range(STEPS - s):
                    if s == 0:
                        last = dve.tensor_scalar(tk[:, k], wp[:, 0], DT, None, ALU.mult)
                    else:
                        last = dve.scalar_tensor_tensor(tk[:, k], wp[:, s], DT * comb(k + s, k), tk[:, k],
                                                        ALU.mult, ALU.add)
                last.then_inc(dve_s, 1)
                dve.wait_ge(dve_s, s + 1)
            for c in range(C):
                dve.wait_ge(act_hi, 2 + c + 1)
                dve.tensor_tensor(a2t_s[:, 1, c], ps_a[:, c], f(a2t_s[:, 0, c]), ALU.subtract).then_inc(dve_lo, 1)
            dve.wait_ge(pe_w, 6)
            for q in range(STEPS + 1):
                k = STEPS - q
                src = ps_w[:, 1 + q // 4, (q % 4) * D:(q % 4 + 1) * D]
                if k == STEPS:
                    last = dve.tensor_copy(tk[:, k], src)
                else:
                    last = dve.scalar_tensor_tensor(tk[:, k], src, float(comb(STEPS, k)), tk[:, k], ALU.mult, ALU.add)
            last.then_inc(dve_w, 1)
            dve.wait_ge(dve_w, 7)
            for j in range(3):
                last = dve.tensor_copy(g_s[:, 0, :, j], tk[:, 3 * j:3 * j + 3])
            last.then_inc(dve_w, 1)
            dve.wait_ge(dve_w, 8)
            for j in range(3):
                last = dve.tensor_tensor(g_s[:, 1, :, j], tk[:, 3 * j:3 * j + 3], f(g_s[:, 0, :, j]), ALU.subtract)
            last.then_inc(dve_w, 1)
            for i, part in enumerate((at_s, a2t_s)):
                last = dve.tensor_reduce(colsum[:, i], f(part[:, 0]).rearrange("p c n -> p n c"), AX.X, ALU.add)
            last.then_inc(dve_w, 1)
            for i, part in enumerate((at_s, a2t_s)):
                for c in range(C):
                    dve.wait_ge(dve_w, 10 + i * C + c)
                    dve.tensor_tensor(colsum[:, i], colsum[:, i], f(part[:, 1, c]), ALU.add).then_inc(dve_w, 1)
            for c in range(C):
                dve.wait_ge(act_hi, 6 + c + 1)
                dve.tensor_tensor(ct_s[:, 1, c], ps_a[:, c], f(ct_s[:, 0, c]), ALU.subtract).then_inc(dve_lo, 1)
            dve.wait_ge(pe_w, 7)
            for q in range(STEPS + 1):
                k = STEPS - q
                src = ps_w[:, 1 + q // 4, (q % 4) * D:(q % 4 + 1) * D]
                last = dve.tensor_scalar(ck[:, k], src, float(comb(STEPS, k)), None, ALU.mult)
            last.then_inc(dve_w, 1)
            for c in range(C):
                dve.wait_ge(act_hi, 10 + c + 1)
                dve.tensor_tensor(a_s[:, 1, c], ps_a[:, c], f(a_s[:, 0, c]), ALU.subtract).then_inc(dve_lo, 1)
            for c in range(C):
                dve.wait_ge(pe_w, 8 + c)
                dve.tensor_tensor(s_all[:, c], ps_w[:, c, 0:3 * D].rearrange("p (j d) -> p j d", j=3),
                                  ck[:, 0:STEPS + 1:3], ALU.add).then_inc(dve_s, 1)
            dve.wait_ge(dve_s, STEPS + C)
            dve.tensor_copy(s_s[:, 0], s_all[:, :, 1:3]).then_inc(dve_s, 1)
            dve.wait_ge(dve_s, STEPS + C + 1)
            dve.tensor_tensor(s_s[:, 1], s_all[:, :, 1:3], f(s_s[:, 0]), ALU.subtract).then_inc(dve_s, 1)
            for c in range(C):
                dve.wait_ge(act_hi, 14 + c + 1)
                dve.tensor_tensor(c2t_s[:, 1, c], ps_a[:, c], f(c2t_s[:, 0, c]), ALU.subtract).then_inc(dve_lo, 1)
            for c in range(C):
                dve.wait_ge(pe_w, 12 + c)
                dve.tensor_tensor(v_sum[:, c], ps_w[:, c, 0:D], s_all[:, c, 0], ALU.add).then_inc(dve_s, 1)

        @block.tensor
        def _(pe):
            pe.wait_ge(dve_w, 2)
            pe.matmul(ps_w[:, 0, 0:D], dw[:], wt[:], start=True, stop=True).then_inc(pe_w, 1)
            pe.wait_ge(dve_w, 3)
            pe.matmul(ps_w[:, 0, 0:D], wp[:, 1], wp[:, 1], start=True, stop=True).then_inc(pe_w, 1)
            pe.wait_ge(dve_w, 4)
            pe.matmul(ps_w[:, 0, 0:2 * D], wp[:, 2], wp[:, 1:3], start=True, stop=True).then_inc(pe_w, 1)
            pe.wait_ge(dve_w, 5)
            pe.matmul(ps_w[:, 0, 0:4 * D], wp[:, 4], wp[:, 1:5], start=True, stop=True).then_inc(pe_w, 1)
            pe.wait_ge(dve_lo, 2)
            for m in range(C):
                for k in range(C):
                    last = products(pe, ps_a[:, m], [a_s[:, h, k, m * P:(m + 1) * P] for h in range(2)],
                                    [at_s[:, h, k] for h in range(2)], k == 0, k == C - 1)
                last.then_inc(pe_a, 1)
            pe.wait_ge(dve_w, 6)
            for bank, lo, k in ((1, 0, 4), (2, 4, 4), (3, 8, 1)):
                last = pe.matmul(ps_w[:, bank, 0:k * D], fcw[:], wp[:, lo:lo + k], start=True, stop=True)
            last.then_inc(pe_w, 2)
            pe.wait_ge(dve_lo, 2 + C)
            for m in range(C):
                for k in range(C):
                    last = products(pe, ps_a[:, m], [a_s[:, h, k, m * P:(m + 1) * P] for h in range(2)],
                                    [a2t_s[:, h, k] for h in range(2)], k == 0, k == C - 1)
                last.then_inc(pe_a, 1)
            pe.wait_ge(dve_w, 7)
            for bank, lo, k in ((1, 0, 4), (2, 4, 4), (3, 8, 1)):
                last = pe.matmul(ps_w[:, bank, 0:k * D], bwide[:], wp[:, lo:lo + k], start=True, stop=True)
            last.then_inc(pe_w, 1)
            pe.wait_ge(act_a, C)
            pe.wait_ge(dve_lo, 2 + 2 * C)
            for m in range(C):
                for k in range(C):
                    last = pe.transpose(ps_a[:, m, k * P:(k + 1) * P], pair[:, k, m * P:(m + 1) * P], ident[:])
                last.then_inc(pe_t, 1)
            pe.wait_ge(dve_w, 11 + 2 * C)
            for c in range(C):
                for i in range(2):
                    last = pe.matmul(ps_w[:, c, 0:3 * D], colsum[:, i, c * P:(c + 1) * P],
                                     ck[:, i + 1:STEPS + 1:3], start=i == 0, stop=i == 1)
                last.then_inc(pe_w, 1)
            pe.wait_ge(dve_lo, 2 + 3 * C)
            for m in range(C):
                for k in range(C):
                    last = products(pe, ps_a[:, m], [a_s[:, h, k, m * P:(m + 1) * P] for h in range(2)],
                                    [ct_s[:, h, k] for h in range(2)], k == 0, k == C - 1)
                last.then_inc(pe_a, 1)
            pe.wait_ge(dve_s, STEPS + C + 2)
            for j, part in ((0, ct_s), (1, c2t_s)):
                if j == 1:
                    pe.wait_ge(dve_lo, 2 + 4 * C)
                for c in range(C):
                    for k in range(C):
                        last = products(pe, ps_w[:, c, 0:D], [part[:, h, k, c * P:(c + 1) * P] for h in range(2)],
                                        [s_s[:, h, k, j] for h in range(2)], j + k == 0, (j, k) == (1, C - 1))
                    if j == 1:
                        last.then_inc(pe_w, 1)


def diffusion(nc, d, keep):
    at_s, a2t_s, ct_s, c2t_s, g_s, v_sum, x = keep
    with ExitStack() as ctx:
        sb = lambda n, s, t=F32: ctx.enter_context(nc.sbuf_tensor(n, s, t))
        count = lambda n, per: Count(ctx.enter_context(nc.semaphore(n)), per, aside)
        x_s = sb("x_split", [P, 2, GB, C, D], F32R)
        xt = sb("xt", [P, 2, N])
        base_s = sb("base_split", [P, 2, 3, 2, N], F32R)
        x_v = sb("x_plus_v", [P, GB, C, D])
        rest = sb("rest", [P, C, GB, D])
        z_s = sb("z_split", [P, 2, 2, C, GB, D], F32R)
        aside = ctx.enter_context(nc.semaphore("aside"))
        norm = Norm(nc, ctx, "ln0", C, aside)
        ps_base = ctx.enter_context(nc.psum_tensor("ps_base", [P, 2, 2, N], F32))
        ps_z = ctx.enter_context(nc.psum_tensor("ps_z", [P, 2, N], F32))
        ps_out = ctx.enter_context(nc.psum_tensor("ps_out", [P, 2, N], F32))

        xt_in = [count(f"xt_in{q}", 16 * GB // 2) for q in range(2)]
        x_hi, x_lo, xt_hi, xt_lo, xv_done = (count(n, GB) for n in ("x_hi", "x_lo", "xt_hi", "xt_lo", "xv_done"))
        base_ready, base_hi, base_lo = (count(n, 2 * GB) for n in ("base_ready", "base_hi", "base_lo"))
        z_ready, z_hi, z_lo, rest_done = (count(n, C * GB) for n in ("z_ready", "z_hi", "z_lo", "rest_done"))
        out_ready = count("out_ready", C)
        block = ctx.enter_context(nc.Block())

        @block.sync
        def _(sp):
            for q in range(2):
                credit(sp, xt_in[q])
            with sp.Fori(0, NG) as g:
                for b in range(GB):
                    wait(sp, xt_lo, g, b - 2)
                    sp.dma_start(xt[:, b % 2], d["xT"][bass.ds(g * GB + b, 1)].rearrange("a d n -> (a d) n")
                                 ).then_inc(xt_in[b % 2].sem, 16)

        @block.gpsimd
        def _(pool):
            credit(pool, x_hi, x_lo, xt_hi, xt_lo, xv_done)
            norm.start_pool(pool)
            rows = lambda g, b: x[:, bass.ds(g * GB + b, 1)].rearrange("p a c d -> p (a c) d")

            def split(g, n):
                b = n % GB
                wait_apart(pool, base_lo, g, 2 * (n - GB) + 1)
                pool.tensor_copy(x_s[:, 0, b], rows(g, n)).then_inc(x_hi.sem, 1)
                wait_apart(pool, x_hi, g, n)
                pool.tensor_tensor(x_s[:, 1, b], rows(g, n), f(x_s[:, 0, b]), ALU.subtract).then_inc(x_lo.sem, 1)

            def split_t(g, n):
                b = n % GB
                wait_apart(pool, xt_in[b % 2], g, 16 * (n // 2) + 15)
                wait_apart(pool, z_lo, g, C * (n - 2) + C - 1)
                pool.tensor_copy(base_s[:, b % 2, 0, 0], xt[:, b % 2]).then_inc(xt_hi.sem, 1)
                wait_apart(pool, xt_hi, g, n)
                pool.tensor_tensor(base_s[:, b % 2, 0, 1], xt[:, b % 2], f(base_s[:, b % 2, 0, 0]),
                                   ALU.subtract).then_inc(xt_lo.sem, 1)
                wait_apart(pool, rest_done, g, C * (n - GB) + C - 1)
                pool.tensor_tensor(x_v[:, b], rows(g, n), v_sum[:], ALU.add).then_inc(xv_done.sem, 1)

            def roots(g):
                for c in range(C):
                    norm.pool_root(pool, g, c)

            split(0, 0)
            split(0, 1)
            split_t(0, 0)
            split(0, 2)
            split_t(0, 1)
            split(0, 3)
            with pool.Fori(0, NG - 1) as g:
                for b in range(GB):
                    split(g, GB + b)
                    split_t(g, 2 + b)
                roots(g)
            split_t(NG - 1, 2)
            split_t(NG - 1, 3)
            roots(NG - 1)

        @block.scalar
        def _(act):
            credit(act, base_hi, z_hi)
            with act.Fori(0, NG) as g:
                def base(b):
                    for i in range(2):
                        wait(act, base_ready, g, 2 * b + i)
                        wait(act, z_lo, g, C * (b - 2) + C - 1)
                        act.copy(base_s[:, b % 2, i + 1, 0], ps_base[:, b % 2, i]).then_inc(base_hi.sem, 1)
                base(0)
                for b in range(GB):
                    if b + 1 < GB:
                        base(b + 1)
                    if b == 0:
                        wait(act, out_ready, g, -1)
                    for c in range(C):
                        wait(act, z_ready, g, C * b + c)
                        act.copy(z_s[:, :, 0, c, b], ps_z[:, c % 2, D:3 * D].rearrange("p (j d) -> p j d", j=2)
                                 ).then_inc(z_hi.sem, 1)

        @block.vector
        def _(dve):
            credit(dve, base_lo, z_lo, rest_done)
            norm.start_dve(dve)
            with dve.Fori(0, NG) as g:
                def base(b):
                    for i in range(2):
                        wait(dve, base_hi, g, 2 * b + i)
                        dve.tensor_tensor(base_s[:, b % 2, i + 1, 1], ps_base[:, b % 2, i],
                                          f(base_s[:, b % 2, i + 1, 0]), ALU.subtract).then_inc(base_lo.sem, 1)
                base(0)
                for b in range(GB):
                    if b + 1 < GB:
                        base(b + 1)
                    wait(dve, xv_done, g, b)
                    for c in range(C):
                        wait(dve, z_hi, g, C * b + c)
                        dve.tensor_tensor(rest[:, c, b], ps_z[:, c % 2, 0:D], x_v[:, b, c],
                                          ALU.add).then_inc(rest_done.sem, 1)
                        dve.tensor_tensor(z_s[:, :, 1, c, b], ps_z[:, c % 2, D:3 * D].rearrange("p (j d) -> p j d", j=2),
                                          f(z_s[:, :, 0, c, b]), ALU.subtract).then_inc(z_lo.sem, 1)
                for c in range(C):
                    wait(dve, out_ready, g, c)
                    wait(dve, norm.normed, g, c - 2)
                    wait(dve, rest_done, g, C * GB - 1)
                    dve.tensor_tensor(norm.sum[:, c % 2], ps_out[:, c % 2].rearrange("p (b d) -> p b d", b=GB),
                                      rest[:, c], ALU.add).then_inc(norm.summed.sem, 1)
                    norm.dve_stats(dve, g, c)
                    norm.dve_apply(dve, g, c, lambda b: x[:, bass.ds(g * GB + b, 1), c].rearrange("p a d -> p (a d)"))

        @block.tensor
        def _(pe):
            credit(pe, base_ready, z_ready, out_ready)
            with pe.Fori(0, NG) as g:
                def base(b):
                    wait(pe, x_lo, g, b)
                    for i, m in enumerate((at_s, a2t_s)):
                        wait(pe, base_lo, g, 2 * (b - 2) + i)
                        for c in range(C):
                            last = products(pe, ps_base[:, b % 2, i], [x_s[:, h, b, c] for h in range(2)],
                                            [m[:, h, c] for h in range(2)], c == 0, c == C - 1)
                        last.then_inc(base_ready.sem, 1)
                base(0)
                for b in range(GB):
                    if b + 1 < GB:
                        base(b + 1)
                    wait(pe, xt_lo, g, b)
                    wait(pe, base_lo, g, 2 * b + 1)
                    for c in range(C):
                        wait(pe, z_lo, g, C * b + c - 2)
                        for i in range(3):
                            last = products(pe, ps_z[:, c % 2, 0:3 * D],
                                            [base_s[:, b % 2, i, h, c * P:(c + 1) * P] for h in range(2)],
                                            [g_s[:, h, i] for h in range(2)], i == 0, i == 2)
                        last.then_inc(z_ready.sem, 1)
                wait(pe, z_lo, g, C * GB - 1)
                for c in range(C):
                    wait(pe, norm.summed, g, c - 2)
                    for j, m in enumerate((ct_s, c2t_s)):
                        for k in range(C):
                            last = products(pe, ps_out[:, c % 2], [m[:, h, k, c * P:(c + 1) * P] for h in range(2)],
                                            [z_s[:, j, h, k] for h in range(2)], j + k == 0, (j, k) == (1, C - 1))
                    last.then_inc(out_ready.sem, 1)


def lstm_steps():
    steps = [(1, 0, b, N, "igo") for b in range(GB)]
    for p in range(2, SKIPS + 1):
        steps += [(p, s, q, N // p, "igfo" if s else "igo") for s in range(p) for q in range(2)]
    return steps


LSTM = lstm_steps()
GATE = {"i": 0, "f": 1, "g": 2, "o": 3}
FIRST_GATE = [sum(len(t[4]) for t in LSTM[:k]) for k in range(len(LSTM) + 1)]


def gate_number(k, gate):
    return FIRST_GATE[k] + LSTM[k][4].index(gate)


def windows(tile, k):
    p, s, q, w, _ = LSTM[k]
    if p == 1:
        return tile[:, q]
    return tile[:, 2 * q:2 * q + 2, s:s + p * (w - 1) + 1:p]


def flat(tile, k):
    p, s, q, w, _ = LSTM[k]
    if p == 1:
        return tile
    return tile[:, 0:2 * w].rearrange("p (b w) -> p b w", b=2)


def columns(k):
    return LSTM[k][3] * (1 if LSTM[k][0] == 1 else 2)


def dilated(nc, d, x):
    with ExitStack() as ctx:
        sb = lambda n, s, t=F32: ctx.enter_context(nc.sbuf_tensor(n, s, t))
        sem = lambda n: ctx.enter_context(nc.semaphore(n))
        at_s = sb("d_at_split", [P, 2, C, N], F32R)
        wg_s = sb("d_wg_split", [P, 2, 2, D], F32R)
        wih_s = sb("d_wih_split", [P, 2, SKIPS, 4 * D], F32R)
        whh_s = sb("d_whh_split", [P, 2, SKIPS, 4 * D], F32R)
        gate_b = sb("d_gate_bias", [P, SKIPS, 4])
        ident = sb("d_ident", [P, P])
        ident_r = sb("d_ident_r", [P, P], F32R)
        b_stack = sb("d_b_stack", [96, 2, D], F32R)
        r_stack = sb("d_r_stack", [96, N], F32R)
        x_s = sb("d_x_split", [P, 2, GB, C, D], F32R)
        ax_s = sb("d_ax_split", [P, GB, 2, N], F32R)
        h1_s = sb("d_h1_split", [P, GB, 2, C, D], F32R)
        ps = ctx.enter_context(nc.psum_tensor("d_banks", [P, 8, N], F32))
        K, GATES = len(LSTM), FIRST_GATE[-1]
        aside = sem("d_aside")
        count = lambda n, per: Count(sem(n), per, aside)
        x_hi, x_lo = count("d_x_hi", GB), count("d_x_lo", GB)
        conv_ready, conv_hi, conv_lo = (count(n, 4 * GB) for n in ("d_conv_ready", "d_conv_hi", "d_conv_lo"))
        RING = 6
        assert GATES % RING == 0 and K == 22
        UNITS_AT = {6: 0, 8: 1, 10: 2, 12: 3, 14: 4, 16: 5, 18: 6, 20: 7}
        TAIL = ((8,), (9,), (10,), (11,))
        OUT_STAGE = 3 * GB

        def split(pool, g, ahead):
            for b in range(GB):
                src = x[:, bass.ds(g * GB + (ahead * GB + b), 1)].rearrange("p a c d -> p (a c) d")
                wait_apart(pool, conv_hi, g, b - 4 * GB * (1 - ahead))
                pool.tensor_copy(x_s[:, 0, b], src).then_inc(x_hi.sem, 1)
                wait_apart(pool, x_hi, g, b + GB * ahead)
                pool.tensor_tensor(x_s[:, 1, b], src, f(x_s[:, 0, b]), ALU.subtract).then_inc(x_lo.sem, 1)

        def unit(pe, g, n):
            stage, b = n // GB % 4, n % GB
            bank = ps[:, RING + n % 2]
            if stage == 0:
                wait(pe, x_lo, g, n // (4 * GB) * GB + b)
            wait(pe, conv_lo, g, n - 2)
            if stage == 0:
                for c in range(C):
                    last = products(pe, bank, [x_s[:, h, b, c] for h in range(2)],
                                    [at_s[:, h, c] for h in range(2)], c == 0, c == C - 1)
            elif stage == 1:
                for c in range(C):
                    cols = slice(c * P, (c + 1) * P)
                    products(pe, bank[:, cols], [ax_s[:, b, h, cols] for h in range(2)],
                             [wg_s[:, h, 0] for h in range(2)], True, False)
                    last = pe.matmul(bank[:, cols], r_stack[:, cols], b_stack[:, 0], start=False, stop=True)
            elif stage == 2:
                for c in range(C):
                    last = products(pe, bank, [h1_s[:, b, h, c] for h in range(2)],
                                    [at_s[:, h, c] for h in range(2)], c == 0, c == C - 1)
            else:
                products(pe, bank, [wg_s[:, h, 1] for h in range(2)],
                         [ax_s[:, b, h] for h in range(2)], True, False)
                last = pe.matmul(bank, b_stack[:, 1], r_stack[:], start=False, stop=True)
            last.then_inc(conv_ready.sem, 1)

        def unit_hi(act, g, n):
            stage, b = n // GB % 4, n % GB
            bank = ps[:, RING + n % 2]
            wait(act, conv_ready, g, n)
            if stage == 1:
                act.activation(h1_s[:, b, 0], bank.rearrange("p (c d) -> p c d", c=C), ACT.Relu
                               ).then_inc(conv_hi.sem, 1)
            elif stage == 3:
                act.activation(h_s[:, 0, b], bank, ACT.Relu).then_inc(conv_hi.sem, 1)
            else:
                act.copy(ax_s[:, b, 0], bank).then_inc(conv_hi.sem, 1)

        def unit_lo(dve, g, n):
            stage, b = n // GB % 4, n % GB
            bank = ps[:, RING + n % 2]
            wait(dve, conv_hi, g, n)
            if stage == 1:
                ins = dve.scalar_tensor_tensor(h1_s[:, b, 1], bank.rearrange("p (c d) -> p c d", c=C), 0.0,
                                               f(h1_s[:, b, 0]), ALU.max, ALU.subtract)
            elif stage == 3:
                ins = dve.scalar_tensor_tensor(h_s[:, 1, b], bank, 0.0, f(h_s[:, 0, b]), ALU.max, ALU.subtract)
            else:
                ins = dve.tensor_tensor(ax_s[:, b, 1], bank, f(ax_s[:, b, 0]), ALU.subtract)
            ins.then_inc(conv_lo.sem, 1)

        with ExitStack() as tmp:
            tb = lambda n, s, t=F32: tmp.enter_context(nc.sbuf_tensor(n, s, t))
            at = tb("d_at", [P, C, N])
            wg = tb("d_wg", [P, 2, D])
            wih = tb("d_wih", [P, SKIPS, 4 * D])
            whh = tb("d_whh", [P, SKIPS, 4 * D])
            bih = tb("d_bih", [P, SKIPS, 4])
            bhh = tb("d_bhh", [P, SKIPS, 4])
            brow = tb("d_brow", [96, 2, D])
            rsum = tb("d_rsum", [96, N])
            ones = tb("d_ones", [P, 96], F32R)
            small_in, adj_in, w_in = (tmp.enter_context(nc.semaphore(n)) for n in ("d_small_in", "d_adj_in", "d_w_in"))
            act_hi, dve_lo, pe_sum, cleared, halved = (tmp.enter_context(nc.semaphore(n)) for n in
                                              ("d_act_hi", "d_dve_lo", "d_pe_sum", "d_cleared", "d_halved"))
            block = tmp.enter_context(nc.Block())

            @block.sync
            def _(sp):
                sp.dma_start(at[:], d["adjT"].rearrange("(c p) m -> p c m", p=P)).then_inc(adj_in, 16)
                for r in range(3):
                    for layer in range(2):
                        sp.dma_start(brow[32 * r:32 * r + 1, layer], d[f"bg{layer}"].rearrange("(a n) -> a n", a=1)
                                     ).then_inc(small_in, 16)
                for layer in range(2):
                    sp.dma_start(wg[:, layer], d[f"Wg{layer}"]).then_inc(small_in, 16)
                sp.dma_start(bih[:], d["bih"]).then_inc(small_in, 16)
                sp.dma_start(bhh[:], d["bhh"]).then_inc(small_in, 16)
                sp.dma_start(ident[:], d["ident"]).then_inc(small_in, 16)
                sp.dma_start(wih[:], d["WihT"]).then_inc(w_in, 16)
                sp.dma_start(whh[:], d["WhhT"]).then_inc(w_in, 16)

            @block.gpsimd
            def _(pool):
                credit(pool, x_hi, x_lo)
                pool.memset(f(b_stack[:]), 0.0)
                pool.memset(f(r_stack[:]), 0.0).then_inc(cleared, 1)
                split(pool, 0, 0)

            @block.scalar
            def _(act):
                credit(act, conv_hi)
                act.wait_ge(adj_in, 16)
                act.copy(at_s[:, 0], at[:]).then_inc(act_hi, 1)
                for u in range(GB + 2):
                    unit_hi(act, 0, u)
                act.wait_ge(w_in, 32)
                act.copy(wih_s[:, 0, 0], wih[:, 0])
                act.wait_ge(halved, 1)
                act.copy(wih_s[:, 0, 1:], wih[:, 1:]).then_inc(act_hi, 1)
                unit_hi(act, 0, GB + 2)
                act.copy(whh_s[:, 0], whh[:]).then_inc(act_hi, 1)
                for u in range(GB + 3, OUT_STAGE):
                    unit_hi(act, 0, u)

            @block.vector
            def _(dve):
                credit(dve, conv_lo)
                dve.memset(f(ones[:]), 1.0)
                dve.wait_ge(adj_in, 16)
                dve.wait_ge(act_hi, 1)
                dve.tensor_tensor(at_s[:, 1], at[:], f(at_s[:, 0]), ALU.subtract).then_inc(dve_lo, 1)
                dve.wait_ge(small_in, 11 * 16)
                dve.tensor_copy(wg_s[:, 0], wg[:])
                dve.tensor_copy(ident_r[:], ident[:])
                dve.tensor_tensor(gate_b[:], bih[:], bhh[:], ALU.add).then_inc(dve_lo, 1)
                dve.wait_ge(cleared, 1)
                for r in range(3):
                    last = dve.tensor_copy(b_stack[32 * r:32 * r + 1], brow[32 * r:32 * r + 1])
                last.then_inc(dve_lo, 1)
                unit_lo(dve, 0, 0)
                dve.wait_ge(dve_lo, 3)
                dve.tensor_tensor(wg_s[:, 1], wg[:], f(wg_s[:, 0]), ALU.subtract)
                for gate in "ifo":
                    dve.tensor_scalar(gate_b[:, :, GATE[gate]], gate_b[:, :, GATE[gate]], 0.5, None, ALU.mult)
                dve.tensor_tensor(b_stack[64:65], brow[64:65], f(b_stack[64:65]), ALU.subtract)
                for u in range(1, GB - 1):
                    unit_lo(dve, 0, u)
                dve.wait_ge(pe_sum, 1)
                dve.tensor_copy(rsum[:], ps[0:96, 0])
                for r in range(3):
                    last = dve.tensor_copy(r_stack[32 * r:32 * r + 1], ps[32 * r:32 * r + 1, 0])
                last.then_inc(dve_lo, 1)
                dve.wait_ge(dve_lo, 4)
                dve.tensor_tensor(r_stack[32:33], rsum[32:33], f(r_stack[32:33]), ALU.subtract).then_inc(dve_lo, 1)
                for u in range(GB - 1, GB + 1):
                    unit_lo(dve, 0, u)
                dve.wait_ge(w_in, 32)
                dve.tensor_scalar(wih[:, 1:], wih[:, 1:], 0.5, None, ALU.mult)
                dve.tensor_scalar(whh[:], whh[:], 0.5, None, ALU.mult).then_inc(halved, 1)
                for u in range(GB + 1, 2 * GB + 1):
                    unit_lo(dve, 0, u)
                dve.wait_ge(act_hi, 2)
                dve.tensor_tensor(wih_s[:, 1], wih[:], f(wih_s[:, 0]), ALU.subtract)
                unit_lo(dve, 0, 2 * GB + 1)
                dve.wait_ge(act_hi, 3)
                dve.tensor_tensor(whh_s[:, 1], whh[:], f(whh_s[:, 0]), ALU.subtract)
                for u in range(2 * GB + 2, OUT_STAGE):
                    unit_lo(dve, 0, u)

            @block.tensor
            def _(pe):
                credit(pe, conv_ready)
                pe.wait_ge(dve_lo, 1)
                for u in range(OUT_STAGE):
                    if u == GB - 2:
                        for c in range(C):
                            for h in range(2):
                                last = pe.matmul(ps[0:96, 0], ones[:], at_s[:, h, c], start=c + h == 0,
                                                 stop=(c, h) == (C - 1, 1))
                        last.then_inc(pe_sum, 1)
                    if u == GB:
                        pe.wait_ge(dve_lo, 5)
                    unit(pe, 0, u)

        h_s = sb("d_h_split", [P, 2, GB, N], F32R)
        cell_s = sb("d_cell_split", [P, 2, 2, N], F32R)
        gates = sb("d_gates", [P, 2, 4, N])
        state = sb("d_state", [P, 2, N])
        ig = sb("d_ig", [P, 2, N])
        fc = sb("d_fc", [P, 2, N])
        tc = sb("d_tc", [P, 2, N])
        h2 = sb("d_h2", [P, 2, N])
        norm = Norm(nc, ctx, "ln1", GB, aside)
        gate_ready, gate_tanh = count("d_gate_ready", GATES), count("d_gate_tanh", GATES)
        LATER = sum(1 for t in LSTM if t[1])
        ig_done, fc_done = count("d_ig_done", LATER), count("d_fc_done", LATER)
        state_done, state_tanh, h2_done, h2_hi, h2_lo = (
            count("d_" + n, K) for n in ("state_done", "state_tanh", "h2_done", "h2_hi", "h2_lo"))
        turned = count("d_turned", GB)
        block = ctx.enter_context(nc.Block())
        @block.gpsimd
        def _(pool):
            norm.start_pool(pool)

            def roots(g):
                for b in range(GB):
                    norm.pool_root(pool, g, b)

            with pool.Fori(0, NG - 1) as g:
                split(pool, g, 1)
                roots(g)
            roots(NG - 1)

        @block.scalar
        def _(act):
            credit(act, gate_tanh, state_tanh)

            def gate_tanhs(g, k, which):
                p, s, q, _, names = LSTM[k]
                for gate in which:
                    if gate in names:
                        n = gate_number(k, gate)
                        wait(act, gate_ready, g, n)
                        act.activation(gates[:, k % 2, GATE[gate], 0:columns(k)], ps[:, n % RING, 0:columns(k)],
                                       ACT.Tanh, bias=gate_b[:, p - 1, GATE[gate]:GATE[gate] + 1],
                                       scale=1.0 if gate == "g" else 0.5).then_inc(gate_tanh.sem, 1)

            def state_tanhs(g, k):
                wait(act, state_done, g, k)
                act.activation(tc[:, k % 2, 0:columns(k)], state[:, k % 2, 0:columns(k)], ACT.Tanh,
                               scale=0.5).then_inc(state_tanh.sem, 1)

            def body(g, ahead):
                unit_hi(act, g, OUT_STAGE)
                for k in range(K):
                    if k < GB - 1:
                        unit_hi(act, g, OUT_STAGE + k + 1)
                    if k >= GB:
                        state_tanhs(g, k - 1)
                    if ahead and k in UNITS_AT:
                        unit_hi(act, g, 4 * GB + UNITS_AT[k])
                    wait(act, h2_done, g, k - 2)
                    gate_tanhs(g, k, "ig")
                    if 0 < k < GB:
                        state_tanhs(g, k - 1)
                    gate_tanhs(g, k, "fo")
                state_tanhs(g, K - 1)
                if ahead:
                    for b in range(GB):
                        for u in TAIL[b]:
                            unit_hi(act, g, 4 * GB + u)

            with act.Fori(0, NG - 1) as g:
                body(g, True)
            body(NG - 1, False)

        @block.vector
        def _(dve):
            credit(dve, ig_done, fc_done, state_done, h2_done, h2_hi, h2_lo)
            norm.start_dve(dve)

            def output(g, k):
                p, s, q, _, _ = LSTM[k]
                w = columns(k)
                gk, hk = gates[:, k % 2], h2[:, k % 2, 0:w]
                hi, lo = ((flat(cell_s[:, k % 2, 0], k), flat(cell_s[:, k % 2, 1], k)) if s < p - 1 else
                          (windows(h_s[:, 0], k), windows(h_s[:, 1], k)))
                wait(dve, gate_tanh, g, gate_number(k, "o"))
                wait(dve, state_tanh, g, k)
                dve.scalar_tensor_tensor(hk, gk[:, 3, 0:w], 1.0, tc[:, k % 2, 0:w], ALU.add, ALU.mult
                                         ).then_inc(h2_done.sem, 1)
                wait(dve, h2_done, g, k)
                dve.tensor_copy(hi, flat(h2[:, k % 2], k)).then_inc(h2_hi.sem, 1)
                wait(dve, h2_hi, g, k)
                dve.tensor_tensor(lo, flat(h2[:, k % 2], k), f(hi), ALU.subtract).then_inc(h2_lo.sem, 1)

            def body(g, ahead):
                unit_lo(dve, g, OUT_STAGE)
                for k in range(K):
                    p, s, q, _, _ = LSTM[k]
                    w = columns(k)
                    gk = gates[:, k % 2]
                    if k < GB - 1:
                        unit_lo(dve, g, OUT_STAGE + k + 1)
                    if k >= GB:
                        output(g, k - 1)
                    if ahead and k in UNITS_AT:
                        unit_lo(dve, g, 4 * GB + UNITS_AT[k])
                    wait(dve, gate_tanh, g, gate_number(k, "g"))
                    target = ig[:, k % 2, 0:w] if s else state[:, k % 2, 0:w]
                    ins = dve.scalar_tensor_tensor(target, gk[:, 0, 0:w], 1.0, gk[:, 2, 0:w], ALU.add, ALU.mult)
                    ins.then_inc((ig_done if s else state_done).sem, 1)
                    if 0 < k < GB:
                        output(g, k - 1)
                    if s:
                        wait(dve, gate_tanh, g, gate_number(k, "f"))
                        dve.scalar_tensor_tensor(fc[:, k % 2, 0:w], gk[:, 1, 0:w], 1.0, state[:, k % 2, 0:w],
                                                 ALU.add, ALU.mult).then_inc(fc_done.sem, 1)
                        later = sum(1 for t in LSTM[:k] if t[1])
                        wait(dve, ig_done, g, later)
                        wait(dve, fc_done, g, later)
                        dve.scalar_tensor_tensor(state[:, k % 2, 0:w], fc[:, k % 2, 0:w], 0.5, ig[:, k % 2, 0:w],
                                                 ALU.mult, ALU.add).then_inc(state_done.sem, 1)
                output(g, K - 1)
                for b in range(GB + 1):
                    if b < GB:
                        wait(dve, turned, g, b)
                        wait(dve, norm.normed, g, b - 2)
                        dve.scalar_tensor_tensor(norm.sum[:, b % 2].rearrange("p c d -> p (c d)"), ps[:, b], 0.5,
                                                 x[:, bass.ds(g * GB + b, 1)].rearrange("p a c d -> p (a c d)"),
                                                 ALU.mult, ALU.add).then_inc(norm.summed.sem, 1)
                        norm.dve_stats(dve, g, b)
                        if ahead:
                            for u in TAIL[b]:
                                unit_lo(dve, g, 4 * GB + u)
                    if b >= 1:
                        norm.dve_apply(dve, g, b - 1,
                                       lambda c: x[:, bass.ds(g * GB + (b - 1), 1), c].rearrange("p a d -> p (a d)"))

            with dve.Fori(0, NG - 1) as g:
                body(g, True)
            body(NG - 1, False)

        @block.tensor
        def _(pe):
            credit(pe, gate_ready, turned)

            def body(g, ahead):
                unit(pe, g, OUT_STAGE)
                for k in range(K):
                    p, s, q, _, names = LSTM[k]
                    if k < GB - 1:
                        unit(pe, g, OUT_STAGE + k + 1)
                    if s == 0 and ahead and k in UNITS_AT:
                        unit(pe, g, 4 * GB + UNITS_AT[k])
                    if p == 1:
                        wait(pe, conv_lo, g, OUT_STAGE + q)
                    elif s == 0:
                        wait(pe, h2_lo, g, 2 * q + 1 if p == 2 else k - 2)
                    for gate in names:
                        n = gate_number(k, gate)
                        cols = slice(GATE[gate] * D, (GATE[gate] + 1) * D)
                        out = ps[:, n % RING, 0:columns(k)]
                        out = out if p == 1 else out.rearrange("p (b w) -> p b w", b=2)
                        if n < GB:
                            wait(pe, norm.summed, g, n - GB)
                        else:
                            wait(pe, gate_tanh, g, n - RING)
                        last = products(pe, out, [wih_s[:, h, p - 1, cols] for h in range(2)],
                                        [windows(h_s[:, h], k) for h in range(2)], True, s == 0)
                        if s == 0:
                            last.then_inc(gate_ready.sem, 1)
                    if s:
                        if ahead and k in UNITS_AT:
                            unit(pe, g, 4 * GB + UNITS_AT[k])
                        wait(pe, h2_lo, g, k - 2)
                        for gate in names:
                            n = gate_number(k, gate)
                            cols = slice(GATE[gate] * D, (GATE[gate] + 1) * D)
                            products(pe, ps[:, n % RING, 0:columns(k)],
                                     [whh_s[:, h, p - 1, cols] for h in range(2)],
                                     [cell_s[:, k % 2, h, 0:columns(k)] for h in range(2)], False, True
                                     ).then_inc(gate_ready.sem, 1)
                for b in range(GB):
                    if b % 2 == 0:
                        wait(pe, h2_lo, g, K - 2 + b // 2)
                    for c in range(C):
                        cols = slice(c * P, (c + 1) * P)
                        for h in range(2):
                            last = pe.matmul(ps[:, b, cols], h_s[:, h, b, cols], ident_r[:], start=h == 0, stop=h == 1)
                    last.then_inc(turned.sem, 1)
                    if ahead:
                        for u in TAIL[b]:
                            unit(pe, g, 4 * GB + u)

            with pe.Fori(0, NG - 1) as g:
                body(g, True)
            body(NG - 1, False)


def edge_attention(nc, d, x, keep):
    with ExitStack() as ctx:
        sb = lambda n, s, t=F32: ctx.enter_context(nc.sbuf_tensor(n, s, t))
        BH = BATCH * HEADS
        gather = sb("e_gather", [P, C, 2, EDGES], F32R)
        scatter = sb("e_scatter", [P, EC, N], F32R)
        w_s = sb("e_w_split", [P, 2, 3, D], F32R)
        a_blocks = sb("e_a_blocks", [P, HEADS])
        log_adj = sb("e_log_adj", [P, EC])
        breaks = sb("e_breaks", [BH, EDGES + 1])
        inside = sb("e_inside", [BH, EDGES])
        ident = keep[3]
        keep = keep + (sb("t_w", [P, 3 * D]), sb("t_adj_t", [P, C, N]))
        loaded, t_step = (ctx.enter_context(nc.semaphore(n)) for n in ("t_loaded", "t_step"))
        v_all = sb("e_v_all", [P, BATCH, EC, D])
        e_all = sb("e_e_all", [P, EC, BH])
        src_hot = sb("e_src_hot", [P, C, EDGES], F32R)
        dst_hot_t = sb("e_dst_hot_t", [P, EC, N])
        adj_s = sb("e_adj_split", [P, 2, C, N], F32R)
        x_s = sb("e_x_split", [P, 2, GB, C, D], F32R)
        aside = ctx.enter_context(nc.semaphore("e_aside"))
        x_hi, x_lo, z_hi = (Count(ctx.enter_context(nc.semaphore(n)), GB, aside) for n in ("e_x_hi", "e_x_lo", "e_z_hi"))
        x_rows = lambda g, n: x[:, bass.ds(g * GB + n, 1)].rearrange("p a c d -> p (a c) d")

        def x_high(act, g, n):
            act.copy(x_s[:, 0, n % GB], x_rows(g, n)).then_inc(x_hi.sem, 1)

        def x_low(pool, g, n):
            wait_apart(pool, x_hi, g, n)
            pool.tensor_tensor(x_s[:, 1, n % GB], x_rows(g, n), f(x_s[:, 0, n % GB]), ALU.subtract).then_inc(x_lo.sem, 1)

        with ExitStack() as tmp:
            tb = lambda n, s, t=F32: tmp.enter_context(nc.sbuf_tensor(n, s, t))
            sem = lambda n: tmp.enter_context(nc.semaphore(n))
            adj = tb("e_adj", [P, C, N])
            w = tb("e_w", [P, 3, D])
            a_col = tb("e_a_col", [P, 1])
            head_mask = tb("e_head_mask", [P, HEADS])
            iota = tb("e_iota", [P, N])
            node = tb("e_node", [P, C])
            ends_i = tb("e_ends_i", [P, EC, 2], I32)
            src_i = tb("e_src_i", [P, EDGES], I32)
            ends = tb("e_ends", [P, EC, 2])
            src_row = tb("e_src_row", [P, EDGES])
            key_row = tb("e_key_row", [P, EDGES])
            key_col = tb("e_key_col", [P, EC])
            ends_r = tb("e_ends_r", [P, EC, 2], F32R)
            less = tb("e_less", [P, EC, EDGES])
            rank = tb("e_rank", [P, EC])
            order = tb("e_order", [P, EC, EDGES], F32R)
            wide = tb("e_wide", [P, EC, 2, P], F32R)
            row = tb("e_row", [P, 2, EDGES])
            col = tb("e_col", [P, EC, 2])
            new = tb("e_new", [BH, EDGES])
            ps = tmp.enter_context(nc.psum_tensor("e_ps", [P, 2, N], F32))
            adj_in, ends_in, small_in, pe_done, step, adj_hi = (sem("e_adj_in"), sem("e_ends_in"), sem("e_small_in"),
                                                                sem("e_pe_done"), sem("e_step"), sem("e_adj_hi"))
            block = tmp.enter_context(nc.Block())

            @block.sync
            def _(sp):
                sp.dma_start(src_i[:], d["src"].rearrange("(a e) -> a e", a=1).to_broadcast([P, EDGES])).then_inc(ends_in, 16)
                sp.dma_start(ends_i[:], d["edge_ends"]).then_inc(ends_in, 16)
                sp.dma_start(iota[:], d["iota"]).then_inc(ends_in, 16)
                sp.dma_start(node[:], d["node"]).then_inc(ends_in, 16)
                sp.dma_start(ident[:], d["ident"]).then_inc(ends_in, 16)
                sp.dma_start(head_mask[:], d["head_mask"]).then_inc(small_in, 16)
                sp.dma_start(a_col[:], d["a"]).then_inc(small_in, 16)
                for i, name in enumerate(("W_linT", "W_valT", "W_outT")):
                    sp.dma_start(w[:, i], d[name]).then_inc(small_in, 16)
                sp.dma_start(adj[:], d["adj"].rearrange("(c p) m -> p c m", p=P)).then_inc(adj_in, 16)
                attention_load(sp, d, keep, loaded)

            @block.scalar
            def _(act):
                credit(act, x_hi)
                for b in range(GB):
                    x_high(act, 0, b)
                act.wait_ge(adj_in, 16)
                act.copy(adj_s[:, 0], adj[:]).then_inc(adj_hi, 1)

            @block.gpsimd
            def _(pool):
                credit(pool, x_lo)
                pool.memset(breaks[:], BIG)
                pool.memset(inside[:, 0:1], 0.0)
                for b in range(GB):
                    x_low(pool, 0, b)
                pool.wait_ge(adj_hi, 1)
                pool.tensor_tensor(adj_s[:, 1], adj[:], f(adj_s[:, 0]), ALU.subtract)

            @block.vector
            def _(dve):
                def then(ins, n):
                    ins.then_inc(step, 1)
                    dve.wait_ge(step, n)

                dve.wait_ge(ends_in, 5 * 16)
                dve.tensor_copy(ends[:], ends_i[:])
                then(dve.tensor_copy(src_row[:], src_i[:]), 1)
                dve.tensor_copy(ends_r[:], ends[:])
                dve.scalar_tensor_tensor(key_row[:], src_row[:], float(EDGES), iota[:, 0:EDGES], ALU.mult, ALU.add)
                then(dve.scalar_tensor_tensor(key_col[:], ends[:, :, 0], float(EDGES), node[:, 0:EC],
                                              ALU.mult, ALU.add), 2)
                for c in range(EC):
                    last = dve.tensor_scalar(less[:, c], key_row[:], key_col[:, c:c + 1], None, ALU.is_lt)
                then(last, 3)
                then(dve.tensor_reduce(rank[:], less[:], AX.X, ALU.add), 4)
                for c in range(EC):
                    dve.tensor_scalar(order[:, c], iota[:, 0:EDGES], rank[:, c:c + 1], None, ALU.is_equal)
                for c in range(EC):
                    for i in range(2):
                        last = dve.tensor_scalar(wide[:, c, i], ident[:], 0.0, ends[:, c, i:i + 1], ALU.mult, ALU.add)
                last.then_inc(step, 1)
                dve.wait_ge(small_in, 5 * 16)
                dve.tensor_scalar(a_blocks[:], head_mask[:], a_col[:], None, ALU.mult)
                dve.tensor_copy(w_s[:, 0], w[:]).then_inc(step, 1)
                dve.wait_ge(pe_done, 2)
                dve.tensor_copy(row[:], ps[:, 0].rearrange("p (i e) -> p i e", i=2))
                then(dve.tensor_copy(col[:], ps[:, 1, 0:2 * EC].rearrange("p (c i) -> p c i", c=EC)), 7)
                for c in range(C):
                    dve.tensor_scalar(gather[:, c, 1], row[:, 1], node[:, c:c + 1], None, ALU.is_equal)
                    last = dve.tensor_scalar(src_hot[:, c], row[:, 0], node[:, c:c + 1], None, ALU.is_equal)
                then(last, 8)
                dve.tensor_tensor(gather[:, :, 0], f(src_hot[:]), f(gather[:, :, 1]), ALU.add)
                for c in range(EC):
                    dve.tensor_scalar(dst_hot_t[:, c], iota[:], col[:, c, 1:2], None, ALU.is_equal)
                    dve.tensor_scalar(scatter[:, c], iota[:], col[:, c, 0:1], None, ALU.is_equal)
                dve.tensor_tensor(w_s[:, 1], w[:], f(w_s[:, 0]), ALU.subtract)
                then(dve.tensor_tensor(new[:, 1:EDGES], row[0:BH, 0, 1:EDGES], row[0:BH, 0, 0:EDGES - 1],
                                       ALU.not_equal), 9)
                dve.tensor_scalar(inside[:, 1:EDGES], new[:, 1:EDGES], -1.0, 1.0, ALU.mult, ALU.add)
                dve.wait_ge(x_lo.sem, GB + 1)
                dve.tensor_scalar(breaks[:, 1:EDGES], new[:, 1:EDGES], BIG, None, ALU.mult)

            @block.tensor
            def _(pe):
                pe.wait_ge(step, 5)
                for i in range(2):
                    for c in range(EC):
                        last = pe.matmul(ps[:, 0, i * EDGES:(i + 1) * EDGES], wide[:, c, i], order[:, c],
                                         start=c == 0, stop=c == EC - 1)
                last.then_inc(pe_done, 1)
                for r in range(EC):
                    for c in range(EC):
                        last = pe.matmul(ps[:, 1, 2 * r:2 * r + 2], order[:, c, r * P:(r + 1) * P], ends_r[:, c],
                                         start=c == 0, stop=c == EC - 1)
                last.then_inc(pe_done, 1)

        with ExitStack() as tmp:
            tb = lambda n, s, t=F32: tmp.enter_context(nc.sbuf_tensor(n, s, t))
            count = lambda n: Count(tmp.enter_context(nc.semaphore(n)), GB, aside)
            picked = tb("e_picked", [P, EC, N])
            a0 = tb("e_a0", [P, EC])
            z_s = tb("e_z_split", [P, 2, 2, 2 * EDGES], F32R)
            q_sum = tb("e_q_sum", [P, 2, EDGES])
            lrelu = tb("e_lrelu", [P, 2, EDGES])
            ps = tmp.enter_context(nc.psum_tensor("e_banks", [P, 8, N], F32))
            z_ready, z_lo, q_ready, q_copied, lrelu_done, v_ready, v_copied, e_ready, e_done = (
                count("e_" + n) for n in ("z_ready", "z_lo", "q_ready", "q_copied",
                                          "lrelu_done", "v_ready", "v_copied", "e_ready", "e_done"))
            adj_rows, step = (tmp.enter_context(nc.semaphore(n)) for n in ("e_adj_rows", "e_pick_step"))
            block = tmp.enter_context(nc.Block())
            Z, Q, V, E = 0, 2, 4, 6

            @block.gpsimd
            def _(pool):
                with pool.Fori(0, NG - 1) as g:
                    for b in range(GB):
                        x_low(pool, g, GB + b)

            @block.scalar
            def _(act):
                credit(act, z_hi, q_copied, v_copied)

                def z_high(g, n):
                    wait(act, z_ready, g, n)
                    wait(act, v_ready, g, n - 2)
                    act.copy(z_s[:, n % 2, 0], ps[:, Z + n % 2]).then_inc(z_hi.sem, 1)

                def copies(g, n):
                    wait(act, q_ready, g, n)
                    wait(act, lrelu_done, g, n - 2)
                    act.copy(q_sum[:, n % 2], ps[:, Q + n % 2, 0:EDGES]).then_inc(q_copied.sem, 1)
                    wait(act, v_ready, g, n)
                    act.copy(v_all[:, bass.ds(g * GB + n, 1)].rearrange("p a c d -> p (a c d)"),
                             ps[:, V + n % 2, 0:EC * D]).then_inc(v_copied.sem, 1)

                def body(g, first, final):
                    for b in range(GB):
                        z_high(g, b)
                        if not final:
                            x_high(act, g, GB + b)
                        if b or not first:
                            copies(g, b - 1)
                body(0, True, False)
                with act.Fori(1, NG - 1) as g:
                    body(g, False, False)
                body(NG - 1, False, True)
                copies(NG - 1, GB - 1)
                act.wait_ge(step, 3)
                act.activation(log_adj[:], a0[:], ACT.Ln)

            @block.vector
            def _(dve):
                credit(dve, z_lo, lrelu_done, e_done)
                attention_constants(dve, keep, loaded, t_step)
                dve.wait_ge(adj_rows, 1)
                dve.tensor_tensor(picked[:], ps[:, Q:Q + 2], dst_hot_t[:], ALU.mult).then_inc(step, 1)
                dve.wait_ge(step, 1)
                dve.tensor_reduce(a0[:], picked[:], AX.X, ALU.add).then_inc(step, 1)
                dve.wait_ge(step, 2)
                dve.tensor_scalar(a0[:], a0[:], 1e-8, None, ALU.add).then_inc(step, 1)

                def z_low(g, n):
                    wait(dve, z_hi, g, n)
                    dve.tensor_tensor(z_s[:, n % 2, 1], ps[:, Z + n % 2], f(z_s[:, n % 2, 0]),
                                      ALU.subtract).then_inc(z_lo.sem, 1)

                def leaky(g, n):
                    wait(dve, q_copied, g, n)
                    wait(dve, e_ready, g, n - 2)
                    dve.scalar_tensor_tensor(lrelu[:, n % 2], q_sum[:, n % 2], 0.2, ps[:, Q + n % 2, 0:EDGES],
                                             ALU.mult, ALU.max).then_inc(lrelu_done.sem, 1)

                def logits(g, n):
                    wait(dve, e_ready, g, n)
                    dve.tensor_copy(e_all[:, :, bass.ds((g * GB + n) * HEADS, HEADS)],
                                    ps[:, E + n % 2, 0:EC * HEADS].rearrange("p (c h) -> p c h", c=EC)
                                    ).then_inc(e_done.sem, 1)
                staggered(dve, ((0, z_low), (1, leaky), (2, logits)))

            @block.tensor
            def _(pe):
                credit(pe, z_ready, q_ready, v_ready, e_ready)
                for r in range(EC):
                    for c in range(C):
                        for h in range(2):
                            last = pe.matmul(ps[:, Q + r], src_hot[:, c, r * P:(r + 1) * P], adj_s[:, h, c],
                                             start=c + h == 0, stop=(c, h) == (C - 1, 1))
                last.then_inc(adj_rows, 1)

                def gathers(g, n):
                    wait(pe, x_lo, g, n)
                    wait(pe, z_lo, g, n - 2)
                    for c in range(C):
                        for h in range(2):
                            last = pe.matmul(ps[:, Z + n % 2], x_s[:, h, n % GB, c],
                                             gather[:, c].rearrange("p i e -> p (i e)"),
                                             start=c + h == 0, stop=(c, h) == (C - 1, 1))
                    last.then_inc(z_ready.sem, 1)

                def images(g, n):
                    wait(pe, z_lo, g, n)
                    wait(pe, lrelu_done, g, n - 2)
                    products(pe, ps[:, Q + n % 2, 0:EDGES], [w_s[:, h, 0] for h in range(2)],
                             [z_s[:, n % 2, h, 0:EDGES] for h in range(2)]).then_inc(q_ready.sem, 1)
                    wait(pe, v_copied, g, n - 2)
                    for c in range(EC):
                        last = products(pe, ps[:, V + n % 2, c * D:(c + 1) * D],
                                        [z_s[:, n % 2, h, EDGES + c * P:EDGES + (c + 1) * P] for h in range(2)],
                                        [w_s[:, h, 1] for h in range(2)])
                    last.then_inc(v_ready.sem, 1)

                def weigh(g, n):
                    wait(pe, lrelu_done, g, n)
                    wait(pe, e_done, g, n - 2)
                    for c in range(EC):
                        last = pe.matmul(ps[:, E + n % 2, c * HEADS:(c + 1) * HEADS],
                                         lrelu[:, n % 2, c * P:(c + 1) * P], a_blocks[:], start=True, stop=True)
                    last.then_inc(e_ready.sem, 1)
                staggered(pe, ((0, gathers), (1, images), (2, weigh)))

        with ExitStack() as tmp:
            tb = lambda n, s: tmp.enter_context(nc.sbuf_tensor(n, s, F32))
            sem = lambda n: tmp.enter_context(nc.semaphore(n))
            e_t, run, top, shifted, ex, total, share = (tb("e_" + n, [BH, EDGES]) for n in
                                                        ("t", "run", "top", "shifted", "ex", "total", "share"))
            ps = tmp.enter_context(nc.psum_tensor("e_turn", [P, 2, N], F32))
            logged, turned, step, ex_done, back = (sem("e_logged"), sem("e_turned"), sem("e_sstep"), sem("e_ex_done"),
                                                   sem("e_back"))
            block = tmp.enter_context(nc.Block())
            flip = lambda t, a, b: t[:, a:b][:, ::-1]

            @block.tensor
            def _(pe):
                pe.wait_ge(logged, 1)
                for c in range(EC):
                    last = pe.transpose(ps[0:BH, 0, c * P:(c + 1) * P], e_all[:, c], ident[:])
                last.then_inc(turned, 1)
                pe.wait_ge(step, 8)
                for c in range(EC):
                    last = pe.transpose(ps[:, 1, c * BH:(c + 1) * BH], share[:, c * P:(c + 1) * P], ident[0:BH, 0:BH])
                last.then_inc(back, 1)

            @block.scalar
            def _(act):
                act.wait_ge(step, 4)
                act.activation(ex[:], shifted[:], ACT.Exp).then_inc(ex_done, 1)

            @block.vector
            def _(dve):
                def then(ins, n):
                    ins.then_inc(step, 1)
                    dve.wait_ge(step, n)

                for c in range(EC):
                    last = dve.tensor_scalar(e_all[:, c], e_all[:, c], log_adj[:, c:c + 1], None, ALU.add)
                last.then_inc(logged, 1)
                dve.wait_ge(turned, 1)
                then(dve.tensor_copy(e_t[:], ps[0:BH, 0, 0:EDGES]), 1)
                then(dve.tensor_tensor_scan(run[:], breaks[:, 0:EDGES], e_t[:], BIG, ALU.add, ALU.max), 2)
                then(dve.tensor_tensor_scan(flip(top, 0, EDGES), flip(breaks, 1, EDGES + 1), flip(run, 0, EDGES), BIG,
                                            ALU.add, ALU.max), 3)
                dve.tensor_tensor(shifted[:], e_t[:], top[:], ALU.subtract).then_inc(step, 1)
                dve.wait_ge(ex_done, 1)
                then(dve.tensor_tensor_scan(run[:], inside[:], ex[:], 0.0, ALU.mult, ALU.add), 5)
                then(dve.tensor_tensor_scan(flip(total, 0, EDGES), flip(breaks, 1, EDGES + 1), flip(run, 0, EDGES), BIG,
                                            ALU.add, ALU.max), 6)
                then(dve.reciprocal(total[:], total[:]), 7)
                dve.tensor_tensor(share[:], ex[:], total[:], ALU.mult).then_inc(step, 1)
                dve.wait_ge(back, 1)
                dve.tensor_copy(e_all[:], ps[:, 1, 0:EC * BH].rearrange("p (c n) -> p c n", c=EC))

        with ExitStack() as tmp:
            tb = lambda n, s, t=F32: tmp.enter_context(nc.sbuf_tensor(n, s, t))
            aside = tmp.enter_context(nc.semaphore("y_aside"))
            count = lambda n: Count(tmp.enter_context(nc.semaphore(n)), GB, aside)
            av = tb("y_av", [P, 2, EC, D])
            av_s = tb("y_av_split", [P, 2, 2, EC, D], F32R)
            y_s = tb("y_y_split", [P, 2, 2, N], F32R)
            norm = Norm(nc, tmp, "ln2", GB, aside)
            ps = tmp.enter_context(nc.psum_tensor("y_banks", [P, 4, N], F32))
            av_done, av_hi, av_lo, y_ready, y_hi, y_lo, o_ready = (
                count("y_" + n) for n in ("av_done", "av_hi", "av_lo", "y_ready", "y_hi", "y_lo", "o_ready"))
            block = tmp.enter_context(nc.Block())

            rows = lambda g, n: x[:, bass.ds(g * GB + n, 1)]

            @block.gpsimd
            def _(pool):
                credit(pool, av_done)
                norm.start_pool(pool)

                def weighted(g, n):
                    wait_apart(pool, av_lo, g, n - 2)
                    pool.tensor_tensor(
                        av[:, n % 2].rearrange("p c (h d) -> p c h d", h=HEADS),
                        v_all[:, bass.ds(g * GB + n, 1)].rearrange("p a c (h d) -> p (a c) h d", h=HEADS),
                        e_all[:, :, bass.ds((g * GB + n) * HEADS, HEADS)].unsqueeze(3)
                        .to_broadcast([P, EC, HEADS, DH]), ALU.mult).then_inc(av_done.sem, 1)

                staggered(pool, ((0, weighted), (3, lambda g, n: norm.pool_root(pool, g, n))))

            @block.scalar
            def _(act):
                credit(act, av_hi, y_hi)

                def av_high(g, n):
                    wait(act, av_done, g, n)
                    wait(act, y_ready, g, n - 2)
                    act.copy(av_s[:, n % 2, 0], av[:, n % 2]).then_inc(av_hi.sem, 1)

                def y_high(g, n):
                    wait(act, y_ready, g, n)
                    wait(act, o_ready, g, n - 2)
                    act.copy(y_s[:, n % 2, 0], ps[:, n % 2]).then_inc(y_hi.sem, 1)
                staggered(act, ((1, av_high), (2, y_high)))

            @block.vector
            def _(dve):
                credit(dve, av_lo, y_lo)
                norm.start_dve(dve)

                def av_low(g, n):
                    wait(dve, av_hi, g, n)
                    dve.tensor_tensor(av_s[:, n % 2, 1], av[:, n % 2], f(av_s[:, n % 2, 0]),
                                      ALU.subtract).then_inc(av_lo.sem, 1)

                def y_low(g, n):
                    wait(dve, y_hi, g, n)
                    dve.tensor_tensor(y_s[:, n % 2, 1], ps[:, n % 2], f(y_s[:, n % 2, 0]),
                                      ALU.subtract).then_inc(y_lo.sem, 1)

                def statistics(g, n):
                    wait(dve, o_ready, g, n)
                    wait(dve, norm.normed, g, n - 2)
                    dve.tensor_tensor(norm.sum[:, n % 2].rearrange("p c d -> p (c d)"), ps[:, 2 + n % 2],
                                      rows(g, n).rearrange("p a c d -> p (a c d)"), ALU.add).then_inc(norm.summed.sem, 1)
                    norm.dve_stats(dve, g, n)

                def apply(g, n):
                    norm.dve_apply(dve, g, n, lambda c: rows(g, n)[:, :, c].rearrange("p a d -> p (a d)"))
                staggered(dve, ((1, av_low), (2, y_low), (3, statistics), (4, apply)))

            @block.tensor
            def _(pe):
                credit(pe, y_ready, o_ready)

                def to_sources(g, n):
                    wait(pe, av_lo, g, n)
                    wait(pe, y_lo, g, n - 2)
                    for c in range(EC):
                        for h in range(2):
                            last = pe.matmul(ps[:, n % 2], av_s[:, n % 2, h, c], scatter[:, c],
                                             start=c + h == 0, stop=(c, h) == (EC - 1, 1))
                    last.then_inc(y_ready.sem, 1)

                def output(g, n):
                    wait(pe, y_lo, g, n)
                    wait(pe, norm.summed, g, n - 2)
                    for c in range(C):
                        cols = slice(c * P, (c + 1) * P)
                        last = products(pe, ps[:, 2 + n % 2, cols], [y_s[:, n % 2, h, cols] for h in range(2)],
                                        [w_s[:, h, 2] for h in range(2)])
                    last.then_inc(o_ready.sem, 1)
                staggered(pe, ((1, to_sources), (2, output)))


BODY = 2
TILES = HEADS * C
BT = BODY * TILES
BHD = BODY * HEADS
FAR = 1.5 * 2.0 ** 127


def attention_load(sp, d, keep, loaded):
    mask, mask_t, w_s, ident, eps, w, adj_t = keep
    sp.dma_start(mask[:], d["adj"].rearrange("(c p) m -> p c m", p=P)).then_inc(loaded, 16)
    sp.dma_start(adj_t[:], d["adjT"].rearrange("(c p) m -> p c m", p=P)).then_inc(loaded, 16)
    sp.dma_start(w[:], d["W_qkv"]).then_inc(loaded, 16)


def attention_constants(dve, keep, loaded, step):
    mask, mask_t, w_s, ident, eps, w, adj_t = keep
    dve.wait_ge(loaded, 48)
    dve.tensor_scalar(w[:, 0:D], w[:, 0:D], -float(DH) ** -0.5, None, ALU.mult)
    dve.tensor_scalar(mask_t[:], adj_t[:], 0.0, FAR, ALU.is_equal, ALU.mult)
    dve.tensor_scalar(mask[:], mask[:], 0.0, FAR, ALU.is_equal, ALU.mult).then_inc(step, 1)
    dve.wait_ge(step, 1)
    dve.tensor_copy(w_s[:, 0], w[:])
    dve.tensor_reduce(eps[:], mask[:], AX.X, ALU.min).then_inc(step, 1)
    dve.wait_ge(step, 2)
    dve.tensor_tensor(w_s[:, 1], w[:], f(w_s[:, 0]), ALU.subtract)
    dve.tensor_scalar(eps[:], eps[:], -BIG, 0.0, ALU.mult, ALU.mult).then_inc(step, 1)
    dve.wait_ge(step, 3)
    dve.tensor_scalar(eps[:], eps[:], EPS, None, ALU.add)


def self_attention(nc, d, x, out, keep):
    with ExitStack() as ctx:
        sb = lambda n, s, t=F32: ctx.enter_context(nc.sbuf_tensor(n, s, t))
        sem = lambda n: ctx.enter_context(nc.semaphore(n))
        mask, mask_t, w_s, ident, eps = keep
        aside = sem("t_aside")
        count = lambda n, per: Count(sem("t_" + n), per, aside)
        ident_r = sb("t_ident_r", [P, P], F32R)
        x_s = sb("t_x_split", [P, BODY, 2, C, D], F32R)
        xt_s = sb("t_xt_split", [P, BODY, 2, N], F32R)
        qk = sb("t_qk", [P, BODY, 4, N], F32R)
        stack = sb("t_stack", [98, BODY, HEADS, 2, N], F32R)
        v_w = sb("t_v", [P, BODY, C, HEADS, DH + 1])
        masked = sb("t_masked", [P, 2, N])
        low = sb("t_low", [P, 4, C])
        low_s = sb("t_low_split", [P, 2, C, 2], F32R)
        prob = sb("t_prob", [P, 4, C, N])
        recip = sb("t_recip", [P, 2, C])
        o_all = sb("t_o_all", [P, BODY, C, D])
        norm = Norm(nc, ctx, "ln3", BODY, aside, eps)
        ps = ctx.enter_context(nc.psum_tensor("t_banks", [P, 8, N], F32))
        S, T, O, M, R = 0, 2, 4, 6, 7

        x_hi, x_lo, xt_ready, xt_hi, xt_lo = (count(n, BODY) for n in ("x_hi", "x_lo", "xt_ready", "xt_hi", "xt_lo"))
        qk_ready, qk_hi, qk_lo = (count(n, 2 * BODY) for n in ("qk_ready", "qk_hi", "qk_lo"))
        v_ready, v_done = (count(n, BODY) for n in ("v_ready", "v_done"))
        stacked = [count(f"stacked{m}", 16 * 3) for m in range(BHD)]
        s_ready, masked_done, t_ready, exp_done = (count(n, BT) for n in ("s_ready", "masked_done", "t_ready", "exp_done"))
        low_hi, low_lo, row_ready, row_done, o_ready, rec_done, o_done = (count(n, BHD) for n in (
            "low_hi", "low_lo", "row_ready", "row_done", "o_ready", "rec_done", "o_done"))
        filled, identity, stored = sem("t_filled"), sem("t_identity"), sem("t_stored")
        BODIES = BATCH // BODY
        AHEAD = 2 * C
        TAIL = 14

        def run(eng, prologue, slot):
            prologue()

            def body(g, first, left):
                inside = lambda n, unit=1: (n >= 0 or not first) and n * unit < left * BT
                for t in range(BT + (TAIL if left == 1 else 0)):
                    slot(g, t, inside)
            body(0, True, BODIES)
            with eng.Fori(1, BODIES - 2) as g:
                body(g, False, BODIES)
            body(BODIES - 2, False, 2)
            body(BODIES - 1, False, 1)

        def batch_of(g, n):
            return x[:, bass.ds(g * BODY + n, 1)] if not isinstance(g, int) else x[:, g * BODY + n:g * BODY + n + 1]

        def wait_stacked(eng, g, m):
            wait(eng, stacked[m % BHD], g, 48 * (m // BHD) + 47)

        def slots_of_batch(t, table):
            return [(what, t // TILES + ahead) for at, ahead, what in table if t % TILES == at]

        block = ctx.enter_context(nc.Block())

        @block.sync
        def _(sp):
            def restack(g, m):
                n, h = m // HEADS, m % HEADS
                wait_apart(sp, qk_lo, g, 2 * n + 1)
                wait_apart(sp, t_ready, g, C * (m - BHD + 1) - 1)
                rows = slice(h * DH, (h + 1) * DH)
                for r, pick in enumerate((slice(0, 3, 2), slice(0, 4, 3), slice(1, 3))):
                    sp.dma_start(f(stack[r * DH:(r + 1) * DH, n % BODY, h]), f(qk[rows, n % BODY, pick])
                                 ).then_inc(stacked[m % BHD].sem, 16)

            def start():
                credit(sp, *stacked)
                for m in range(BHD):
                    restack(0, m)

            def slot(g, t, inside):
                if t % C == C - 1 and inside(t // C + BHD, C):
                    restack(g, t // C + BHD)
                if t % TILES == 13 and inside((t - 29) // TILES, TILES):
                    n = (t - 29) // TILES
                    wait_apart(sp, norm.normed, g, n)
                    dst = out[bass.ds(g * BODY + n, 1)] if not isinstance(g, int) else out[g * BODY + n:g * BODY + n + 1]
                    sp.dma_start(dst.rearrange("a (c p) d -> p (a c) d", p=P),
                                 batch_of(g, n).rearrange("p a c d -> p (a c) d")).then_inc(stored, 16)
            run(sp, start, slot)
            sp.wait_ge(stored, 16 * BATCH)

        @block.gpsimd
        def _(pool):
            def split(g, n):
                j, src = n % BODY, batch_of(g, n).rearrange("p a c d -> p (a c) d")
                wait_apart(pool, xt_hi, g, n - BODY)
                pool.tensor_copy(x_s[:, j, 0], src).then_inc(x_hi.sem, 1)
                wait_apart(pool, x_hi, g, n)
                pool.tensor_tensor(x_s[:, j, 1], src, f(x_s[:, j, 0]), ALU.subtract).then_inc(x_lo.sem, 1)

            def start():
                credit(pool, x_hi, x_lo, norm.summed)
                norm.start_pool(pool)
                for n in range(3):
                    split(0, n)

            def slot(g, t, inside):
                if t % TILES == 6 and inside((t - 22) // TILES, TILES):
                    n = (t - 22) // TILES
                    wait_apart(pool, o_done, g, HEADS * (n + 1) - 1)
                    wait_apart(pool, norm.normed, g, n - 2)
                    pool.tensor_tensor(norm.sum[:, n % BODY], batch_of(g, n).rearrange("p a c d -> p (a c) d"),
                                       o_all[:, n % BODY], ALU.add).then_inc(norm.summed.sem, 1)
                    norm.pool_root(pool, g, n)
                for what, n in slots_of_batch(t, ((1, 3, split),)):
                    if inside(n, TILES):
                        what(g, n)
            run(pool, start, slot)

        @block.scalar
        def _(act):
            def exponent(g, t):
                m, c = t // C, t % C
                wait(act, t_ready, g, t)
                wait(act, o_ready, g, m - 4)
                act.activation(prob[:, m % 4, c], ps[:, T + t % 2], ACT.Exp, scale=-1.0).then_inc(exp_done.sem, 1)

            def turned_x(g, n):
                wait(act, xt_ready, g, n)
                wait(act, v_ready, g, n - 2)
                act.copy(xt_s[:, n % BODY, 0], ps[:, M]).then_inc(xt_hi.sem, 1)

            def q_high(g, n, i=0):
                if i == 0:
                    for m in range(HEADS * (n - BODY), HEADS * (n - BODY + 1)):
                        wait_stacked(act, g, m)
                wait(act, qk_ready, g, 2 * n + i)
                act.copy(qk[:, n % BODY, 2 * i], ps[:, M]).then_inc(qk_hi.sem, 1)

            def k_high(g, n):
                q_high(g, n, 1)

            def v_copy(g, n):
                wait(act, v_ready, g, n)
                wait(act, o_ready, g, HEADS * (n - 1) - 1)
                act.copy(v_w[:, n % BODY, :, :, 0:DH], ps[:, M].rearrange("p (c h d) -> p c h d", c=C, h=HEADS)
                         ).then_inc(v_done.sem, 1)

            def row(g, m):
                wait(act, row_ready, g, m)
                wait(act, t_ready, g, C * (m - BHD + 1) - 1)
                act.copy(stack[96:98, m // HEADS % BODY, m % HEADS, 0], ps[0:2, R]).then_inc(row_done.sem, 1)

            def start():
                credit(act, exp_done, xt_hi, qk_hi, v_done, row_done)
                act.copy(ident_r[:], ident[:]).then_inc(identity, 1)
                turned_x(0, 0)
                q_high(0, 0)
                k_high(0, 0)
                v_copy(0, 0)
                turned_x(0, 1)
                q_high(0, 1)
                k_high(0, 1)
                turned_x(0, 2)
                row(0, 0)
                q_high(0, 2)
                k_high(0, 2)

            def slot(g, t, inside):
                if inside(t):
                    exponent(g, t)
                if t % C == 2 and inside(t // C + 1, C):
                    row(g, t // C + 1)
                for what, n in slots_of_batch(t, ((8, 1, v_copy), (10, 3, turned_x), (12, 3, q_high), (14, 3, k_high))):
                    if inside(n, TILES):
                        what(g, n)
            run(act, start, slot)

        @block.vector
        def _(dve):
            def mask_scores(g, t):
                m, c = t // C, t % C
                if c == 0:
                    wait_apart(dve, low_lo, g, m - 4)
                wait_apart(dve, s_ready, g, t)
                dve.tensor_tensor_reduce(masked[:, t % 2], ps[:, S + t % 2], mask[:, c], 1.0, -BIG, ALU.add, ALU.min,
                                         low[:, m % 4, c:c + 1]).then_inc(masked_done.sem, 1)

            def split_low(g, m):
                wait(dve, masked_done, g, C * m + C - 1)
                wait(dve, row_ready, g, m - 2)
                dve.tensor_copy(low_s[:, m % 2, :, 0], low[:, m % 4]).then_inc(low_hi.sem, 1)
                wait(dve, low_hi, g, m)
                dve.tensor_tensor(low_s[:, m % 2, :, 1], low[:, m % 4], f(low_s[:, m % 2, :, 0]), ALU.subtract
                                  ).then_inc(low_lo.sem, 1)

            def turned_x(g, n):
                wait(dve, xt_hi, g, n)
                dve.tensor_tensor(xt_s[:, n % BODY, 1], ps[:, M], f(xt_s[:, n % BODY, 0]), ALU.subtract
                                  ).then_inc(xt_lo.sem, 1)

            def q_low(g, n, i=0):
                wait(dve, qk_hi, g, 2 * n + i)
                dve.tensor_tensor(qk[:, n % BODY, 2 * i + 1], ps[:, M], f(qk[:, n % BODY, 2 * i]), ALU.subtract
                                  ).then_inc(qk_lo.sem, 1)

            def k_low(g, n):
                q_low(g, n, 1)

            def start():
                credit(dve, masked_done, low_hi, low_lo, xt_lo, qk_lo, rec_done, o_done)
                credit(dve, norm.counted, norm.averaged, norm.normed)
                dve.memset(v_w[:, :, :, :, DH], 1.0)
                dve.memset(f(stack[96:98, :, :, 1]), -1.0).then_inc(filled, 1)
                turned_x(0, 0)
                q_low(0, 0)
                k_low(0, 0)
                turned_x(0, 1)
                q_low(0, 1)
                mask_scores(0, 0)
                mask_scores(0, 1)
                k_low(0, 1)
                mask_scores(0, 2)
                turned_x(0, 2)
                mask_scores(0, 3)
                mask_scores(0, 4)
                split_low(0, 0)
                q_low(0, 2)
                mask_scores(0, 5)
                mask_scores(0, 6)
                k_low(0, 2)
                mask_scores(0, 7)

            def slot(g, t, inside):
                if inside(t + AHEAD):
                    mask_scores(g, t + AHEAD)
                if t % C == 0 and inside(t // C + 1, C):
                    split_low(g, t // C + 1)
                if t % C == 1 and inside((t - 9) // C, C):
                    m = (t - 9) // C
                    j, h = m // HEADS % BODY, m % HEADS
                    if h == 0:
                        wait(dve, norm.summed, g, m // HEADS - 2)
                    bank = ps[:, O + m % 2, 0:C * (DH + 1)].rearrange("p (c d) -> p c d", c=C)
                    wait(dve, o_ready, g, m)
                    wait(dve, o_done, g, m - 2)
                    dve.reciprocal(recip[:, m % 2], bank[:, :, DH]).then_inc(rec_done.sem, 1)
                    wait(dve, rec_done, g, m)
                    dve.tensor_tensor(o_all[:, j, :, h * DH:(h + 1) * DH], bank[:, :, 0:DH],
                                      recip[:, m % 2].unsqueeze(2).to_broadcast([P, C, DH]), ALU.mult
                                      ).then_inc(o_done.sem, 1)
                if t % TILES == 8 and inside((t - 24) // TILES, TILES):
                    norm.dve_stats(dve, g, (t - 24) // TILES)
                if t % TILES == 11 and inside((t - 27) // TILES, TILES):
                    n = (t - 27) // TILES
                    norm.dve_apply(dve, g, n, lambda c: batch_of(g, n)[:, :, c].rearrange("p a d -> p (a d)"))
                for what, n in slots_of_batch(t, ((10, 3, turned_x), (12, 3, q_low), (14, 3, k_low))):
                    if inside(n, TILES):
                        what(g, n)
            run(dve, start, slot)

        @block.tensor
        def _(pe):
            def scores(g, t):
                m, c = t // C, t % C
                if c == 0:
                    wait_stacked(pe, g, m)
                wait(pe, masked_done, g, t - 2)
                j, h = m // HEADS % BODY, m % HEADS
                pe.matmul(ps[:, S + t % 2], stack[0:96, j, h, 0, c * P:(c + 1) * P], stack[0:96, j, h, 1],
                          start=True, stop=True).then_inc(s_ready.sem, 1)

            def low_row(g, m):
                wait(pe, low_lo, g, m)
                wait(pe, row_done, g, m - 1)
                for c in range(C):
                    last = pe.matmul(ps[0:2, R, c * P:(c + 1) * P], low_s[:, m % 2, c], ident_r[:], start=True, stop=True)
                last.then_inc(row_ready.sem, 1)

            def turned_scores(g, t):
                m, c = t // C, t % C
                if c == 0:
                    wait(pe, row_done, g, m)
                wait(pe, exp_done, g, t - 2)
                j, h = m // HEADS % BODY, m % HEADS
                pe.matmul(ps[:, T + t % 2], stack[:, j, h, 1, c * P:(c + 1) * P], stack[:, j, h, 0],
                          start=True, stop=False)
                pe.matmul(ps[:, T + t % 2], ident_r[:], mask_t[:, c], start=False, stop=True).then_inc(t_ready.sem, 1)

            def output(g, m, q):
                j, h = m // HEADS % BODY, m % HEADS
                if q == 0:
                    wait(pe, exp_done, g, C * m + C - 1)
                    wait(pe, o_done, g, m - 2)
                    if h == 0:
                        wait(pe, v_done, g, m // HEADS)
                for c in range(C):
                    last = pe.matmul(ps[:, O + m % 2, q * (DH + 1):(q + 1) * (DH + 1)],
                                     prob[:, m % 4, c, q * P:(q + 1) * P], v_w[:, j, c, h],
                                     start=c == 0, stop=c == C - 1)
                if q == C - 1:
                    last.then_inc(o_ready.sem, 1)

            def turn_x(g, n, before=2):
                wait(pe, x_lo, g, n)
                wait(pe, v_done, g, n - before)
                wait(pe, qk_lo, g, 2 * (n - 1) + 1)
                for c in range(C):
                    for part in range(2):
                        last = pe.matmul(ps[:, M, c * P:(c + 1) * P], x_s[:, n % BODY, part, c], ident_r[:],
                                         start=part == 0, stop=part == 1)
                last.then_inc(xt_ready.sem, 1)

            def q(g, n):
                wait(pe, xt_lo, g, n)
                products(pe, ps[:, M], [w_s[:, h, 0:D] for h in range(2)],
                         [xt_s[:, n % BODY, h] for h in range(2)]).then_inc(qk_ready.sem, 1)

            def k(g, n):
                wait(pe, qk_lo, g, 2 * n)
                products(pe, ps[:, M], [w_s[:, h, D:2 * D] for h in range(2)],
                         [xt_s[:, n % BODY, h] for h in range(2)]).then_inc(qk_ready.sem, 1)

            def v(g, n, before=1):
                wait(pe, qk_lo, g, 2 * (n + before) + 1)
                wait(pe, v_done, g, n - 1)
                for c in range(C):
                    cols = slice(c * P, (c + 1) * P)
                    last = products(pe, ps[:, M, cols], [xt_s[:, n % BODY, h, cols] for h in range(2)],
                                    [w_s[:, h, 2 * D:] for h in range(2)])
                last.then_inc(v_ready.sem, 1)

            def start():
                credit(pe, s_ready, xt_ready, qk_ready, v_ready, t_ready, o_ready, row_ready)
                pe.wait_ge(identity, 1)
                pe.wait_ge(filled, 1)
                turn_x(0, 0)
                q(0, 0)
                k(0, 0)
                v(0, 0, 0)
                turn_x(0, 1, 1)
                q(0, 1)
                scores(0, 0)
                scores(0, 1)
                k(0, 1)
                scores(0, 2)
                turn_x(0, 2)
                scores(0, 3)
                scores(0, 4)
                low_row(0, 0)
                q(0, 2)
                scores(0, 5)
                scores(0, 6)
                k(0, 2)
                scores(0, 7)

            def slot(g, t, inside):
                if inside(t):
                    turned_scores(g, t)
                if inside(t + AHEAD):
                    scores(g, t + AHEAD)
                if inside((t - 5) // C, C):
                    output(g, (t - 5) // C, (t - 5) % C)
                if t % C == 1 and inside(t // C + 1, C):
                    low_row(g, t // C + 1)
                for what, n in slots_of_batch(t, ((8, 1, v), (10, 3, turn_x), (12, 3, q), (14, 3, k))):
                    if inside(n, TILES):
                        if what is v:
                            v(g, n, 1 if inside(n + 1, TILES) else 0)
                        else:
                            what(g, n)
            run(pe, start, slot)


def build(nc, d, out):
    with ExitStack() as ctx:
        x = ctx.enter_context(nc.sbuf_tensor("x_all", [P, BATCH, C, D], F32))
        with ExitStack() as first:
            sb = lambda n, s, t=F32R: first.enter_context(nc.sbuf_tensor(n, s, t))
            keep = (sb("at_split", [P, 2, C, N]), sb("a2t_split", [P, 2, C, N]), sb("ct_split", [P, 2, C, N]),
                    sb("c2t_split", [P, 2, C, N]), sb("g_split", [P, 2, 3, 3, D]), sb("v_sum", [P, C, D], F32), x)
            diffusion_setup(nc, d, keep)
            diffusion(nc, d, keep)
        dilated(nc, d, x)
        sb = lambda n, s, t=F32: ctx.enter_context(nc.sbuf_tensor(n, s, t))
        keep = (sb("t_mask", [P, C, N]), sb("t_mask_t", [P, C, N], F32R), sb("t_w_split", [P, 2, 3 * D], F32R),
                sb("ident", [P, P]), sb("t_eps", [P, C]))
        edge_attention(nc, d, x, keep)
        self_attention(nc, d, x, out, keep)


def kernel(**inputs):
    import numpy as np
    import concourse.bacc as bacc
    from concourse.bass_utils import run_bass_kernel_spmd

    a = {k: np.ascontiguousarray(v) for k, v in inputs.items()}
    flip = lambda v: np.ascontiguousarray(np.swapaxes(v, -1, -2))
    cols = lambda v: np.ascontiguousarray(v.reshape(-1, P).T)
    by_input = lambda w: np.ascontiguousarray(w.transpose(2, 0, 1))
    by_gate = lambda b: np.ascontiguousarray(b.reshape(SKIPS, 4, D).transpose(2, 0, 1))
    laid = {
        "x": a["x"], "xT": flip(a["x"]), "adj": a["adj"], "adjT": flip(a["adj"]),
        "alpha": a["L0_gnn_alpha_train"], "alpha_cols": cols(a["L0_gnn_alpha_train"]), "wT": flip(a["L0_gnn_w"]), "d": a["L0_gnn_d"],
        "fc_w": a["L0_gnn_fc_in_w"], "fc_b": a["L0_gnn_fc_in_b"],
        "Wg0": a["L1_gnn_Wg0"], "bg0": a["L1_gnn_bg0"], "Wg1": a["L1_gnn_Wg1"], "bg1": a["L1_gnn_bg1"],
        "WihT": by_input(a["L1_gnn_Wih"]), "WhhT": by_input(a["L1_gnn_Whh"]),
        "bih": by_gate(a["L1_gnn_bih"]), "bhh": by_gate(a["L1_gnn_bhh"]),
        "W_linT": flip(a["L2_gnn_W_lin"]), "W_valT": flip(a["L2_gnn_W_val"]), "W_outT": flip(a["L2_gnn_W_out"]),
        "a": a["L2_gnn_a"].reshape(D, 1), "src": a["L2_gnn_src"],
        "edge_ends": np.ascontiguousarray(np.stack([cols(a["L2_gnn_src"]), cols(a["L2_gnn_dst"])], -1)),
        "iota": np.tile(np.arange(N, dtype=np.float32), (P, 1)),
        "node": cols(np.arange(N, dtype=np.float32)),
        "head_mask": np.repeat(np.eye(HEADS, dtype=np.float32), DH, axis=0),
        "W_qkv": a["L3_gnn_W"],
        "ident": np.eye(P, dtype=np.float32),
    }
    nc = bacc.Bacc("TRN2", target_bir_lowering=False, num_devices=1)
    d, arrays = {}, {}
    for name, v in laid.items():
        arrays[f"in_{name}"] = v
        d[name] = nc.dram_tensor(f"in_{name}", v.shape, mybir.dt.from_np(v.dtype), kind="ExternalInput").ap()
    out = nc.dram_tensor("out", (BATCH, N, D), F32, kind="ExternalOutput").ap()
    build(nc, d, out)
    return run_bass_kernel_spmd(nc, [arrays], core_ids=[0]).results[0]["out"]
```
